# Optimizing a Trainium2 kernel written in Bass

```python
import numpy as np
import jax
import jax.numpy as jnp

def _softmax(x, axis=-1):
    return jax.nn.softmax(x, axis=axis)

def _gelu(x):
    return jax.nn.gelu(x, approximate=True)

def _silu(x):
    return jax.nn.silu(x)

def _sigmoid(x):
    return jax.nn.sigmoid(x)

def _layernorm(x, axis=-1, eps=1e-05):
    m = jnp.mean(x, axis=axis, keepdims=True)
    v = jnp.var(x, axis=axis, keepdims=True)
    return (x - m) / jnp.sqrt(v + eps)

def _scatter_add(tgt, idx, src, axis=0):
    return tgt.at[idx].add(src)

def _segment_sum(src, seg, n):
    return jax.ops.segment_sum(src, seg, n)
kernel_name = 'mk_decoder_postln_d1_seqx_r4_6032bb'

def setup_inputs(seed: int=0):
    np.random.seed(seed)
    _w = jnp.asarray

    def _rec_inputs():
        import jax
        import jax.numpy as jnp
        _rk = jax.random.key(seed)
        x = -0.000125 + 0.9999 * jax.random.normal(jax.random.fold_in(_rk, 1), (4, 512, 512), jnp.float32)
        _lenS = 512 - jax.random.randint(jax.random.fold_in(_rk, 7), (4,), 0, max(1, 512 // 4) + 1, jnp.int32)
        _lenS2 = 512 - jax.random.randint(jax.random.fold_in(_rk, 8), (4,), 0, max(1, 512 // 4) + 1, jnp.int32)
        itok_BxS_13_99985 = jax.random.randint(jax.random.fold_in(_rk, 11), (4, 512), 13, 99986, jnp.int32)
        _ctx_2048P = jax.random.normal(jax.random.fold_in(_rk, 12), (4, 16, 512), jnp.float32)
        _ctx_2048c = jax.random.dirichlet(jax.random.fold_in(_rk, 512), 0.3 * jnp.ones((16,), jnp.float32), (4, 512))
        _ctx_2048t = jnp.einsum('bsk,bkd->bsd', _ctx_2048c, _ctx_2048P)
        _ctx_2048t = _ctx_2048t * jax.lax.rsqrt(jnp.mean(jnp.square(_ctx_2048t)) + 1e-12) * 0.953939
        ctx_2048 = 6.82029e-06 + 0.0200006 * (_ctx_2048t + 0.3 * jax.random.normal(jax.random.fold_in(_rk, 612), (4, 512, 512), jnp.float32))
        return (x, itok_BxS_13_99985, ctx_2048)
    x, itok_BxS_13_99985, ctx_2048 = _rec_inputs()

    def _L0_attn_setup():
        import jax, jax.numpy as jnp
        import numpy as np
        HEADS = 16
        key = jax.random.key(seed)
        ks = jax.random.split(key, 5)
        B, T, D = (2, 512, 512)
        s = 0.02
        return {'x': jax.random.normal(ks[0], (B, T, D), dtype=jnp.float32), 'Wq': jax.random.normal(ks[1], (D, D), dtype=jnp.float32) * s, 'Wk': jax.random.normal(ks[2], (D, D), dtype=jnp.float32) * s, 'Wv': jax.random.normal(ks[3], (D, D), dtype=jnp.float32) * s, 'Wo': jax.random.normal(ks[4], (D, D), dtype=jnp.float32) * s}
    _L0_attn_all = _L0_attn_setup()
    _L0_attn_in = {k: v for k, v in _L0_attn_all.items() if k in ('Wq', 'Wk', 'Wv', 'Wo')}
    del _L0_attn_all

    def _L0_xattn_setup():
        import jax, jax.numpy as jnp
        import numpy as np
        B, S, D = (4, 1024, 512)
        E = 4
        F = 2048 // E
        VOCAB = 25000
        key = jax.random.key(seed)
        k1, k2, k3, k4, k5 = jax.random.split(key, 5)
        hidden_states = jax.random.normal(k1, (B, S, D), dtype=jnp.float32)
        token_ids = jax.random.randint(k2, (B, S), 0, VOCAB, dtype=jnp.int64)
        Wg = jax.random.normal(k3, (E, F, D), dtype=jnp.float32) * 0.02
        Wu = jax.random.normal(k4, (E, F, D), dtype=jnp.float32) * 0.02
        Wd = jax.random.normal(k5, (E, D, F), dtype=jnp.float32) * 0.02
        return {'hidden_states': hidden_states, 'token_ids': token_ids, 'Wg': Wg, 'Wu': Wu, 'Wd': Wd}
    _L0_xattn_all = _L0_xattn_setup()
    _L0_xattn_in = {k: v for k, v in _L0_xattn_all.items() if k in ()}
    del _L0_xattn_all

    def _L0_ffn_setup():
        import jax, jax.numpy as jnp
        import numpy as np

        def _sparsify_2to4(h):
            B, S, I = h.shape
            g = h.reshape(B, S, I // 4, 4)
            a = jnp.abs(g)
            _, idx = jax.lax.top_k(a, 2)
            pos = jnp.arange(4)
            mask = (pos == idx[..., 0:1]) | (pos == idx[..., 1:2])
            return (g * mask.astype(g.dtype)).reshape(B, S, I)
        key = jax.random.key(seed)
        k1, k2, k3, k4 = jax.random.split(key, 4)
        B, S, H, I = (4, 512, 512, 2048)
        x = jax.random.normal(k1, (B, S, H), dtype=jnp.float32)
        w_gate = jax.random.normal(k2, (H, I), dtype=jnp.float32) / np.sqrt(H)
        w_up = jax.random.normal(k3, (H, I), dtype=jnp.float32) / np.sqrt(H)
        w_down = jax.random.normal(k4, (I, H), dtype=jnp.float32) / np.sqrt(I)
        return {'x': x, 'w_gate': w_gate, 'w_up': w_up, 'w_down': w_down}
    _L0_ffn_all = _L0_ffn_setup()
    _L0_ffn_in = {k: v for k, v in _L0_ffn_all.items() if k in ('w_gate', 'w_up', 'w_down')}
    del _L0_ffn_all
    return {'x': x, 'itok_BxS_13_99985': itok_BxS_13_99985, 'ctx_2048': ctx_2048, 'L0_attn_Wq': _L0_attn_in['Wq'], 'L0_attn_Wk': _L0_attn_in['Wk'], 'L0_attn_Wv': _L0_attn_in['Wv'], 'L0_attn_Wo': _L0_attn_in['Wo'], 'L0_ffn_w_gate': _L0_ffn_in['w_gate'], 'L0_ffn_w_up': _L0_ffn_in['w_up'], 'L0_ffn_w_down': _L0_ffn_in['w_down']}

def reference(x, itok_BxS_13_99985, ctx_2048, L0_attn_Wq, L0_attn_Wk, L0_attn_Wv, L0_attn_Wo, L0_ffn_w_gate, L0_ffn_w_up, L0_ffn_w_down):
    import jax
    import jax.numpy as jnp

    def _L0_attn_ref(x, Wq, Wk, Wv, Wo):
        import jax, jax.numpy as jnp
        import numpy as np
        HEADS = 16
        B, T, _ = x.shape
        H = HEADS
        Dh = Wq.shape[1] // H
        q = (x @ Wq).reshape(B, T, H, Dh)
        k = (x @ Wk).reshape(B, T, H, Dh)
        v = (x @ Wv).reshape(B, T, H, Dh)
        scores = jnp.einsum('bthd,bshd->bhts', q, k)
        mask = jnp.tril(jnp.ones((T, T), dtype=scores.dtype))
        scores = scores * mask
        attn = jax.nn.softmax(scores / T ** 0.5, axis=-1)
        out = jnp.einsum('bhts,bshd->bthd', attn, v).reshape(B, T, H * Dh)
        return out @ Wo

    def _L0_xattn_ref(hidden_states, token_ids, Wg, Wu, Wd):
        import jax, jax.numpy as jnp
        import numpy as np
        B, S, D = (4, 1024, 512)
        E = 4
        F = 2048 // E
        VOCAB = 25000
        tokens_per_expert = VOCAB // E
        tid = jnp.clip(token_ids, 0, VOCAB - 1)
        expert_ids = jnp.minimum(tid // tokens_per_expert, E - 1)
        out = jnp.zeros_like(hidden_states)
        for e in range(E):
            g = jax.nn.silu(jnp.einsum('bsd,fd->bsf', hidden_states, Wg[e]))
            u = jnp.einsum('bsd,fd->bsf', hidden_states, Wu[e])
            y = jnp.einsum('bsf,df->bsd', g * u, Wd[e])
            out = jnp.where((expert_ids == e)[..., None], y, out)
        return out

    def _L0_ffn_ref(x, w_gate, w_up, w_down):
        import jax, jax.numpy as jnp
        import numpy as np

        def _sparsify_2to4(h):
            B, S, I = h.shape
            g = h.reshape(B, S, I // 4, 4)
            a = jnp.abs(g)
            _, idx = jax.lax.top_k(a, 2)
            pos = jnp.arange(4)
            mask = (pos == idx[..., 0:1]) | (pos == idx[..., 1:2])
            return (g * mask.astype(g.dtype)).reshape(B, S, I)
        h = jax.nn.silu(jnp.einsum('bsh,hi->bsi', x, w_gate)) * jnp.einsum('bsh,hi->bsi', x, w_up)
        h_sparse = _sparsify_2to4(h)
        return jnp.einsum('bsi,ih->bsh', h_sparse, w_down)
    x = _layernorm(x + _L0_attn_ref(x, L0_attn_Wq, L0_attn_Wk, L0_attn_Wv, L0_attn_Wo), axis=-1)
    x = _layernorm(x + _L0_xattn_ref(x, itok_BxS_13_99985, ctx_2048, ctx_2048, ctx_2048), axis=-1)
    x = _layernorm(x + _L0_ffn_ref(x, L0_ffn_w_gate, L0_ffn_w_up, L0_ffn_w_down), axis=-1)
    return x

_drawn_inputs = setup_inputs


def setup_inputs(seed=0):
    import zlib

    import numpy as np

    out = dict(_drawn_inputs(seed))
    spreads = {}
    factors = {'L0_attn_Wq': 8.0, 'L0_attn_Wk': 8.0, 'L0_attn_Wv': 3.335, 'L0_attn_Wo': 3.335}
    for name, (base, spread) in spreads.items():
        noise = np.random.default_rng([zlib.crc32(name.encode()), seed]).standard_normal(out[name].shape)
        drawn = base * np.exp(spread * noise) if base else spread * noise
        out[name] = jnp.asarray(drawn.astype(out[name].dtype))
    for name, factor in factors.items():
        out[name] = (out[name] * factor).astype(out[name].dtype)
    return out
```

```python
from contextlib import ExitStack

import concourse.bass as bass
from concourse import mybir

F32 = mybir.dt.float32
F32R = mybir.dt.float32r
BF16 = mybir.dt.bfloat16
F16 = mybir.dt.float16
I32 = mybir.dt.int32
ALU = mybir.AluOpType
ACT = mybir.ActivationFunctionType
AX = mybir.AxisListType

P = 128
HEADS = 16
EPS = 1e-5
NEG = -3.0e38


def wait_apart(eng, passed, waits):
    for sem, value in waits:
        eng.wait_ge(sem, value)
    eng.sem_inc(passed, 1)


def matmul3(pe, out, a, b, steps, first=0, last=None):
    chain = [(k, i, j) for k in range(steps) for i, j in ((0, 0), (0, 1), (1, 0))]
    last = len(chain) if last is None else last
    for n in range(first, last):
        k, i, j = chain[n]
        ins = pe.matmul(out, a(k, i), b(k, j), start=(n == 0), stop=(n == len(chain) - 1))
    return ins


def attention(nc, w_split, ident, idx_all, x_t, x_rows, x1_rows, sorted_rows, scratch, B, T, D):
    KT = D // P
    NB = T // P
    HD = D // HEADS
    SLOTS = P // HD
    HPT = P // HD
    NM = D // P
    UPM = HPT * NB
    UPB = NM * UPM
    RS_, PR = 3, 3
    scale = 1.0 / float(T) ** 0.5

    wh, wl = w_split
    with ExitStack() as ctx:
        def sb(name, shape, dt):
            return ctx.enter_context(nc.sbuf_tensor(name, shape, dt))

        def sem(name):
            return ctx.enter_context(nc.semaphore(name))

        x_raw = sb("x_raw", [P, KT, T], F32)
        x_hl = [sb("x_hi", [P, KT, T], F32R), sb("x_lo", [P, KT, T], F32R)]
        x_res = sb("x_res", [P, NB, D], F32)
        qk_hl = [[sb(f"{n}_{h}", [P, T], F32R) for h in ("hi", "lo")] for n in "qk"]
        stack = [[sb(f"{n}_stack{i}", [P, HPT, T], F32R) for i in range(2)] for n in "qk"]
        v3 = sb("v3", [P, NB, 3, D], BF16)
        v_rest = [sb(f"v_rest{i}", [P, D], F32) for i in range(2)]
        v_tail = sb("v_tail", [P, NB - 1, D], F32)
        probs = [sb(f"probs{i}", [P, T], F32) for i in range(RS_)]
        pt_hi = [sb(f"pt_hi{i}", [P, T], F16) for i in range(PR)]
        pt_lo = [sb(f"pt_lo{i}", [P, T], F16) for i in range(PR)]
        o_raw = sb("o_raw", [P, NB, HEADS, HD], F32)
        o_tmp = sb("o_tmp", [P, NB - 1, HEADS, HD], F32)
        ot_hl = [[sb(f"ot_{h}{i}", [P, KT, P], F32R) for i in range(2)] for h in ("hi", "lo")]
        mask = sb("mask", [P, T], F32)
        ones_bf = sb("ones_bf", [P, P], BF16)
        smax = sb("smax", [P, NB, HEADS], F32)
        nmax = sb("nmax", [P, NB, HEADS], F32)
        rsum = sb("rsum", [P, NB, HEADS], F32)
        c_up = sb("c_up", [P, NB, HEADS], F32)
        n_up = sb("n_up", [P, NB, HEADS], F32)
        den = sb("den", [P, NB, HEADS], F32)
        den2 = sb("den2", [P, NB, HEADS], F32)
        rinv = sb("rinv", [P, NB, HEADS], F32)
        z = [sb(f"z{i}", [P, D], F32) for i in range(2)]
        x1 = [sb(f"x1_{i}", [P, D], F32) for i in range(2)]
        idx = sb("idx", [P, NB], I32)
        s_sc = [sem(f"s_sc{i}") for i in range(2)]
        s_idx = sem("s_idx")
        ln = LayerNorm(nc, ctx, "ln1", D)
        bank = [ctx.enter_context(nc.psum_tensor(f"bank{i}", [P, 512], F32)) for i in range(8)]
        S, TP, OB, PJ = bank[0:3], bank[3:5], bank[5:7], bank[7]

        s_const = sem("s_const")
        s_passed, s_passed_sp = sem("s_passed"), sem("s_passed_sp")
        s_xraw = sem("s_xraw")
        s_xh = sem("s_xh")
        s_xl = sem("s_xl")
        s_xres = sem("s_xres")
        s_vp = sem("s_vp")
        s_v0 = sem("s_v0")
        s_vr = sem("s_vr")
        s_v1 = sem("s_v1")
        s_v2 = sem("s_v2")
        s_sf = sem("s_sf")
        s_sfe = sem("s_sfe")
        s_pj = sem("s_pj")
        s_pjh = sem("s_pjh")
        s_pjl = sem("s_pjl")
        s_dw = sem("s_dw")
        s_st = [sem("s_stq"), sem("s_stk")]
        s_S = sem("s_S")
        s_mx = sem("s_mx")
        s_nm = sem("s_nm")
        s_e = sem("s_e")
        s_T = sem("s_T")
        s_hi = sem("s_hi")
        s_lo = sem("s_lo")
        s_pv = sem("s_pv")
        s_oe = sem("s_oe")
        s_c = sem("s_c")
        s_t = sem("s_t")
        s_on = sem("s_on")
        s_ot = sem("s_ot")
        s_oth = sem("s_oth")
        s_otl = sem("s_otl")
        s_wo = sem("s_wo")
        s_z = sem("s_z")
        s_x1 = sem("s_x1")
        s_x1d = [sem(f"s_x1d{i}") for i in range(2)]

        units = [(u // UPM, (u // NB) % HPT, NB - 1 - u % NB) for u in range(UPB)]

        def cols(r):
            return (r + 1) * P

        block = ctx.enter_context(nc.Block())

        @block.gpsimd
        def _(pool):
            pool.memset(mask[:, :], 1.0).then_inc(s_const, 1)
            ln.start(pool)
            pool.memset(ones_bf[:, :], 1.0).then_inc(s_const, 1)
            for r in range(NB):
                pool.memset(n_up[:, r, :], float((NB - 1 - r) * P)).then_inc(s_const, 1)
            pool.wait_ge(s_const, 2 + NB)
            pool.affine_select(out=mask[:, T - P:T], in_=mask[:, T - P:T], compare_op=ALU.is_ge, fill=0.0,
                               base=0, pattern=[[-1, P]], channel_multiplier=1).then_inc(s_const, 1)
            with pool.Fori(0, B) as b:
                for i in range(2):
                    pool.wait_ge(s_sc[i], b * (NB // 2) * 16)
                pool.tensor_copy(idx[:, :], idx_all[:, bass.ds(b * NB, NB)]).then_inc(s_idx, 1)
                for r in range(NB):
                    ln.rstd(pool, b * NB + r, r)
                    wait_apart(pool, ln.s_passed[1], [(s_x1, b * NB + r + 1)] + [(s_idx, b + 1)] * (r == 0))
                    pool.indirect_dma_start(sorted_rows, bass.IndirectOffsetOnAxis(idx[:, r:r + 1], 0),
                                            x1[r % 2][:, :], None).then_inc(s_sc[r % 2], 16)
            for i in range(2):
                pool.wait_ge(s_sc[i], B * (NB // 2) * 16)

        NCONST = 3 + NB

        @block.sync
        def _(sp):
            with sp.Fori(0, B) as b:
                sp.wait_ge(s_xl, b * KT)
                sp.dma_start(x_raw[:, :, :], x_t[b]).then_inc(s_xraw, 16)
                for g in range(2 * NM):
                    m, side = g // 2, g % 2
                    hd = scratch[side]
                    sp.wait_ge(s_pjh, b * 2 * NM + g + 1)
                    sp.dma_start(hd[0], qk_hl[side][0][:, :].bitcast(F32)).then_inc(s_dw, 16)
                    sp.wait_ge(s_pjl, b * 2 * NM + g + 1)
                    sp.dma_start(hd[1], qk_hl[side][1][:, :].bitcast(F32)).then_inc(s_dw, 16)
                    wait_apart(sp, s_passed_sp, [(s_dw, (b * 2 * NM + g + 1) * 32)])
                    sp.wait_ge(s_S, b * UPB + max(m - 1, 0) * UPM)
                    order = (0, 1, 0, 1) if side == 0 else (0, 0, 1, 1)
                    for slot, half in enumerate(order):
                        sp.dma_start(stack[side][m % 2][slot * HD:(slot + 1) * HD, :, :].bitcast(F32),
                                     hd[half].rearrange("(h r) t -> r h t", r=HD)).then_inc(s_st[side], 16)
                    if g == 1:
                        sp.wait_ge(s_z, b * NB)
                        sp.dma_start(x_res[:, :, :], x_rows[b]).then_inc(s_xres, 16)
                for r in range(NB):
                    sp.wait_ge(s_x1, b * NB + r + 1)
                    sp.dma_start(x1_rows[b][:, r, :], x1[r % 2][:, :]).then_inc(s_x1d[r % 2], 16)
            for i in range(2):
                sp.wait_ge(s_x1d[i], B * NB // 2 * 16)

        @block.tensor
        def _(pe):
            pe.wait_ge(s_const, NCONST)

            def project(b, g, first, last):
                m, side = g // 2, g % 2
                if first == 0:
                    pe.wait_ge(s_pjl, b * 2 * NM + g)
                ins = matmul3(pe, PJ[:, :], lambda k, i: (wh, wl)[i][side][:, k, m * P:(m + 1) * P],
                              lambda k, j: x_hl[j][:, k, :], KT, first, last)
                if last == 3 * KT:
                    ins.then_inc(s_pj, 1)

            def scores(b, u):
                m, h, r = units[u]
                if u % UPM == 0:
                    for side in range(2):
                        pe.wait_ge(s_st[side], (b * NM + m + 1) * 16 * SLOTS)
                if u >= 3:
                    pe.wait_ge(s_e, b * UPB + u - 2)
                pe.matmul(S[u % 3][:, 0:cols(r)], stack[0][m % 2][:, h, r * P:(r + 1) * P],
                          stack[1][m % 2][:, h, 0:cols(r)], start=True, stop=True).then_inc(s_S, 1)

            def transposes(b, u):
                _, _, r = units[u]
                pe.wait_ge(s_e, b * UPB + u + 1)
                if u >= 2:
                    pe.wait_ge(s_lo, b * UPB + u - 1)
                for j in range(r + 1):
                    ins = pe.transpose(TP[u % 2][:, j * P:(j + 1) * P], probs[u % RS_][:, j * P:(j + 1) * P],
                                       ident[:, :])
                ins.then_inc(s_T, 1)

            def values(b, u):
                m, h, r = units[u]
                if u % UPM == 0 and m >= 2:
                    pe.wait_ge(s_oe, b * NM + m - 1)
                pe.wait_ge(s_lo, b * UPB + u + 1)
                out = OB[m % 2][:, (h * NB + r) * HD:(h * NB + r + 1) * HD]
                c = (m * HPT + h) * HD
                chain = [(j, half, part) for j in range(r + 1)
                         for half, part in ((0, 0), (0, 1), (0, 2), (1, 0), (1, 1))]
                for n, (j, half, part) in enumerate(chain):
                    p = (pt_hi, pt_lo)[half][u % PR][:, j * P:(j + 1) * P]
                    ins = pe.matmul(out, p, v3[:, j, part, c:c + HD], start=(n == 0), stop=(n == len(chain) - 1))
                ins.then_inc(s_pv, 1)

            with pe.Fori(0, B) as b:
                pe.wait_ge(s_xl, (b + 1) * KT)
                for j in range(NB):
                    matmul3(pe, bank[j][:, :], lambda k, i: x_hl[i][:, k, j * P:(j + 1) * P],
                            lambda k, i: (wh, wl)[i][2][:, k, :], KT).then_inc(s_vp, 1)
                project(b, 0, 0, 3 * KT)
                for n in range(NB - 1):
                    j = NB - 1 - n
                    if n == 0:
                        pe.wait_ge(s_z, b * NB)
                        pe.wait_ge(s_v2, (b + 1) * NB)
                    for part in range(3):
                        ins = pe.matmul(bank[4 + n][:, :], ones_bf[:, :], v3[:, j, part, :],
                                        start=(part == 0), stop=(part == 2))
                    ins.then_inc(s_sf, 1)
                project(b, 1, 0, 3 * KT)
                pe.wait_ge(s_sfe, (b + 1) * (NB - 1))
                for u in range(-2, UPB + 2):
                    if u + 2 < UPB:
                        scores(b, u + 2)
                    if 0 <= u < UPB:
                        transposes(b, u)
                    if u >= 2:
                        values(b, u - 2)
                    if u >= 0 and u // UPM + 1 < NM:
                        s, m = u % UPM, u // UPM + 1
                        if s < 4:
                            project(b, 2 * m, 3 * s, 3 * s + 3)
                        elif 5 <= s < 9:
                            project(b, 2 * m + 1, 3 * s - 15, 3 * s - 12)
                for r in range(NB + 1):
                    if r < NB:
                        pe.wait_ge(s_on, b * NB + r + 1)
                        for k in range(KT):
                            ins = pe.transpose(bank[r][:, k * P:(k + 1) * P],
                                               o_raw[:, r, k * HPT:(k + 1) * HPT, :].rearrange("p h d -> p (h d)"),
                                               ident[:, :])
                        ins.then_inc(s_ot, 1)
                    if r >= 1:
                        pe.wait_ge(s_otl, b * NB + r)
                        matmul3(pe, bank[3 + r][:, :], lambda k, i: ot_hl[i][(r - 1) % 2][:, k, :],
                                lambda k, i: (wh, wl)[i][3][:, k, :], KT).then_inc(s_wo, 1)

        @block.scalar
        def _(act):
            act.wait_ge(s_const, NCONST)

            def split_proj(b, g):
                side = g % 2
                act.wait_ge(s_pj, b * 2 * NM + g + 1)
                act.wait_ge(s_dw, b * 2 * NM * 32 + max(g - 1, 0) * 32)
                act.activation(qk_hl[side][0][:, :], PJ[:, :], ACT.Copy,
                               scale=(scale if side == 0 else 1.0)).then_inc(s_pjh, 1)

            def exps(b, u):
                m, h, r = units[u]
                c = m * HPT + h
                act.wait_ge(s_nm, b * UPB + u + 1)
                if u >= RS_:
                    act.wait_ge(s_T, b * UPB + u - RS_ + 1)
                act.activation(probs[u % RS_][:, 0:cols(r)], S[u % 3][:, 0:cols(r)], ACT.Exp,
                               bias=nmax[:, r, c:c + 1], accum_out=rsum[:, r, c:c + 1]).then_inc(s_e, 1)

            def hi(b, u):
                _, _, r = units[u]
                act.wait_ge(s_T, b * UPB + u + 1)
                if u >= PR:
                    act.wait_ge(s_pv, b * UPB + u - PR + 1)
                act.activation(pt_hi[u % PR][:, 0:cols(r)], TP[u % 2][:, 0:cols(r)], ACT.Copy).then_inc(s_hi, 1)

            with act.Fori(0, B) as b:
                act.wait_ge(s_xraw, (b + 1) * 16)
                for k in range(KT):
                    act.activation(x_hl[0][:, k, :], x_raw[:, k, :], ACT.Copy).then_inc(s_xh, 1)
                for j in range(NB):
                    act.wait_ge(s_vp, b * NB + j + 1)
                    act.activation(v3[:, j, 0, :], bank[j][:, :], ACT.Copy).then_inc(s_v0, 1)
                    act.wait_ge(s_vr, b * NB + j + 1)
                    act.activation(v3[:, j, 1, :], v_rest[j % 2][:, :], ACT.Copy).then_inc(s_v1, 1)
                split_proj(b, 0)
                split_proj(b, 1)
                for u in range(UPB + 1):
                    if u < UPB:
                        exps(b, u)
                    if u >= 1:
                        hi(b, u - 1)
                    if u // UPM + 1 < NM:
                        if u % UPM == 4:
                            split_proj(b, 2 * (u // UPM + 1))
                        elif u % UPM == 9:
                            split_proj(b, 2 * (u // UPM + 1) + 1)
                act.wait_ge(s_nm, (b + 1) * UPB)
                act.activation(c_up[:, :, :], nmax[:, :, :], ACT.Exp).then_inc(s_c, 1)
                for r in range(NB):
                    act.wait_ge(s_ot, b * NB + r + 1)
                    if r >= 2:
                        act.wait_ge(s_wo, b * NB + r - 1)
                    act.activation(ot_hl[0][r % 2][:, :, :].rearrange("p k t -> p (k t)"), bank[r][:, :],
                                   ACT.Copy).then_inc(s_oth, 1)

        @block.vector
        def _(dve):
            dve.wait_ge(s_const, NCONST)

            def split_proj(b, g):
                side = g % 2
                dve.wait_ge(s_pjh, b * 2 * NM + g + 1)
                dve.scalar_tensor_tensor(out=qk_hl[side][1][:, :], in0=PJ[:, :],
                                         scalar=(scale if side == 0 else 1.0),
                                         in1=qk_hl[side][0][:, :].bitcast(F32), op0=ALU.mult,
                                         op1=ALU.subtract).then_inc(s_pjl, 1)

            def maxima(b, u):
                m, h, r = units[u]
                c = m * HPT + h
                wait_apart(dve, s_passed, [(s_S, b * UPB + u + 1)])
                dve.tensor_tensor_reduce(out=S[u % 3][:, 0:cols(r)], in0=S[u % 3][:, 0:cols(r)],
                                         in1=mask[:, T - cols(r):T], scale=1.0, scalar=NEG, op0=ALU.mult,
                                         op1=ALU.max, accum_out=smax[:, r, c:c + 1]).then_inc(s_mx, 1)
                dve.wait_ge(s_mx, b * UPB + u + 1)
                if r < NB - 1:
                    dve.tensor_scalar(nmax[:, r, c:c + 1], smax[:, r, c:c + 1], 0.0, -1.0, ALU.max,
                                      ALU.mult).then_inc(s_nm, 1)
                else:
                    dve.tensor_scalar(nmax[:, r, c:c + 1], smax[:, r, c:c + 1], -1.0, None,
                                      ALU.mult).then_inc(s_nm, 1)

            def lo(b, u):
                _, _, r = units[u]
                dve.wait_ge(s_hi, b * UPB + u + 1)
                dve.tensor_tensor(pt_lo[u % PR][:, 0:cols(r)], TP[u % 2][:, 0:cols(r)],
                                  pt_hi[u % PR][:, 0:cols(r)], ALU.subtract).then_inc(s_lo, 1)

            def copy_out(b, m):
                dve.wait_ge(s_pv, b * UPB + (m + 1) * UPM)
                dve.tensor_copy(o_raw[:, :, m * HPT:(m + 1) * HPT, :].rearrange("p r h d -> p h r d"),
                                OB[m % 2][:, :].rearrange("p (h r d) -> p h r d", h=HPT, r=NB)).then_inc(s_oe, 1)

            def link(ins, b, n):
                ins.then_inc(s_t, 1)
                dve.wait_ge(s_t, b * CH + n)

            CH = 5

            with dve.Fori(0, B) as b:
                for k in range(KT):
                    dve.wait_ge(s_xh, b * KT + k + 1)
                    dve.tensor_tensor(x_hl[1][:, k, :], x_raw[:, k, :], x_hl[0][:, k, :].bitcast(F32),
                                      ALU.subtract).then_inc(s_xl, 1)
                for j in range(NB):
                    dve.wait_ge(s_v0, b * NB + j + 1)
                    dve.tensor_tensor(v_rest[j % 2][:, :], bank[j][:, :], v3[:, j, 0, :],
                                      ALU.subtract).then_inc(s_vr, 1)
                    dve.wait_ge(s_v1, b * NB + j + 1)
                    dve.tensor_tensor(v3[:, j, 2, :], v_rest[j % 2][:, :], v3[:, j, 1, :],
                                      ALU.subtract).then_inc(s_v2, 1)
                split_proj(b, 0)
                for n in range(NB - 1):
                    r = NB - 2 - n
                    dve.wait_ge(s_sf, b * (NB - 1) + n + 1)
                    if n == 0:
                        dve.tensor_copy(v_tail[:, r, :], bank[4 + n][:, :]).then_inc(s_sfe, 1)
                    else:
                        dve.wait_ge(s_sfe, b * (NB - 1) + n)
                        dve.tensor_tensor(v_tail[:, r, :], bank[4 + n][:, :], v_tail[:, r + 1, :],
                                          ALU.add).then_inc(s_sfe, 1)
                split_proj(b, 1)
                for u in range(-1, UPB + 1):
                    if u + 1 < UPB:
                        maxima(b, u + 1)
                    if u >= 1:
                        lo(b, u - 1)
                    if u >= 0 and u // UPM + 1 < NM:
                        if u % UPM == 4:
                            split_proj(b, 2 * (u // UPM + 1))
                        elif u % UPM == 9:
                            split_proj(b, 2 * (u // UPM + 1) + 1)
                    if u % UPM == 5 and u >= UPM:
                        copy_out(b, u // UPM - 1)
                dve.wait_ge(s_c, b + 1)
                dve.wait_ge(s_e, (b + 1) * UPB)
                link(dve.tensor_tensor(den[:, :, :], c_up[:, :, :], n_up[:, :, :], ALU.mult), b, 1)
                link(dve.tensor_tensor(den2[:, :, :], den[:, :, :], rsum[:, :, :], ALU.add), b, 2)
                link(dve.reciprocal(rinv[:, :, :], den2[:, :, :]), b, 3)
                up = c_up[:, 0:NB - 1, :].unsqueeze(3).broadcast_to([P, NB - 1, HEADS, HD])
                link(dve.tensor_tensor(o_tmp[:, :, :, :], v_tail[:, :, :].rearrange("p r (h d) -> p r h d", h=HEADS),
                                       up, ALU.mult), b, 4)
                copy_out(b, NM - 1)
                dve.wait_ge(s_oe, (b + 1) * NM)
                link(dve.tensor_tensor(o_raw[:, 0:NB - 1, :, :], o_raw[:, 0:NB - 1, :, :], o_tmp[:, :, :, :],
                                       ALU.add), b, 5)
                for r in range(NB):
                    dve.tensor_tensor(o_raw[:, r, :, :], o_raw[:, r, :, :],
                                      rinv[:, r, :].unsqueeze(2).broadcast_to([P, HEADS, HD]), ALU.mult).then_inc(s_on, 1)
                for r in range(NB + 1):
                    if r < NB:
                        dve.wait_ge(s_oth, b * NB + r + 1)
                        if r >= 2:
                            dve.wait_ge(s_wo, b * NB + r - 1)
                        dve.tensor_tensor(ot_hl[1][r % 2][:, :, :].rearrange("p k t -> p (k t)"), bank[r][:, :],
                                          ot_hl[0][r % 2][:, :, :].rearrange("p k t -> p (k t)").bitcast(F32),
                                          ALU.subtract).then_inc(s_otl, 1)
                    if r >= 1:
                        q = r - 1
                        dve.wait_ge(s_wo, b * NB + q + 1)
                        dve.wait_ge(s_xres, (b + 1) * 16)
                        dve.wait_ge(s_x1d[q % 2], (b * (NB // 2) + q // 2) * 16)
                        dve.wait_ge(s_sc[q % 2], (b * (NB // 2) + q // 2) * 16)
                        dve.tensor_tensor(z[q % 2][:, :], bank[4 + q][:, :], x_res[:, q, :],
                                          ALU.add).then_inc(s_z, 1)
                        ln.norm(dve, z[q % 2], x1[q % 2], s_z, b * NB + q + 1, b * NB + q, q, s_x1)


class LayerNorm:

    def __init__(self, nc, ctx, name, D, ring=4):
        self.D = D
        sb = lambda n, shape: ctx.enter_context(nc.sbuf_tensor(f"{name}_{n}", shape, F32))
        self.stats = sb("stats", [P, ring, 6])
        self.mv = sb("mv", [P, ring, 2])
        self.var = sb("var", [P, ring, 1])
        self.r = sb("r", [P, ring, 1])
        self.half = sb("half", [P, 1])
        self.s_half = ctx.enter_context(nc.semaphore(f"{name}_s_half"))
        self.s_passed = [ctx.enter_context(nc.semaphore(f"{name}_s_passed{i}")) for i in range(2)]
        self.s_st = ctx.enter_context(nc.semaphore(f"{name}_s_stats"))
        self.s_mv = ctx.enter_context(nc.semaphore(f"{name}_s_mv"))
        self.s_ve = ctx.enter_context(nc.semaphore(f"{name}_s_ve"))
        self.s_r = ctx.enter_context(nc.semaphore(f"{name}_s_r"))

    def start(self, pool):
        pool.memset(self.half[:, :], -0.5).then_inc(self.s_half, 1)

    def norm(self, dve, z, out, s_z, z_count, n, i, s_out):
        dve.wait_ge(s_z, z_count)
        dve.bn_stats(self.stats[:, i, :], z[:, :]).then_inc(self.s_st, 1)
        wait_apart(dve, self.s_passed[0], [(self.s_st, n + 1)])
        dve.bn_aggr(self.mv[:, i, :], self.stats[:, i, :]).then_inc(self.s_mv, 1)
        dve.wait_ge(self.s_r, n + 1)
        dve.tensor_scalar(out[:, :], z[:, :], self.mv[:, i, 0:1], self.r[:, i, :], ALU.subtract,
                          ALU.mult).then_inc(s_out, 1)

    def rstd(self, pool, n, i):
        wait_apart(pool, self.s_passed[1], [(self.s_mv, n + 1)])
        pool.tensor_scalar(self.var[:, i, :], self.mv[:, i, 1:2], EPS, None, ALU.add).then_inc(self.s_ve, 1)
        pool.wait_ge(self.s_ve, n + 1)
        pool.tensor_tensor(self.r[:, i, :], self.var[:, i, :], self.half[:, :], ALU.pow).then_inc(self.s_r, 1)


def setup(nc, w_dram, w_split, ident, D):
    KT = D // P
    wh, wl = w_split
    n_w = len(w_dram)
    with ExitStack() as ctx:
        raw = [ctx.enter_context(nc.sbuf_tensor(f"w_raw{i}", [P, KT, D], F32)) for i in range(n_w)]
        s_w = [ctx.enter_context(nc.semaphore(f"s_w{i}")) for i in range(n_w)]
        s_id = ctx.enter_context(nc.semaphore("s_id"))
        s_wh = ctx.enter_context(nc.semaphore("s_wh"))
        block = ctx.enter_context(nc.Block())

        @block.sync
        def _(sp):
            for i in range(n_w):
                sp.dma_start(raw[i][:, :, :], w_dram[i]).then_inc(s_w[i], 16)

        @block.gpsimd
        def _(pool):
            pool.memset(ident[:, :], 0.0).then_inc(s_id, 1)
            pool.wait_ge(s_id, 1)
            pool.affine_select(out=ident[:, :], in_=ident[:, :], compare_op=ALU.not_equal, fill=1.0, base=0,
                               pattern=[[-1, P]], channel_multiplier=1).then_inc(s_id, 1)

        @block.scalar
        def _(act):
            for i in range(n_w):
                act.wait_ge(s_w[i], 16)
                act.activation(wh[i][:, :, :], raw[i][:, :, :], ACT.Copy).then_inc(s_wh, 1)

        @block.vector
        def _(dve):
            for i in range(n_w):
                dve.wait_ge(s_wh, i + 1)
                dve.tensor_tensor(wl[i][:, :, :], raw[i][:, :, :], wh[i][:, :, :].bitcast(F32), ALU.subtract)


def route(nc, tok_dram, idx_all, tile_expert, sorted_rows, N, E, VOCAB, D):
    NT = N // P
    NS = NT + E - 1
    per_expert = VOCAB // E
    with ExitStack() as ctx:
        def sb(name, shape, dt=F32):
            return ctx.enter_context(nc.sbuf_tensor(name, shape, dt))

        tok = sb("tok_sb", [P, NT], I32)
        tok_f = sb("tok_f", [P, NT])
        ge = sb("ge", [P, E + 1, NT])
        onehot = sb("onehot", [P, E, NT])
        onehot_bf = sb("onehot_bf", [P, E, NT], BF16)
        before = sb("before", [P, P], BF16)
        ones = sb("ones", [P, P], BF16)
        run = [sb(f"run{i}", [P, E, 2 * NT]) for i in range(2)]
        total = sb("total", [P, E, NT])
        rank = sb("rank", [P, E, NT])
        n_pad = sb("n_pad", [P, E], I32)
        n_tiles = sb("n_tiles", [P, E], I32)
        n_rows = sb("n_rows", [P, E], I32)
        rows_f = sb("rows_f", [P, E])
        base = sb("base", [P, E])
        at = sb("at", [P, E, NT])
        at2 = sb("at2", [P, E, NT])
        pos = sb("pos", [P, NT])
        tile_i = sb("tile_i", [P, NS], I32)
        tile_f = sb("tile_f", [P, NS])
        past = sb("past", [P, E - 1, NS])
        expert_f = sb("expert_f", [P, NS])
        zero = sb("zero", [P, D])
        inside = ctx.enter_context(nc.psum_tensor("inside", [P, E, NT], F32))
        tiles = ctx.enter_context(nc.psum_tensor("tiles", [P, E, NT], F32))
        s_tok = ctx.enter_context(nc.semaphore("s_tok"))
        s_c = ctx.enter_context(nc.semaphore("s_rc"))
        s_v = ctx.enter_context(nc.semaphore("s_rv"))
        s_m = ctx.enter_context(nc.semaphore("s_rm"))
        s_zero = ctx.enter_context(nc.semaphore("s_zero"))
        N_ONEHOT = 3 + 2 * E + 1
        block = ctx.enter_context(nc.Block())

        @block.sync
        def _(sp):
            sp.dma_start(tok[:, :], tok_dram).then_inc(s_tok, 16)
            sp.wait_ge(s_c, 1)
            with sp.Fori(0, NS) as t:
                sp.dma_start(sorted_rows.rearrange("(t p) d -> t p d", p=P)[t], zero[:, :]).then_inc(s_zero, 16)
            sp.wait_ge(s_zero, NS * 16)

        @block.gpsimd
        def _(pool):
            pool.memset(zero[:, :], 0.0).then_inc(s_c, 1)
            pool.memset(ones[:, :], 1.0).then_inc(s_c, 1)
            pool.memset(before[:, :], 1.0).then_inc(s_c, 1)
            pool.iota(tile_i[:, :], [[P, NS]], base=0, channel_multiplier=0).then_inc(s_c, 1)
            pool.wait_ge(s_c, 4)
            pool.affine_select(out=before[:, :], in_=before[:, :], compare_op=ALU.is_gt, fill=0.0, base=0,
                               pattern=[[1, P]], channel_multiplier=-1).then_inc(s_c, 1)

        @block.tensor
        def _(pe):
            pe.wait_ge(s_c, 5)
            pe.wait_ge(s_v, N_ONEHOT)
            flat = onehot_bf[:, :, :].rearrange("p e t -> p (e t)")
            pe.matmul(inside[:, :, :].rearrange("p e t -> p (e t)"), before[:, :], flat, start=True, stop=True)
            pe.matmul(tiles[:, :, :].rearrange("p e t -> p (e t)"), ones[:, :], flat, start=True,
                      stop=True).then_inc(s_m, 1)

        @block.vector
        def _(dve):
            count = [0]

            def step(ins):
                count[0] += 1
                ins.then_inc(s_v, 1)
                dve.wait_ge(s_v, count[0])

            dve.wait_ge(s_tok, 16)
            step(dve.tensor_copy(tok_f[:, :], tok[:, :]))
            step(dve.memset(ge[:, 0, :], 1.0))
            step(dve.memset(ge[:, E, :], 0.0))
            for e in range(1, E):
                step(dve.tensor_scalar(ge[:, e, :], tok_f[:, :], float(e * per_expert), None, ALU.is_ge))
            step(dve.tensor_tensor(onehot[:, :, :], ge[:, 0:E, :], ge[:, 1:E + 1, :], ALU.subtract))
            step(dve.tensor_copy(onehot_bf[:, :, :], onehot[:, :, :]))
            while count[0] < N_ONEHOT:
                step(dve.memset(run[count[0] % 2][:, :, :], 0.0))
            dve.wait_ge(s_m, 1)
            step(dve.tensor_copy(total[:, :, :], tiles[:, :, :]))
            step(dve.tensor_copy(run[0][:, :, NT:], total[:, :, :]))
            shift, i = 1, 0
            while shift < NT:
                step(dve.tensor_tensor(run[1 - i][:, :, NT:], run[i][:, :, NT:],
                                       run[i][:, :, NT - shift:2 * NT - shift], ALU.add))
                shift, i = 2 * shift, 1 - i
            step(dve.tensor_tensor(rank[:, :, :], run[i][:, :, NT:], total[:, :, :], ALU.subtract))
            step(dve.tensor_tensor(at[:, :, :], inside[:, :, :], rank[:, :, :], ALU.add))
            step(dve.tensor_scalar(n_pad[:, :], run[i][:, :, 2 * NT - 1], float(P - 1), None, ALU.add))
            step(dve.tensor_scalar(n_tiles[:, :], n_pad[:, :], P.bit_length() - 1, None, ALU.logical_shift_right))
            step(dve.tensor_scalar(n_rows[:, :], n_tiles[:, :], P.bit_length() - 1, None, ALU.logical_shift_left))
            step(dve.tensor_copy(rows_f[:, :], n_rows[:, :]))
            step(dve.memset(base[:, :], 0.0))
            for e in range(1, E):
                step(dve.tensor_tensor(base[:, e:e + 1], base[:, e - 1:e], rows_f[:, e - 1:e], ALU.add))
            step(dve.tensor_tensor(at2[:, :, :], at[:, :, :], base[:, :].unsqueeze(2).broadcast_to([P, E, NT]),
                                   ALU.add))
            step(dve.tensor_tensor(at[:, :, :], at2[:, :, :], onehot[:, :, :], ALU.mult))
            step(dve.tensor_reduce(pos[:, :], at[:, :, :].rearrange("p e t -> p t e"), AX.X, ALU.add))
            step(dve.tensor_copy(idx_all[:, :], pos[:, :]))
            step(dve.tensor_copy(tile_f[:, :], tile_i[:, :]))
            for e in range(1, E):
                step(dve.tensor_scalar(past[:, e - 1, :], tile_f[:, :], base[:, e:e + 1], None, ALU.is_ge))
            step(dve.tensor_reduce(expert_f[:, :], past[:, :, :].rearrange("p e t -> p t e"), AX.X, ALU.add))
            step(dve.tensor_copy(tile_expert[:, :], expert_f[:, :]))


def experts(nc, big, ident, tile_expert, ctx_t, sorted_rows, out_rows, N, E, D):
    KT = D // P
    NS = N // P + E - 1
    m_hl = [b[:, 0:E * KT * D].rearrange("p (e k n) -> p e k n", e=E, k=KT) for b in big]
    src = sorted_rows.rearrange("(t p) d -> t p d", p=P)
    dst = out_rows.rearrange("(t p) d -> t p d", p=P)
    with ExitStack() as ctx:
        def sb(name, shape, dt=F32):
            return ctx.enter_context(nc.sbuf_tensor(name, shape, dt))

        def sem(name):
            return ctx.enter_context(nc.semaphore(name))

        raw = [sb(f"m_raw{i}", [P, KT, D]) for i in range(2)]
        rows = [sb(f"rows{i}", [P, D]) for i in range(2)]
        xt = [[sb(f"xt_{h}{i}", [P, KT, P], F32R) for i in range(2)] for h in ("hi", "lo")]
        sg = [sb(f"sg{i}", [P, D]) for i in range(2)]
        gu = [sb(f"gu{i}", [P, D]) for i in range(2)]
        gt = [[sb(f"gt_{h}{i}", [P, KT, P], F32R) for i in range(2)] for h in ("hi", "lo")]
        y = [sb(f"y{i}", [P, D]) for i in range(2)]
        bank = [ctx.enter_context(nc.psum_tensor(f"e_bank{i}", [P, 512], F32)) for i in range(8)]
        XB, UB, GB, YB = bank[0:2], bank[2:4], bank[4:6], bank[6:8]
        s_raw = [sem(f"s_mraw{i}") for i in range(2)]
        s_mh, s_ml = sem("s_mh"), sem("s_ml")
        s_rows = [sem(f"s_rows{i}") for i in range(2)]
        s_xT, s_xh, s_xl = sem("s_xT"), sem("s_xTh"), sem("s_xTl")
        s_u, s_sg, s_gu = sem("s_u"), sem("s_sg"), sem("s_gu")
        s_gT, s_gh, s_gl = sem("s_gT"), sem("s_gTh"), sem("s_gTl")
        s_y = sem("s_y")
        s_ye = [sem(f"s_ye{i}") for i in range(2)]
        s_yd = [sem(f"s_yd{i}") for i in range(2)]
        block = ctx.enter_context(nc.Block())

        def tiles(eng, step):
            step(0, 0, 0)
            with eng.Fori(0, (NS - 3) // 2) as i:
                step(2 * i + 1, 1, 1)
                step(2 * i + 2, 0, 1)
            for n in range(NS - 2, NS):
                step(n, n % 2, 1 if n < NS - 1 else 2)

        assert NS % 2 == 1

        @block.sync
        def _(sp):
            for e in range(E):
                if e >= 2:
                    sp.wait_ge(s_ml, e - 1)
                sp.dma_start(raw[e % 2][:, :, :], ctx_t[e]).then_inc(s_raw[e % 2], 16)

            def load(n, i):
                sp.wait_ge(s_xT, n - 1)
                sp.dma_start(rows[i][:, :], src[n]).then_inc(s_rows[i], 16)

            def store(n, i):
                sp.wait_ge(s_ye[i], n - i + 2)
                sp.dma_start(dst[n], y[i][:, :]).then_inc(s_yd[i], 16)

            sp.dma_start(rows[0][:, :], src[0]).then_inc(s_rows[0], 16)
            sp.dma_start(rows[1][:, :], src[1]).then_inc(s_rows[1], 16)
            store_after = lambda n, i: store(n, i)
            with sp.Fori(0, (NS - 3) // 2) as i:
                load(2 * i + 2, 0)
                store_after(2 * i, 0)
                load(2 * i + 3, 1)
                store_after(2 * i + 1, 1)
            load(NS - 1, 0)
            for n in range(NS - 3, NS):
                store(n, n % 2)
            sp.wait_ge(s_yd[0], (NS + 1) // 2 * 16)
            sp.wait_ge(s_yd[1], NS // 2 * 16)

        @block.tensor
        def _(pe):
            def x_transposes(n, i):
                pe.wait_ge(s_rows[i], (n - i) * 8 + 16)
                pe.wait_ge(s_xl, n - 1 if not isinstance(n, int) or n > 1 else 0)
                for k in range(KT):
                    ins = pe.transpose(XB[i][:, k * P:(k + 1) * P], rows[i][:, k * P:(k + 1) * P], ident[:, :])
                ins.then_inc(s_xT, 1)

            def gu_transposes(n, i):
                pe.wait_ge(s_gu, n + 1)
                if not isinstance(n, int) or n > 1:
                    pe.wait_ge(s_gl, n - 1)
                for k in range(KT):
                    ins = pe.transpose(GB[i][:, k * P:(k + 1) * P], gu[i][:, k * P:(k + 1) * P], ident[:, :])
                ins.then_inc(s_gT, 1)

            def times_expert(n, out, a):
                e = pe.value_load(tile_expert[0:1, bass.ds(n, 1)], min_val=0, max_val=E - 1)
                return matmul3(pe, out[:, :], lambda k, i: a[i][:, k, :],
                               lambda k, j: m_hl[j][:, bass.ds(e, 1), k, :].rearrange("p a n -> p (a n)"), KT)

            def step(n, i, where):
                pe.wait_ge(s_ml, E)
                pe.wait_ge(s_xl, n + 1)
                if not isinstance(n, int) or n > 1:
                    pe.wait_ge(s_gu, n - 1)
                times_expert(n, UB[i], [xt[h][i] for h in range(2)]).then_inc(s_u, 1)
                if where < 2:
                    x_transposes(n + 1, 1 - i)
                if where > 0:
                    last(n - 1, 1 - i)
                gu_transposes(n, i)

            def last(n, i):
                pe.wait_ge(s_ml, E)
                pe.wait_ge(s_gl, n + 1)
                pe.wait_ge(s_ye[i], n - i)
                times_expert(n, YB[i], [gt[h][i] for h in range(2)]).then_inc(s_y, 1)

            pe.wait_ge(s_ml, E)
            x_transposes(0, 0)
            tiles(pe, step)
            last(NS - 1, 0)

        @block.scalar
        def _(act):
            for e in range(E):
                act.wait_ge(s_raw[e % 2], 16 * (e // 2 + 1))
                act.activation(m_hl[0][:, e, :, :], raw[e % 2][:, :, :], ACT.Copy).then_inc(s_mh, 1)

            def x_hi(n, i):
                act.wait_ge(s_xT, n + 1)
                if not isinstance(n, int) or n > 1:
                    act.wait_ge(s_u, n - 1)
                act.activation(xt[0][i][:, :, :].rearrange("p k t -> p (k t)"), XB[i][:, :],
                               ACT.Copy).then_inc(s_xh, 1)

            def step(n, i, where):
                act.wait_ge(s_u, n + 1)
                if not isinstance(n, int) or n > 1:
                    act.wait_ge(s_gu, n - 1)
                act.activation(sg[i][:, :], UB[i][:, :], ACT.Silu).then_inc(s_sg, 1)
                if where < 2:
                    x_hi(n + 1, 1 - i)
                if where > 0:
                    y_out(n - 1, 1 - i)
                act.wait_ge(s_gT, n + 1)
                if not isinstance(n, int) or n > 1:
                    act.wait_ge(s_y, n - 1)
                act.activation(gt[0][i][:, :, :].rearrange("p k t -> p (k t)"), GB[i][:, :],
                               ACT.Copy).then_inc(s_gh, 1)

            def y_out(n, i):
                act.wait_ge(s_y, n + 1)
                if not isinstance(n, int) or n > 1:
                    act.wait_ge(s_yd[i], (n - i) * 8)
                act.activation(y[i][:, :], YB[i][:, :], ACT.Copy).then_inc(s_ye[i], 2)

            x_hi(0, 0)
            tiles(act, step)
            y_out(NS - 1, 0)

        @block.vector
        def _(dve):
            for e in range(E):
                dve.wait_ge(s_mh, e + 1)
                dve.tensor_tensor(m_hl[1][:, e, :, :], raw[e % 2][:, :, :], m_hl[0][:, e, :, :].bitcast(F32),
                                  ALU.subtract).then_inc(s_ml, 1)

            def lo(dst_hl, banks, i, s_in, s_out, n):
                dve.wait_ge(s_in, n + 1)
                dve.tensor_tensor(dst_hl[1][i][:, :, :].rearrange("p k t -> p (k t)"), banks[i][:, :],
                                  dst_hl[0][i][:, :, :].rearrange("p k t -> p (k t)").bitcast(F32),
                                  ALU.subtract).then_inc(s_out, 1)

            def step(n, i, where):
                dve.wait_ge(s_sg, n + 1)
                if not isinstance(n, int) or n > 1:
                    dve.wait_ge(s_gT, n - 1)
                dve.tensor_tensor(gu[i][:, :], UB[i][:, :], sg[i][:, :], ALU.mult).then_inc(s_gu, 1)
                if where < 2:
                    lo(xt, XB, 1 - i, s_xh, s_xl, n + 1)
                lo(gt, GB, i, s_gh, s_gl, n)

            lo(xt, XB, 0, s_xh, s_xl, 0)
            tiles(dve, step)


def norm_and_turn(nc, big, x2, ident, idx_all, x1_rows, expert_rows, N, D):
    KT = D // P
    NT = N // P
    G = 4
    xt = [b[:, 0:KT * N].rearrange("p (k n) -> p k n", k=KT) for b in big]
    with ExitStack() as ctx:
        def sb(name, shape, dt=F32):
            return ctx.enter_context(nc.sbuf_tensor(name, shape, dt))

        def sem(name):
            return ctx.enter_context(nc.semaphore(name))

        x1 = [sb(f"x1r{i}", [P, D]) for i in range(G)]
        yg = [sb(f"yg{i}", [P, D]) for i in range(G)]
        z = [sb(f"z2_{i}", [P, D]) for i in range(2)]
        xn = [sb(f"xn{i}", [P, D]) for i in range(G)]
        idx = sb("idx2", [P, G], I32)
        ln = LayerNorm(nc, ctx, "ln2", D)
        bank = [ctx.enter_context(nc.psum_tensor(f"n_bank{i}", [P, 512], F32)) for i in range(4)]
        s_x1 = [sem(f"s_x1r{i}") for i in range(G)]
        s_yg = [sem(f"s_yg{i}") for i in range(G)]
        s_idx, s_x2 = sem("s_idx2"), sem("s_x2")
        s_z = [sem(f"s_z2_{i}") for i in range(G)]
        s_tT, s_th = sem("s_tT"), sem("s_th")
        s_tl = [sem(f"s_tl{i}") for i in range(G)]
        s_keep = [sem(f"s_keep{i}") for i in range(G)]
        block = ctx.enter_context(nc.Block())
        rows = x1_rows.rearrange("b (r p) d -> (b r) p d", p=P)

        @block.sync
        def _(sp):
            with sp.Fori(0, NT // G) as c:
                for r in range(G):
                    sp.wait_ge(s_z[r], c)
                    sp.dma_start(x1[r][:, :], rows[c * G + r]).then_inc(s_x1[r], 16)

        @block.gpsimd
        def _(pool):
            ln.start(pool)
            with pool.Fori(0, NT // G) as c:
                for r in range(G):
                    pool.wait_ge(s_yg[r], c * 16)
                pool.tensor_copy(idx[:, :], idx_all[:, bass.ds(c * G, G)]).then_inc(s_idx, 1)
                for r in range(G):
                    wait_apart(pool, ln.s_passed[1], [(s_z[r], c)] + [(s_idx, c + 1)] * (r == 0))
                    pool.indirect_dma_start(yg[r][:, :], None, expert_rows,
                                            bass.IndirectOffsetOnAxis(idx[:, r:r + 1], 0)).then_inc(s_yg[r], 16)
                for r in range(G):
                    ln.rstd(pool, c * G + r, r)

        @block.vector
        def _(dve):
            def lo(c, r):
                dve.wait_ge(s_th, c * G + r + 1)
                t = xt[1][:, :, bass.ds((c * G + r) * P, P)]
                h = xt[0][:, :, bass.ds((c * G + r) * P, P)].bitcast(F32)
                dve.tensor_tensor(t, bank[r][:, :].rearrange("p (k t) -> p k t", k=KT), h,
                                  ALU.subtract).then_inc(s_tl[r], 1)

            with dve.Fori(0, NT // G) as c:
                for r in range(G):
                    dve.wait_ge(s_x1[r], (c + 1) * 16)
                    dve.wait_ge(s_yg[r], (c + 1) * 16)
                    dve.tensor_tensor(z[r % 2][:, :], x1[r][:, :], yg[r][:, :], ALU.add).then_inc(s_z[r], 1)
                    dve.wait_ge(s_keep[r], c)
                    ln.norm(dve, z[r % 2], xn[r], s_z[r],
                            c + 1, c * G + r, r, s_x2)
                    if r >= 1:
                        lo(c, r - 1)
                lo(c, G - 1)

        @block.tensor
        def _(pe):
            with pe.Fori(0, NT // G) as c:
                for r in range(G):
                    pe.wait_ge(s_x2, c * G + r + 1)
                    pe.wait_ge(s_tl[r], c)
                    for k in range(KT):
                        ins = pe.transpose(bank[r][:, k * P:(k + 1) * P],
                                           xn[r][:, k * P:(k + 1) * P], ident[:, :])
                    ins.then_inc(s_tT, 1)

        @block.scalar
        def _(act):
            with act.Fori(0, NT // G) as c:
                for r in range(G):
                    act.wait_ge(s_tT, c * G + r + 1)
                    act.activation(xt[0][:, :, bass.ds((c * G + r) * P, P)],
                                   bank[r][:, :].rearrange("p (k t) -> p k t", k=KT), ACT.Copy).then_inc(s_th, 1)
                    act.activation(x2[:, bass.ds(c * G + r, 1), :].rearrange("p a d -> p (a d)"), xn[r][:, :],
                                   ACT.Copy).then_inc(s_keep[r], 1)


def ffn(nc, big, x2, gate, up, down, out_rows, N, D, I):
    KT = D // P
    J = 4
    TW = 512
    RW = TW // P
    CH = J * P
    NCH = I // CH
    NR = N // TW
    GUP, DP, RING = 2 * J, J, 4
    PIECES = GUP + DP
    LINKS = 11
    xt = [b[:, 0:KT * N].rearrange("p (k n) -> p k n", k=KT) for b in big]
    with ExitStack() as ctx:
        def sb(name, shape, dt=F32):
            return ctx.enter_context(nc.sbuf_tensor(name, shape, dt))

        def sem(name):
            return ctx.enter_context(nc.semaphore(name))

        w_raw = [sb(f"fw_raw{i}", [P, D]) for i in range(RING)]
        wg = [sb(f"wg_{h}", [P, J, KT, P], F32R) for h in ("hi", "lo")]
        wu = [sb(f"wu_{h}", [P, J, KT, P], F32R) for h in ("hi", "lo")]
        wd = [sb(f"wd_{h}", [P, J, D], F32R) for h in ("hi", "lo")]
        sg = [sb(f"fsg{i}", [P, TW]) for i in range(2)]
        h = [sb(f"h{i}", [P, J, TW]) for i in range(2)]
        mag = sb("mag", [P, J, TW])
        beats = sb("beats", [P, 6, TW], BF16)
        wins = sb("wins", [P, J, TW], BF16)
        hs = [sb(f"hs_{x}", [P, J, TW], F32R) for x in ("hi", "lo")]
        ln = LayerNorm(nc, ctx, "ln3", D)
        bank = [ctx.enter_context(nc.psum_tensor(f"f_bank{i}", [P, 512], F32)) for i in range(8)]
        GB, UB, YB = bank[0:2], bank[2:4], bank[4:8]
        s_raw = [sem(f"s_fraw{i}") for i in range(RING)]
        s_ph, s_pl = sem("s_ph"), sem("s_pl")
        s_g, s_u, s_sg, s_h = sem("s_fg"), sem("s_fu"), sem("s_fsg"), sem("s_fh")
        s_mag, s_ch, s_hh, s_hl = sem("s_mag"), sem("s_ch"), sem("s_hh"), sem("s_hl")
        s_y, s_acc = sem("s_fy"), sem("s_facc")
        s_x3, s_out = sem("s_x3"), sem("s_fout")
        block = ctx.enter_context(nc.Block())

        def chunks(eng, body):
            body(0, True, False)
            with eng.Fori(1, NCH - 1) as c:
                body(c, False, False)
            body(NCH - 1, False, True)

        def gate_up(i):
            return i % 2, i // 2

        @block.sync
        def _(sp):
            def load(n, i, src):
                if not isinstance(n, int) or n >= RING:
                    sp.wait_ge(s_pl, n - RING + 1)
                sp.dma_start(w_raw[i % RING][:, :], src).then_inc(s_raw[i % RING], 16)

            def load_gate_up(c, base):
                for i in range(GUP):
                    m, j = gate_up(i)
                    load(base + i, i, (gate, up)[m][c, j])

            def body(c, first, last):
                for j in range(J):
                    load(PIECES * c + GUP + j, j, down[c][:, j, :])
                if not last:
                    load_gate_up(c + 1, PIECES * (c + 1))

            load_gate_up(0, 0)
            chunks(sp, body)
            for t in range(N // P):
                sp.wait_ge(s_x3, t + 1)
                sp.dma_start(out_rows[t], x2[:, t, :]).then_inc(s_out, 16)
            sp.wait_ge(s_out, N // P * 16)

        @block.gpsimd
        def _(pool):
            ln.start(pool)
            for t in range(N // P):
                ln.rstd(pool, t, t % 4)

        @block.tensor
        def _(pe):
            def inner(c, v):
                r, j = v // J, v % J
                n = c * NR * J + v
                for m, (w, banks, s_read, s_done) in enumerate(((wg, GB, s_sg, s_g), (wu, UB, s_h, s_u))):
                    if r == 0:
                        pe.wait_ge(s_pl, PIECES * c + 2 * j + m + 1)
                    if not isinstance(n, int) or n >= 2:
                        pe.wait_ge(s_read, n - 1)
                    matmul3(pe, banks[v % 2][:, :], lambda k, i: w[i][:, j, k, :],
                            lambda k, i: xt[i][:, k, r * TW:(r + 1) * TW], KT).then_inc(s_done, 1)

            def outer(c, r):
                n = c * NR + r
                pe.wait_ge(s_pl, PIECES * c + PIECES)
                pe.wait_ge(s_hl, n + 1)
                for t in range(RW):
                    if not isinstance(n, int) or n >= 1:
                        pe.wait_ge(s_acc, RW * (n - 1) + t + 1)
                    matmul3(pe, YB[t][:, :], lambda k, i: hs[i][:, k, t * P:(t + 1) * P],
                            lambda k, i: wd[i][:, k, :], J).then_inc(s_y, 1)

            def body(c, first, last):
                for v in range(NR * J):
                    inner(c, v)
                    if v % J == 2:
                        if v > J:
                            outer(c, v // J - 1)
                        elif not first:
                            outer(c - 1, NR - 1)

            chunks(pe, body)
            outer(NCH - 1, NR - 1)

        @block.scalar
        def _(act):
            def piece(n, i, dst, s_free=None, free=0):
                act.wait_ge(s_raw[i % RING], (n - i % RING) * (16 // RING) + 16)
                if s_free is not None:
                    act.wait_ge(s_free, free)
                act.activation(dst, w_raw[i % RING][:, :], ACT.Copy).then_inc(s_ph, 1)

            def gate_up_piece(c, i, base, guarded):
                m, j = gate_up(i)
                dst = (wg, wu)[m][0][:, j, :, :].rearrange("p k n -> p (k n)")
                if guarded:
                    piece(base + i, i, dst, (s_g, s_u)[m], c * NR * J + (NR - 1) * J + j + 1)
                else:
                    piece(base + i, i, dst)

            def silu(c, v):
                n = c * NR * J + v
                act.wait_ge(s_g, n + 1)
                if not isinstance(n, int) or n >= 2:
                    act.wait_ge(s_h, n - 1)
                act.activation(sg[v % 2][:, :], GB[v % 2][:, :], ACT.Silu).then_inc(s_sg, 1)

            def magnitudes(c, r):
                n = c * NR + r
                act.wait_ge(s_h, J * (n + 1))
                if not isinstance(n, int) or n >= 1:
                    act.wait_ge(s_ch, LINKS * (n - 1) + 3)
                act.activation(mag[:, :, :], h[r % 2][:, :, :], ACT.Abs).then_inc(s_mag, 1)

            def kept_hi(c, r):
                n = c * NR + r
                act.wait_ge(s_ch, LINKS * (n + 1))
                act.wait_ge(s_y, RW * n)
                act.activation(hs[0][:, :, :], h[r % 2][:, :, :], ACT.Copy).then_inc(s_hh, 1)

            def body(c, first, last):
                for v in range(NR * J):
                    silu(c, v)
                    if v == 3:
                        for j in range(J):
                            n = c * NR
                            piece(PIECES * c + GUP + j, j, wd[0][:, j, :], s_y, RW * n)
                    if v % J == 1 and (v > J or not first):
                        kept_hi(*((c, v // J - 1) if v > J else (c - 1, NR - 1)))
                    if v % J == J - 1:
                        magnitudes(c, v // J)
                    if v > (NR - 1) * J and not last:
                        j = v - (NR - 1) * J - 1
                        for i in (2 * j, 2 * j + 1):
                            gate_up_piece(c, i, PIECES * (c + 1), True)
                if not last:
                    for i in (2 * J - 2, 2 * J - 1):
                        gate_up_piece(c, i, PIECES * (c + 1), True)

            for i in range(GUP):
                gate_up_piece(0, i, 0, False)
            chunks(act, body)
            kept_hi(NCH - 1, NR - 1)

        @block.vector
        def _(dve):
            def piece(n, i, dst, hi):
                dve.wait_ge(s_ph, n + 1)
                dve.tensor_tensor(dst, w_raw[i % RING][:, :], hi.bitcast(F32), ALU.subtract).then_inc(s_pl, 1)

            def gate_up_piece(i, base):
                m, j = gate_up(i)
                w = (wg, wu)[m]
                piece(base + i, i, w[1][:, j, :, :].rearrange("p k n -> p (k n)"),
                      w[0][:, j, :, :].rearrange("p k n -> p (k n)"))

            def product(c, v):
                r, j = v // J, v % J
                n = c * NR * J + v
                dve.wait_ge(s_u, n + 1)
                dve.wait_ge(s_sg, n + 1)
                rr = c * NR + r
                if j == 0 and (not isinstance(rr, int) or rr >= 2):
                    dve.wait_ge(s_hh, rr - 1)
                dve.tensor_tensor(h[r % 2][:, j, :], UB[v % 2][:, :], sg[v % 2][:, :], ALU.mult).then_inc(s_h, 1)

            def pair(x, i, j):
                return x[:, i:j + 1:j - i, :]

            def compare(c, r):
                n = c * NR + r
                dve.wait_ge(s_mag, n + 1)
                for i, at in ((0, 0), (1, 3), (2, 5)):
                    w = J - 1 - i
                    dve.tensor_tensor(beats[:, at:at + w, :], mag[:, i:i + 1, :].broadcast_to([P, w, TW]),
                                      mag[:, i + 1:J, :], ALU.is_ge).then_inc(s_ch, 1)
                dve.wait_ge(s_ch, LINKS * n + 3)

            def choose(c, r):
                n = c * NR + r
                hr = h[r % 2]
                b01, b02, b03, b12, b13, b23 = range(6)
                dve.tensor_tensor(pair(wins, 0, 3), pair(beats, b01, b03), pair(beats, b02, b13),
                                  ALU.add).then_inc(s_ch, 1)
                dve.tensor_tensor(wins[:, 1, :], beats[:, b12, :], beats[:, b13, :], ALU.add).then_inc(s_ch, 1)
                dve.tensor_tensor(wins[:, 2, :], beats[:, b02, :], beats[:, b12, :], ALU.add).then_inc(s_ch, 1)
                dve.wait_ge(s_ch, LINKS * n + 6)
                dve.tensor_tensor(pair(wins, 0, 3), pair(wins, 0, 3), pair(beats, b03, b23),
                                  ALU.add).then_inc(s_ch, 1)
                dve.tensor_tensor(wins[:, 1, :], wins[:, 1, :], beats[:, b01, :], ALU.subtract)
                dve.tensor_tensor(wins[:, 2, :], wins[:, 2, :], beats[:, b23, :], ALU.subtract).then_inc(s_ch, 1)
                dve.wait_ge(s_ch, LINKS * n + 8)
                for j, (op, least) in enumerate(((ALU.is_ge, 1.5), (ALU.is_ge, 0.5), (ALU.is_le, 0.5),
                                                 (ALU.is_le, 1.5))):
                    ins = dve.scalar_tensor_tensor(out=hr[:, j, :], in0=wins[:, j, :], scalar=least,
                                                   in1=hr[:, j, :], op0=op, op1=ALU.mult)
                    if j > 0:
                        ins.then_inc(s_ch, 1)

            def kept_lo(c, r):
                n = c * NR + r
                dve.wait_ge(s_hh, n + 1)
                dve.wait_ge(s_y, RW * n)
                dve.tensor_tensor(hs[1][:, :, :], h[r % 2][:, :, :], hs[0][:, :, :].bitcast(F32),
                                  ALU.subtract).then_inc(s_hl, 1)

            def add_up(c, r, norm):
                n = c * NR + r
                for t in range(RW):
                    dve.wait_ge(s_y, RW * n + t + 1)
                    rows = x2[:, r * RW + t, :]
                    dve.tensor_tensor(rows, YB[t][:, :], rows, ALU.add).then_inc(s_acc, 1)
                    if norm:
                        i = r * RW + t
                        ln.norm(dve, rows, rows, s_acc, RW * n + t + 1, i, i % 4, s_x3)

            def body(c, first, last):
                for v in range(NR * J):
                    product(c, v)
                    prev = (c, v // J - 1) if v >= J else None if first else (c - 1, NR - 1)
                    if prev and v % J == 0:
                        compare(*prev)
                        choose(*prev)
                    if prev and v % J == 1:
                        kept_lo(*prev)
                    if prev and v % J == 3:
                        add_up(*prev, last and v >= J)
                    if v == 3:
                        for j in range(J):
                            piece(PIECES * c + GUP + j, j, wd[1][:, j, :], wd[0][:, j, :])
                    if v > (NR - 1) * J and not last:
                        j = v - (NR - 1) * J - 1
                        for i in (2 * j, 2 * j + 1):
                            gate_up_piece(i, PIECES * (c + 1))
                if not last:
                    for i in (2 * J - 2, 2 * J - 1):
                        gate_up_piece(i, PIECES * (c + 1))

            for i in range(GUP):
                gate_up_piece(i, 0)
            chunks(dve, body)
            last = (NCH - 1, NR - 1)
            compare(*last)
            choose(*last)
            kept_lo(*last)
            add_up(*last, True)


def build(nc, x, x_t, tok, ctx_t, wq, wk, wv, wo, gate, up, down, out):
    B, T, D = x.shape
    N = B * T
    E = ctx_t.shape[0]
    I = down.shape[0]
    VOCAB = 25000
    KT = D // P
    NS = N // P + E - 1

    def scratch(name, shape):
        return nc.dram_tensor(name, shape, F32, kind="Internal").ap()

    qk_dram = [[scratch(f"{n}_{h}_dram", [P, T]) for h in ("hi", "lo")] for n in "qk"]
    x1_rows = scratch("x1_dram", [B, T, D])
    sorted_rows = scratch("sorted_dram", [NS * P, D])
    expert_rows = scratch("expert_dram", [NS * P, D])
    with ExitStack() as ctx:
        def sb(name, shape, dt):
            return ctx.enter_context(nc.sbuf_tensor(name, shape, dt))

        ident = sb("ident", [P, P], F32)
        idx_all = sb("idx_all", [P, N // P], I32)
        tile_expert = sb("tile_expert", [P, NS], I32)
        route(nc, tok, idx_all, tile_expert, sorted_rows, N, E, VOCAB, D)
        with ExitStack() as wctx:
            w_split = [[wctx.enter_context(nc.sbuf_tensor(f"w{n}_{h}", [P, KT, D], F32R)) for n in "qkvo"]
                       for h in ("hi", "lo")]
            setup(nc, [w.rearrange("(k p) n -> p k n", p=P) for w in (wq, wk, wv, wo)], w_split, ident, D)
            attention(nc, w_split, ident, idx_all, x_t.rearrange("b (k p) t -> b p k t", p=P),
                      x.rearrange("b (r p) d -> b p r d", p=P),
                      x1_rows.rearrange("b (r p) d -> b p r d", p=P), sorted_rows, qk_dram, B, T, D)
        big = [sb(f"big_{h}", [P, max(E * KT * D, KT * N)], F32R) for h in ("hi", "lo")]
        experts(nc, big, ident, tile_expert, ctx_t.rearrange("e (k p) n -> e p k n", p=P), sorted_rows,
                expert_rows, N, E, D)
        x2 = sb("x2", [P, N // P, D], F32)
        norm_and_turn(nc, big, x2, ident, idx_all, x1_rows, expert_rows, N, D)
        ffn(nc, big, x2, gate, up, down.rearrange("(c p j) n -> c p j n", p=P, j=4),
            out.rearrange("b (r p) d -> (b r) p d", p=P), N, D, I)


def kernel(x, itok_BxS_13_99985, ctx_2048, L0_attn_Wq, L0_attn_Wk, L0_attn_Wv, L0_attn_Wo, L0_ffn_w_gate,
           L0_ffn_w_up, L0_ffn_w_down):
    import numpy as np
    from concourse import bacc
    from concourse.bass_utils import run_bass_kernel_spmd

    def by_group(w):
        d, i = w.shape
        w = w.reshape(d // P, P, i // 512, P, 4)
        return np.ascontiguousarray(w.transpose(2, 4, 1, 0, 3)).reshape(i // 512, 4, P, d)

    x = np.asarray(x)
    arrays = {
        "x": x,
        "x_t": np.ascontiguousarray(x.transpose(0, 2, 1)),
        "tok": np.ascontiguousarray(np.asarray(itok_BxS_13_99985).reshape(-1, P).T),
        "ctx_t": np.ascontiguousarray(np.asarray(ctx_2048).transpose(0, 2, 1)),
        "wq": np.asarray(L0_attn_Wq),
        "wk": np.asarray(L0_attn_Wk),
        "wv": np.asarray(L0_attn_Wv),
        "wo": np.asarray(L0_attn_Wo),
        "gate": by_group(np.asarray(L0_ffn_w_gate)),
        "up": by_group(np.asarray(L0_ffn_w_up)),
        "down": np.asarray(L0_ffn_w_down),
    }
    nc = bacc.Bacc("TRN2", target_bir_lowering=False, num_devices=1)
    aps = [nc.dram_tensor(n, a.shape, mybir.dt.from_np(a.dtype), kind="ExternalInput").ap()
           for n, a in arrays.items()]
    out = nc.dram_tensor("out", x.shape, F32, kind="ExternalOutput").ap()
    build(nc, *aps, out)
    got = run_bass_kernel_spmd(nc, [arrays], core_ids=[0])
    return got.results[0]["out"]
```

```python
from contextlib import ExitStack

import concourse.bass as bass
from concourse import mybir

F32 = mybir.dt.float32
F32R = mybir.dt.float32r
BF16 = mybir.dt.bfloat16
F16 = mybir.dt.float16
I32 = mybir.dt.int32
ALU = mybir.AluOpType
ACT = mybir.ActivationFunctionType
AX = mybir.AxisListType

P = 128
HEADS = 16
EPS = 1e-5
NEG = -3.0e38


def wait_apart(eng, passed, waits):
    for sem, value in waits:
        eng.wait_ge(sem, value)
    eng.sem_inc(passed, 1)


def matmul3(pe, out, a, b, steps, first=0, last=None):
    chain = [(k, i, j) for k in range(steps) for i, j in ((0, 0), (0, 1), (1, 0))]
    last = len(chain) if last is None else last
    for n in range(first, last):
        k, i, j = chain[n]
        ins = pe.matmul(out, a(k, i), b(k, j), start=(n == 0), stop=(n == len(chain) - 1))
    return ins


def attention(nc, w_split, ident, idx_all, x_t, x_rows, x1_rows, sorted_rows, scratch, B, T, D):
    KT = D // P
    NB = T // P
    HD = D // HEADS
    SLOTS = P // HD
    HPT = P // HD
    NM = D // P
    UPM = HPT * NB
    UPB = NM * UPM
    AHEAD_S, AHEAD_MAX, AHEAD_HI, AHEAD_LO, AHEAD_V = 2, 1, -1, -1, -2
    RP = 4
    scale = 1.0 / float(T) ** 0.5

    wh, wl = w_split
    with ExitStack() as ctx:
        def sb(name, shape, dt):
            return ctx.enter_context(nc.sbuf_tensor(name, shape, dt))

        def sem(name):
            return ctx.enter_context(nc.semaphore(name))

        x_raw = sb("x_raw", [P, KT * T], F32)
        x_turned = x_raw[:, :].rearrange("p (k t) -> p k t", k=KT)
        x_res = x_raw[:, :].rearrange("p (r d) -> p r d", r=NB)
        x_hl = [sb("x_hi", [P, KT, T], F32R), sb("x_lo", [P, KT, T], F32R)]
        qk_hl = [[sb(f"{n}_{h}", [P, T], F32R) for h in ("hi", "lo")] for n in "qk"]
        stack = [[sb(f"{n}_stack{i}", [P, HPT, T], F32R) for i in range(2)] for n in "qk"]
        v3 = sb("v3", [P, NB, 3, D], BF16)
        v_rest = [sb(f"v_rest{i}", [P, D], F32) for i in range(2)]
        v_tail = sb("v_tail", [P, NB - 1, D], F32)
        probs = [sb(f"probs{i}", [P, T], F32) for i in range(RP)]
        pt_hi = [sb(f"pt_hi{i}", [P, T], F16) for i in range(RP)]
        pt_lo = [sb(f"pt_lo{i}", [P, T], F16) for i in range(RP)]
        o_raw = sb("o_raw", [P, NB, HEADS, HD], F32)
        o_tmp = [sb(f"o_tmp{i}", [P, NB - 1, HPT, HD], F32) for i in range(2)]
        ot_hl = [[sb(f"ot_{h}{i}", [P, KT, P], F32R) for i in range(2)] for h in ("hi", "lo")]
        mask = sb("mask", [P, T], F32)
        minus_one = sb("minus_one", [P, 1], F32)
        ones_bf = sb("ones_bf", [P, P], BF16)
        smax = sb("smax", [P, NB, HEADS], F32)
        nmax = sb("nmax", [P, NB, HEADS], F32)
        rsum = sb("rsum", [P, NB, HEADS], F32)
        c_up = sb("c_up", [P, NB, HEADS], F32)
        n_up = sb("n_up", [P, NB, HEADS], F32)
        den = sb("den", [P, NB, HEADS], F32)
        den2 = sb("den2", [P, NB, HEADS], F32)
        rinv = sb("rinv", [P, NB, HEADS], F32)
        z = [sb(f"z{i}", [P, D], F32) for i in range(2)]
        x1 = [sb(f"x1_{i}", [P, D], F32) for i in range(2)]
        idx = sb("idx", [P, NB], I32)
        s_sc = [sem(f"s_sc{i}") for i in range(2)]
        s_idx = sem("s_idx")
        ln = LayerNorm(nc, ctx, "ln1", D)
        bank = [ctx.enter_context(nc.psum_tensor(f"bank{i}", [P, 512], F32)) for i in range(8)]
        S, TP, OB, PJ = bank[0:3], bank[3:5], bank[5:7], bank[7]
        VB, SF, OT, WB = bank[0:4], bank[0:3], bank[5:7], (bank[4], bank[7])
        SR, TR, OR = len(S), len(TP), len(OB)

        s_const = sem("s_const")
        s_passed, s_passed_sp = sem("s_passed"), sem("s_passed_sp")
        s_xraw = sem("s_xraw")
        s_xh = sem("s_xh")
        s_xl = sem("s_xl")
        s_xres = sem("s_xres")
        s_vp = sem("s_vp")
        s_v0 = sem("s_v0")
        s_vr = sem("s_vr")
        s_v1 = sem("s_v1")
        s_v2 = sem("s_v2")
        s_sf = sem("s_sf")
        s_sfe = sem("s_sfe")
        s_pj = sem("s_pj")
        s_pjh = sem("s_pjh")
        s_pjl = sem("s_pjl")
        s_dw = sem("s_dw")
        s_st = [sem("s_stq"), sem("s_stk")]
        s_S = sem("s_S")
        s_mx = sem("s_mx")
        s_nm = sem("s_nm")
        s_e = sem("s_e")
        s_T = sem("s_T")
        s_hi = sem("s_hi")
        s_lo = sem("s_lo")
        s_pv = sem("s_pv")
        s_oe = sem("s_oe")
        s_c = sem("s_c")
        s_t = [sem("s_t_pool"), sem("s_t_dve")]
        s_on = [sem("s_on_pool"), sem("s_on_dve")]
        s_ot = sem("s_ot")
        s_oth = sem("s_oth")
        s_otl = sem("s_otl")
        s_wo = sem("s_wo")
        s_z = sem("s_z")
        s_x1 = sem("s_x1")
        s_x1d = [sem(f"s_x1d{i}") for i in range(2)]

        row_blocks = [(NB - 1 - n // 2) if n % 2 == 0 else n // 2 for n in range(NB)]
        units = [(u // UPM, (u // NB) % HPT, row_blocks[u % NB]) for u in range(UPB)]

        starts = {4: (2, 2), 5: (9, 2), 6: (17, 2), 7: (24, 2),
                  8: (38, 2), 9: (45, 2), 10: (52, 2), 11: (59, 3)}
        pieces = {}
        for g, (first, n) in starts.items():
            for i in range(0, 3 * KT, n):
                pieces[first + i // n] = (g, i, i + n)
        split_at = {first + 3 * KT // n: g for g, (first, n) in starts.items()}
        x_split_at = {31 + 2 * k: k for k in range(KT)}
        G_AHEAD = 4
        between = [("v", 0), ("turn", 0), ("turn", 1), ("v", 2), ("out", 0), ("turn", 2), ("out", 1),
                   ("turn", 3), ("out", 2), ("out", 3), ("sums", 0)]

        def cols(r):
            return (r + 1) * P

        def norm_heads(eng, side, b, m):
            per_batch = (NM - 1, 1)[side]
            n = (b * per_batch + (m if side == 0 else 0)) * 5
            hs = slice(m * HPT, (m + 1) * HPT)
            count = [0]

            def link(ins):
                count[0] += 1
                ins.then_inc(s_t[side], 1)
                eng.wait_ge(s_t[side], n + count[0])

            eng.wait_ge(s_e, b * UPB + (m + 1) * UPM)
            eng.wait_ge(s_c, b * NM + m + 1)
            eng.wait_ge(s_oe, b * NM + m + 1)
            link(eng.tensor_tensor(den[:, :, hs], c_up[:, :, hs], n_up[:, :, hs], ALU.mult))
            link(eng.tensor_tensor(den2[:, :, hs], den[:, :, hs], rsum[:, :, hs], ALU.add))
            if side == 0:
                link(eng.tensor_tensor(rinv[:, :, hs], den2[:, :, hs],
                                       minus_one[:, :].unsqueeze(2).broadcast_to([P, NB, HPT]), ALU.pow))
            else:
                link(eng.reciprocal(rinv[:, :, hs], den2[:, :, hs]))
            link(eng.tensor_tensor(o_tmp[side][:, :, :, :],
                                   v_tail[:, :, m * P:(m + 1) * P].rearrange("p r (h d) -> p r h d", h=HPT),
                                   c_up[:, 0:NB - 1, hs].unsqueeze(3).broadcast_to([P, NB - 1, HPT, HD]), ALU.mult))
            link(eng.tensor_tensor(o_raw[:, 0:NB - 1, hs, :], o_raw[:, 0:NB - 1, hs, :], o_tmp[side][:, :, :, :],
                                   ALU.add))
            ins = eng.tensor_tensor(o_raw[:, :, hs, :], o_raw[:, :, hs, :],
                                    rinv[:, :, hs].unsqueeze(3).broadcast_to([P, NB, HPT, HD]), ALU.mult)
            ins.then_inc(s_on[side], 1)

        block = ctx.enter_context(nc.Block())

        @block.gpsimd
        def _(pool):
            pool.memset(mask[:, :], 1.0).then_inc(s_const, 1)
            ln.start(pool)
            pool.memset(ones_bf[:, :], 1.0).then_inc(s_const, 1)
            pool.memset(minus_one[:, :], -1.0).then_inc(s_const, 1)
            for r in range(NB):
                pool.memset(n_up[:, r, :], float((NB - 1 - r) * P)).then_inc(s_const, 1)
            pool.wait_ge(s_const, 3 + NB)
            pool.affine_select(out=mask[:, T - P:T], in_=mask[:, T - P:T], compare_op=ALU.is_ge, fill=0.0,
                               base=0, pattern=[[-1, P]], channel_multiplier=1).then_inc(s_const, 1)
            with pool.Fori(0, B) as b:
                for i in range(2):
                    pool.wait_ge(s_sc[i], b * (NB // 2) * 16)
                pool.tensor_copy(idx[:, :], idx_all[:, bass.ds(b * NB, NB)]).then_inc(s_idx, 1)
                for m in range(NM - 1):
                    norm_heads(pool, 0, b, m)
                for n in range(NB + 1):
                    if n < NB:
                        ln.rstd(pool, b * NB + n, n)
                    if n > 0:
                        r = n - 1
                        wait_apart(pool, ln.s_passed[1], [(s_x1, b * NB + r + 1)] + [(s_idx, b + 1)] * (r == 0))
                        pool.indirect_dma_start(sorted_rows, bass.IndirectOffsetOnAxis(idx[:, r:r + 1], 0),
                                                x1[r % 2][:, :], None).then_inc(s_sc[r % 2], 16)
            for i in range(2):
                pool.wait_ge(s_sc[i], B * (NB // 2) * 16)

        NCONST = 4 + NB

        @block.sync
        def _(sp):
            def stack_up(b, g):
                m, side = g // 2, g % 2
                hd = scratch[side]
                sp.wait_ge(s_pjh, b * 2 * NM + g + 1)
                sp.dma_start(hd[0], qk_hl[side][0][:, :].bitcast(F32)).then_inc(s_dw, 16)
                sp.wait_ge(s_pjl, b * 2 * NM + g + 1)
                sp.dma_start(hd[1], qk_hl[side][1][:, :].bitcast(F32)).then_inc(s_dw, 16)
                wait_apart(sp, s_passed_sp, [(s_dw, (b * 2 * NM + g + 1) * 32)])
                sp.wait_ge(s_S, b * UPB + max(m - 1, 0) * UPM)
                order = (0, 1, 0, 1) if side == 0 else (0, 0, 1, 1)
                for slot, half in enumerate(order):
                    sp.dma_start(stack[side][m % 2][slot * HD:(slot + 1) * HD, :, :].bitcast(F32),
                                 hd[half].rearrange("(h r) t -> r h t", r=HD)).then_inc(s_st[side], 16)

            def batch(b, more):
                if more:
                    wait_apart(sp, s_passed_sp, [(s_xl, (b + 1) * KT)])
                    sp.wait_ge(s_z, b * NB)
                    sp.dma_start(x_turned, x_t[b + 1]).then_inc(s_xraw, 16)
                for g in range(G_AHEAD, 2 * NM):
                    stack_up(b, g)
                sp.wait_ge(s_xl, (b + 1 + more) * KT)
                if not more:
                    sp.wait_ge(s_z, b * NB)
                sp.dma_start(x_res, x_rows[b]).then_inc(s_xres, 16)
                if more:
                    for g in range(2 * NM, 2 * NM + G_AHEAD):
                        stack_up(b, g)
                for r in range(NB):
                    sp.wait_ge(s_x1, b * NB + r + 1)
                    sp.dma_start(x1_rows[b][:, r, :], x1[r % 2][:, :]).then_inc(s_x1d[r % 2], 16)

            sp.dma_start(x_turned, x_t[0]).then_inc(s_xraw, 16)
            for g in range(G_AHEAD):
                stack_up(0, g)
            with sp.Fori(0, B - 1) as b:
                batch(b, True)
            batch(B - 1, False)
            for i in range(2):
                sp.wait_ge(s_x1d[i], B * NB // 2 * 16)

        @block.tensor
        def _(pe):
            pe.wait_ge(s_const, NCONST)

            def project(b, g, first, last):
                m, side = g // 2 % NM, g % 2
                if first == 0:
                    pe.wait_ge(s_xl, (b + 1 + g // (2 * NM)) * KT)
                    pe.wait_ge(s_pjl, b * 2 * NM + g)
                ins = matmul3(pe, PJ[:, :], lambda k, i: (wh, wl)[i][side][:, k, m * P:(m + 1) * P],
                              lambda k, j: x_hl[j][:, k, :], KT, first, last)
                if last == 3 * KT:
                    ins.then_inc(s_pj, 1)

            def scores(b, u):
                m, h, r = units[u]
                if u % UPM == 0:
                    for side in range(2):
                        pe.wait_ge(s_st[side], (b * NM + m + 1) * 16 * SLOTS)
                if u >= SR:
                    pe.wait_ge(s_e, b * UPB + u - SR + 1)
                pe.matmul(S[u % SR][:, 0:cols(r)], stack[0][m % 2][:, h, r * P:(r + 1) * P],
                          stack[1][m % 2][:, h, 0:cols(r)], start=True, stop=True).then_inc(s_S, 1)

            def transposes(b, u):
                _, _, r = units[u]
                pe.wait_ge(s_e, b * UPB + u + 1)
                if u >= TR:
                    pe.wait_ge(s_lo, b * UPB + u - TR + 1)
                for j in range(r + 1):
                    ins = pe.transpose(TP[u % TR][:, j * P:(j + 1) * P], probs[u % RP][:, j * P:(j + 1) * P],
                                       ident[:, :])
                ins.then_inc(s_T, 1)

            def values(b, u):
                m, h, r = units[u]
                if u % UPM == 0 and m >= OR:
                    pe.wait_ge(s_oe, b * NM + m - OR + 1)
                pe.wait_ge(s_lo, b * UPB + u + 1)
                out = OB[m % OR][:, (h * NB + r) * HD:(h * NB + r + 1) * HD]
                c = (m * HPT + h) * HD
                chain = [(j, half, part) for j in range(r + 1)
                         for half, part in ((0, 0), (0, 1), (0, 2), (1, 0), (1, 1))]
                for n, (j, half, part) in enumerate(chain):
                    p = (pt_hi, pt_lo)[half][u % RP][:, j * P:(j + 1) * P]
                    ins = pe.matmul(out, p, v3[:, j, part, c:c + HD], start=(n == 0), stop=(n == len(chain) - 1))
                ins.then_inc(s_pv, 1)

            def v_product(j):
                matmul3(pe, VB[j][:, :], lambda k, i: x_hl[i][:, k, j * P:(j + 1) * P],
                        lambda k, i: (wh, wl)[i][2][:, k, :], KT).then_inc(s_vp, 1)

            def v_sums(b):
                pe.wait_ge(s_v2, (b + 1) * NB)
                for n in range(NB - 1):
                    for part in range(3):
                        ins = pe.matmul(SF[n][:, :], ones_bf[:, :], v3[:, NB - 1 - n, part, :],
                                        start=(part == 0), stop=(part == 2))
                    ins.then_inc(s_sf, 1)

            def turn_heads(b, r):
                if r == 0:
                    pe.wait_ge(s_on[0], (b + 1) * (NM - 1))
                    pe.wait_ge(s_on[1], b + 1)
                if r >= 2:
                    pe.wait_ge(s_otl, b * NB + r - 1)
                for k in range(KT):
                    ins = pe.transpose(OT[r % 2][:, k * P:(k + 1) * P],
                                       o_raw[:, r, k * HPT:(k + 1) * HPT, :].rearrange("p h d -> p (h d)"),
                                       ident[:, :])
                ins.then_inc(s_ot, 1)

            def out_product(b, r):
                pe.wait_ge(s_otl, b * NB + r + 1)
                if r >= 2:
                    pe.wait_ge(s_z, b * NB + r - 1)
                matmul3(pe, WB[r % 2][:, :], lambda k, i: ot_hl[i][r % 2][:, k, :],
                        lambda k, i: (wh, wl)[i][3][:, k, :], KT).then_inc(s_wo, 1)

            def batch(b, more):
                pe.wait_ge(s_sfe, (b + 1) * (NB - 1))
                for u in range(-AHEAD_S, UPB - AHEAD_V):
                    if u + AHEAD_S < UPB:
                        scores(b, u + AHEAD_S)
                    if u == 0:
                        pe.wait_ge(s_z, b * NB)
                    if 0 <= u < UPB:
                        transposes(b, u)
                    if u in pieces and (more or pieces[u][0] < 2 * NM):
                        project(b, *pieces[u])
                    if u + AHEAD_V >= 0:
                        values(b, u + AHEAD_V)
                for step, r in between:
                    if step == "v" and more:
                        v_product(r)
                        v_product(r + 1)
                    elif step == "turn":
                        turn_heads(b, r)
                    elif step == "out":
                        out_product(b, r)
                    elif step == "sums" and more:
                        v_sums(b + 1)

            for g in range(G_AHEAD):
                project(0, g, 0, 3 * KT)
                v_product(g)
            v_sums(0)
            with pe.Fori(0, B - 1) as b:
                batch(b, True)
            batch(B - 1, False)

        @block.scalar
        def _(act):
            act.wait_ge(s_const, NCONST)

            def split_proj(b, g):
                side = g % 2
                act.wait_ge(s_pj, b * 2 * NM + g + 1)
                act.wait_ge(s_dw, b * 2 * NM * 32 + max(g - 1, 0) * 32)
                act.activation(qk_hl[side][0][:, :], PJ[:, :], ACT.Copy,
                               scale=(scale if side == 0 else 1.0)).then_inc(s_pjh, 1)

            def exps(b, u):
                m, h, r = units[u]
                c = m * HPT + h
                act.wait_ge(s_nm, b * UPB + u + 1)
                if u >= RP:
                    act.wait_ge(s_T, b * UPB + u - RP + 1)
                act.activation(probs[u % RP][:, 0:cols(r)], S[u % SR][:, 0:cols(r)], ACT.Exp,
                               bias=nmax[:, r, c:c + 1], accum_out=rsum[:, r, c:c + 1]).then_inc(s_e, 1)

            def hi(b, u):
                _, _, r = units[u]
                act.wait_ge(s_T, b * UPB + u + 1)
                if u >= RP:
                    act.wait_ge(s_pv, b * UPB + u - RP + 1)
                act.activation(pt_hi[u % RP][:, 0:cols(r)], TP[u % TR][:, 0:cols(r)], ACT.Copy).then_inc(s_hi, 1)

            def x_split(b, k):
                act.wait_ge(s_xraw, (b + 1) * 16)
                act.activation(x_hl[0][:, k, :], x_turned[:, k, :], ACT.Copy).then_inc(s_xh, 1)

            def v_split(b, blocks):
                for j in blocks:
                    act.wait_ge(s_vp, b * NB + j + 1)
                    act.activation(v3[:, j, 0, :], VB[j][:, :], ACT.Copy).then_inc(s_v0, 1)
                for j in blocks:
                    act.wait_ge(s_vr, b * NB + j + 1)
                    act.activation(v3[:, j, 1, :], v_rest[j % 2][:, :], ACT.Copy).then_inc(s_v1, 1)

            def turned_hi(b, r):
                act.wait_ge(s_ot, b * NB + r + 1)
                if r >= 2:
                    act.wait_ge(s_wo, b * NB + r - 1)
                act.activation(ot_hl[0][r % 2][:, :, :].rearrange("p k t -> p (k t)"), OT[r % 2][:, :],
                               ACT.Copy).then_inc(s_oth, 1)

            def above(b, m):
                act.wait_ge(s_nm, b * UPB + (m + 1) * UPM)
                act.activation(c_up[:, :, m * HPT:(m + 1) * HPT], nmax[:, :, m * HPT:(m + 1) * HPT],
                               ACT.Exp).then_inc(s_c, 1)

            def batch(b, more):
                for u in range(UPB - AHEAD_HI):
                    if u < UPB:
                        exps(b, u)
                    if u + AHEAD_HI >= 0:
                        hi(b, u + AHEAD_HI)
                    if u in split_at and (more or split_at[u] < 2 * NM):
                        split_proj(b, split_at[u])
                    if more and u in x_split_at:
                        if x_split_at[u] == 0:
                            act.wait_ge(s_pj, (b + 1) * 2 * NM)
                        x_split(b + 1, x_split_at[u])
                    if u % UPM == 1 and UPM < u < UPB:
                        above(b, u // UPM - 1)
                above(b, NM - 1)
                act.wait_ge(s_pv, (b + 1) * UPB)
                for step, r in between:
                    if step == "v" and more:
                        v_split(b + 1, (r, r + 1))
                    elif step == "turn":
                        turned_hi(b, r)

            for k in range(KT):
                x_split(0, k)
            for g in range(G_AHEAD):
                split_proj(0, g)
                v_split(0, (g,))
            with act.Fori(0, B - 1) as b:
                batch(b, True)
            batch(B - 1, False)

        @block.vector
        def _(dve):
            dve.wait_ge(s_const, NCONST)

            def split_proj(b, g):
                side = g % 2
                dve.wait_ge(s_pjh, b * 2 * NM + g + 1)
                dve.scalar_tensor_tensor(out=qk_hl[side][1][:, :], in0=PJ[:, :],
                                         scalar=(scale if side == 0 else 1.0),
                                         in1=qk_hl[side][0][:, :].bitcast(F32), op0=ALU.mult,
                                         op1=ALU.subtract).then_inc(s_pjl, 1)

            def maxima(b, u):
                m, h, r = units[u]
                c = m * HPT + h
                wait_apart(dve, s_passed, [(s_S, b * UPB + u + 1)])
                dve.tensor_tensor_reduce(out=S[u % SR][:, 0:cols(r)], in0=S[u % SR][:, 0:cols(r)],
                                         in1=mask[:, T - cols(r):T], scale=1.0, scalar=NEG, op0=ALU.mult,
                                         op1=ALU.max, accum_out=smax[:, r, c:c + 1]).then_inc(s_mx, 1)
                dve.wait_ge(s_mx, b * UPB + u + 1)
                if r < NB - 1:
                    dve.tensor_scalar(nmax[:, r, c:c + 1], smax[:, r, c:c + 1], 0.0, -1.0, ALU.max,
                                      ALU.mult).then_inc(s_nm, 1)
                else:
                    dve.tensor_scalar(nmax[:, r, c:c + 1], smax[:, r, c:c + 1], -1.0, None,
                                      ALU.mult).then_inc(s_nm, 1)

            def lo(b, u):
                _, _, r = units[u]
                dve.wait_ge(s_hi, b * UPB + u + 1)
                dve.tensor_tensor(pt_lo[u % RP][:, 0:cols(r)], TP[u % TR][:, 0:cols(r)],
                                  pt_hi[u % RP][:, 0:cols(r)], ALU.subtract).then_inc(s_lo, 1)

            def copy_out(b, m):
                dve.wait_ge(s_pv, b * UPB + (m + 1) * UPM)
                dve.tensor_copy(o_raw[:, :, m * HPT:(m + 1) * HPT, :].rearrange("p r h d -> p h r d"),
                                OB[m % OR][:, :].rearrange("p (h r d) -> p h r d", h=HPT, r=NB)).then_inc(s_oe, 1)

            def x_split(b, k):
                dve.wait_ge(s_xh, b * KT + k + 1)
                dve.tensor_tensor(x_hl[1][:, k, :], x_turned[:, k, :], x_hl[0][:, k, :].bitcast(F32),
                                  ALU.subtract).then_inc(s_xl, 1)

            def v_split(b, blocks):
                for j in blocks:
                    dve.wait_ge(s_v0, b * NB + j + 1)
                    dve.wait_ge(s_v2, b * NB + max(j - 1, 0))
                    dve.tensor_tensor(v_rest[j % 2][:, :], VB[j][:, :], v3[:, j, 0, :],
                                      ALU.subtract).then_inc(s_vr, 1)
                for j in blocks:
                    dve.wait_ge(s_v1, b * NB + j + 1)
                    dve.tensor_tensor(v3[:, j, 2, :], v_rest[j % 2][:, :], v3[:, j, 1, :],
                                      ALU.subtract).then_inc(s_v2, 1)

            def v_above(b):
                for n in range(NB - 1):
                    r = NB - 2 - n
                    dve.wait_ge(s_sf, b * (NB - 1) + n + 1)
                    if n == 0:
                        dve.tensor_copy(v_tail[:, r, :], SF[n][:, :]).then_inc(s_sfe, 1)
                    else:
                        dve.wait_ge(s_sfe, b * (NB - 1) + n)
                        dve.tensor_tensor(v_tail[:, r, :], SF[n][:, :], v_tail[:, r + 1, :],
                                          ALU.add).then_inc(s_sfe, 1)

            def turned_lo(b, r):
                dve.wait_ge(s_oth, b * NB + r + 1)
                if r >= 2:
                    dve.wait_ge(s_wo, b * NB + r - 1)
                dve.tensor_tensor(ot_hl[1][r % 2][:, :, :].rearrange("p k t -> p (k t)"), OT[r % 2][:, :],
                                  ot_hl[0][r % 2][:, :, :].rearrange("p k t -> p (k t)").bitcast(F32),
                                  ALU.subtract).then_inc(s_otl, 1)

            def add_x(b, r):
                dve.wait_ge(s_wo, b * NB + r + 1)
                dve.wait_ge(s_xres, (b + 1) * 16)
                dve.wait_ge(s_x1, b * NB + max(r - 1, 0))
                dve.tensor_tensor(z[r % 2][:, :], WB[r % 2][:, :], x_res[:, r, :], ALU.add).then_inc(s_z, 1)
                ln.statistics(dve, z[r % 2], s_z, b * NB + r + 1, b * NB + r, r)

            def norm_rows(b, r):
                dve.wait_ge(s_x1d[r % 2], (b * (NB // 2) + r // 2) * 16)
                dve.wait_ge(s_sc[r % 2], (b * (NB // 2) + r // 2) * 16)
                ln.scale(dve, z[r % 2], x1[r % 2], b * NB + r, r, s_x1)

            def batch(b, more):
                for u in range(-AHEAD_MAX, UPB - AHEAD_LO):
                    if u + AHEAD_MAX < UPB:
                        maxima(b, u + AHEAD_MAX)
                    if u + AHEAD_LO >= 0:
                        lo(b, u + AHEAD_LO)
                    if u in split_at and (more or split_at[u] < 2 * NM):
                        split_proj(b, split_at[u])
                    if more and u in x_split_at:
                        x_split(b + 1, x_split_at[u])
                    if u % UPM == 1 - AHEAD_V and UPM <= u < UPB:
                        copy_out(b, u // UPM - 1)
                copy_out(b, NM - 1)
                norm_heads(dve, 1, b, NM - 1)
                for step, r in between:
                    if step == "v" and more:
                        v_split(b + 1, (r, r + 1))
                    elif step == "turn":
                        turned_lo(b, r)
                    elif step == "out":
                        add_x(b, r)
                        if r >= 1:
                            norm_rows(b, r - 1)
                    elif step == "sums" and more:
                        v_above(b + 1)
                norm_rows(b, NB - 1)

            for k in range(KT):
                x_split(0, k)
            for g in range(G_AHEAD):
                split_proj(0, g)
                v_split(0, (g,))
            v_above(0)
            with dve.Fori(0, B - 1) as b:
                batch(b, True)
            batch(B - 1, False)


class LayerNorm:

    def __init__(self, nc, ctx, name, D, ring=4):
        self.D = D
        sb = lambda n, shape: ctx.enter_context(nc.sbuf_tensor(f"{name}_{n}", shape, F32))
        self.stats = sb("stats", [P, ring, 6])
        self.mv = sb("mv", [P, ring, 2])
        self.var = sb("var", [P, ring, 1])
        self.r = sb("r", [P, ring, 1])
        self.half = sb("half", [P, 1])
        self.s_half = ctx.enter_context(nc.semaphore(f"{name}_s_half"))
        self.s_passed = [ctx.enter_context(nc.semaphore(f"{name}_s_passed{i}")) for i in range(2)]
        self.s_st = ctx.enter_context(nc.semaphore(f"{name}_s_stats"))
        self.s_mv = ctx.enter_context(nc.semaphore(f"{name}_s_mv"))
        self.s_ve = ctx.enter_context(nc.semaphore(f"{name}_s_ve"))
        self.s_r = ctx.enter_context(nc.semaphore(f"{name}_s_r"))

    def start(self, pool):
        pool.memset(self.half[:, :], -0.5).then_inc(self.s_half, 1)

    def norm(self, dve, z, out, s_z, z_count, n, i, s_out):
        self.statistics(dve, z, s_z, z_count, n, i)
        self.scale(dve, z, out, n, i, s_out)

    def statistics(self, dve, z, s_z, z_count, n, i):
        dve.wait_ge(s_z, z_count)
        dve.bn_stats(self.stats[:, i, :], z[:, :]).then_inc(self.s_st, 1)
        wait_apart(dve, self.s_passed[0], [(self.s_st, n + 1)])
        dve.bn_aggr(self.mv[:, i, :], self.stats[:, i, :]).then_inc(self.s_mv, 1)

    def scale(self, dve, z, out, n, i, s_out):
        dve.wait_ge(self.s_r, n + 1)
        dve.tensor_scalar(out[:, :], z[:, :], self.mv[:, i, 0:1], self.r[:, i, :], ALU.subtract,
                          ALU.mult).then_inc(s_out, 1)

    def rstd(self, pool, n, i):
        wait_apart(pool, self.s_passed[1], [(self.s_mv, n + 1)])
        pool.tensor_scalar(self.var[:, i, :], self.mv[:, i, 1:2], EPS, None, ALU.add).then_inc(self.s_ve, 1)
        pool.wait_ge(self.s_ve, n + 1)
        pool.tensor_tensor(self.r[:, i, :], self.var[:, i, :], self.half[:, :], ALU.pow).then_inc(self.s_r, 1)


def setup(nc, w_dram, w_split, ident, D):
    KT = D // P
    wh, wl = w_split
    n_w = len(w_dram)
    with ExitStack() as ctx:
        raw = [ctx.enter_context(nc.sbuf_tensor(f"w_raw{i}", [P, KT, D], F32)) for i in range(n_w)]
        s_w = [ctx.enter_context(nc.semaphore(f"s_w{i}")) for i in range(n_w)]
        s_id = ctx.enter_context(nc.semaphore("s_id"))
        s_wh = ctx.enter_context(nc.semaphore("s_wh"))
        block = ctx.enter_context(nc.Block())

        @block.sync
        def _(sp):
            for i in range(n_w):
                sp.dma_start(raw[i][:, :, :], w_dram[i]).then_inc(s_w[i], 16)

        @block.gpsimd
        def _(pool):
            pool.memset(ident[:, :], 0.0).then_inc(s_id, 1)
            pool.wait_ge(s_id, 1)
            pool.affine_select(out=ident[:, :], in_=ident[:, :], compare_op=ALU.not_equal, fill=1.0, base=0,
                               pattern=[[-1, P]], channel_multiplier=1).then_inc(s_id, 1)

        @block.scalar
        def _(act):
            for i in range(n_w):
                act.wait_ge(s_w[i], 16)
                act.activation(wh[i][:, :, :], raw[i][:, :, :], ACT.Copy).then_inc(s_wh, 1)

        @block.vector
        def _(dve):
            for i in range(n_w):
                dve.wait_ge(s_wh, i + 1)
                dve.tensor_tensor(wl[i][:, :, :], raw[i][:, :, :], wh[i][:, :, :].bitcast(F32), ALU.subtract)


def route(nc, tok_dram, idx_all, tile_expert, sorted_rows, N, E, VOCAB, D):
    NT = N // P
    NS = NT + E - 1
    per_expert = VOCAB // E
    with ExitStack() as ctx:
        def sb(name, shape, dt=F32):
            return ctx.enter_context(nc.sbuf_tensor(name, shape, dt))

        tok = sb("tok_sb", [P, NT], I32)
        tok_f = sb("tok_f", [P, NT])
        ge = sb("ge", [P, E + 1, NT])
        onehot = sb("onehot", [P, E, NT])
        onehot_bf = sb("onehot_bf", [P, E, NT], BF16)
        before = sb("before", [P, P], BF16)
        ones = sb("ones", [P, P], BF16)
        run = [sb(f"run{i}", [P, E, 2 * NT]) for i in range(2)]
        total = sb("total", [P, E, NT])
        rank = sb("rank", [P, E, NT])
        n_pad = sb("n_pad", [P, E], I32)
        n_tiles = sb("n_tiles", [P, E], I32)
        n_rows = sb("n_rows", [P, E], I32)
        rows_f = sb("rows_f", [P, E])
        base = sb("base", [P, E])
        at = sb("at", [P, E, NT])
        at2 = sb("at2", [P, E, NT])
        pos = sb("pos", [P, NT])
        tile_i = sb("tile_i", [P, NS], I32)
        tile_f = sb("tile_f", [P, NS])
        past = sb("past", [P, E - 1, NS])
        expert_f = sb("expert_f", [P, NS])
        zero = sb("zero", [P, D])
        inside = ctx.enter_context(nc.psum_tensor("inside", [P, E, NT], F32))
        tiles = ctx.enter_context(nc.psum_tensor("tiles", [P, E, NT], F32))
        s_tok = ctx.enter_context(nc.semaphore("s_tok"))
        s_c = ctx.enter_context(nc.semaphore("s_rc"))
        s_v = ctx.enter_context(nc.semaphore("s_rv"))
        s_m = ctx.enter_context(nc.semaphore("s_rm"))
        s_zero = ctx.enter_context(nc.semaphore("s_zero"))
        N_ONEHOT = 3 + 2 * E + 1
        block = ctx.enter_context(nc.Block())

        @block.sync
        def _(sp):
            sp.dma_start(tok[:, :], tok_dram).then_inc(s_tok, 16)
            sp.wait_ge(s_c, 1)
            with sp.Fori(0, NS) as t:
                sp.dma_start(sorted_rows.rearrange("(t p) d -> t p d", p=P)[t], zero[:, :]).then_inc(s_zero, 16)
            sp.wait_ge(s_zero, NS * 16)

        @block.gpsimd
        def _(pool):
            pool.memset(zero[:, :], 0.0).then_inc(s_c, 1)
            pool.memset(ones[:, :], 1.0).then_inc(s_c, 1)
            pool.memset(before[:, :], 1.0).then_inc(s_c, 1)
            pool.iota(tile_i[:, :], [[P, NS]], base=0, channel_multiplier=0).then_inc(s_c, 1)
            pool.wait_ge(s_c, 4)
            pool.affine_select(out=before[:, :], in_=before[:, :], compare_op=ALU.is_gt, fill=0.0, base=0,
                               pattern=[[1, P]], channel_multiplier=-1).then_inc(s_c, 1)

        @block.tensor
        def _(pe):
            pe.wait_ge(s_c, 5)
            pe.wait_ge(s_v, N_ONEHOT)
            flat = onehot_bf[:, :, :].rearrange("p e t -> p (e t)")
            pe.matmul(inside[:, :, :].rearrange("p e t -> p (e t)"), before[:, :], flat, start=True, stop=True)
            pe.matmul(tiles[:, :, :].rearrange("p e t -> p (e t)"), ones[:, :], flat, start=True,
                      stop=True).then_inc(s_m, 1)

        @block.vector
        def _(dve):
            count = [0]

            def step(ins):
                count[0] += 1
                ins.then_inc(s_v, 1)
                dve.wait_ge(s_v, count[0])

            dve.wait_ge(s_tok, 16)
            step(dve.tensor_copy(tok_f[:, :], tok[:, :]))
            step(dve.memset(ge[:, 0, :], 1.0))
            step(dve.memset(ge[:, E, :], 0.0))
            for e in range(1, E):
                step(dve.tensor_scalar(ge[:, e, :], tok_f[:, :], float(e * per_expert), None, ALU.is_ge))
            step(dve.tensor_tensor(onehot[:, :, :], ge[:, 0:E, :], ge[:, 1:E + 1, :], ALU.subtract))
            step(dve.tensor_copy(onehot_bf[:, :, :], onehot[:, :, :]))
            while count[0] < N_ONEHOT:
                step(dve.memset(run[count[0] % 2][:, :, :], 0.0))
            dve.wait_ge(s_m, 1)
            step(dve.tensor_copy(total[:, :, :], tiles[:, :, :]))
            step(dve.tensor_copy(run[0][:, :, NT:], total[:, :, :]))
            shift, i = 1, 0
            while shift < NT:
                step(dve.tensor_tensor(run[1 - i][:, :, NT:], run[i][:, :, NT:],
                                       run[i][:, :, NT - shift:2 * NT - shift], ALU.add))
                shift, i = 2 * shift, 1 - i
            step(dve.tensor_tensor(rank[:, :, :], run[i][:, :, NT:], total[:, :, :], ALU.subtract))
            step(dve.tensor_tensor(at[:, :, :], inside[:, :, :], rank[:, :, :], ALU.add))
            step(dve.tensor_scalar(n_pad[:, :], run[i][:, :, 2 * NT - 1], float(P - 1), None, ALU.add))
            step(dve.tensor_scalar(n_tiles[:, :], n_pad[:, :], P.bit_length() - 1, None, ALU.logical_shift_right))
            step(dve.tensor_scalar(n_rows[:, :], n_tiles[:, :], P.bit_length() - 1, None, ALU.logical_shift_left))
            step(dve.tensor_copy(rows_f[:, :], n_rows[:, :]))
            step(dve.memset(base[:, :], 0.0))
            for e in range(1, E):
                step(dve.tensor_tensor(base[:, e:e + 1], base[:, e - 1:e], rows_f[:, e - 1:e], ALU.add))
            step(dve.tensor_tensor(at2[:, :, :], at[:, :, :], base[:, :].unsqueeze(2).broadcast_to([P, E, NT]),
                                   ALU.add))
            step(dve.tensor_tensor(at[:, :, :], at2[:, :, :], onehot[:, :, :], ALU.mult))
            step(dve.tensor_reduce(pos[:, :], at[:, :, :].rearrange("p e t -> p t e"), AX.X, ALU.add))
            step(dve.tensor_copy(idx_all[:, :], pos[:, :]))
            step(dve.tensor_copy(tile_f[:, :], tile_i[:, :]))
            for e in range(1, E):
                step(dve.tensor_scalar(past[:, e - 1, :], tile_f[:, :], base[:, e:e + 1], None, ALU.is_ge))
            step(dve.tensor_reduce(expert_f[:, :], past[:, :, :].rearrange("p e t -> p t e"), AX.X, ALU.add))
            step(dve.tensor_copy(tile_expert[:, :], expert_f[:, :]))


def experts(nc, big, ident, tile_expert, ctx_t, sorted_rows, out_rows, N, E, D):
    KT = D // P
    NS = N // P + E - 1
    m_hl = [b[:, 0:E * KT * D].rearrange("p (e k n) -> p e k n", e=E, k=KT) for b in big]
    src = sorted_rows.rearrange("(t p) d -> t p d", p=P)
    dst = out_rows.rearrange("(t p) d -> t p d", p=P)
    with ExitStack() as ctx:
        def sb(name, shape, dt=F32):
            return ctx.enter_context(nc.sbuf_tensor(name, shape, dt))

        def sem(name):
            return ctx.enter_context(nc.semaphore(name))

        raw = [sb(f"m_raw{i}", [P, KT, D]) for i in range(2)]
        rows = [sb(f"rows{i}", [P, D]) for i in range(2)]
        xt = [[sb(f"xt_{h}{i}", [P, KT, P], F32R) for i in range(2)] for h in ("hi", "lo")]
        sg = [sb(f"sg{i}", [P, D]) for i in range(2)]
        gu = [sb(f"gu{i}", [P, D]) for i in range(2)]
        gt = [[sb(f"gt_{h}{i}", [P, KT, P], F32R) for i in range(2)] for h in ("hi", "lo")]
        y = [sb(f"y{i}", [P, D]) for i in range(2)]
        bank = [ctx.enter_context(nc.psum_tensor(f"e_bank{i}", [P, 512], F32)) for i in range(8)]
        XB, UB, GB, YB = bank[0:2], bank[2:4], bank[4:6], bank[6:8]
        s_raw = [sem(f"s_mraw{i}") for i in range(2)]
        s_mh, s_ml = sem("s_mh"), sem("s_ml")
        s_rows = [sem(f"s_rows{i}") for i in range(2)]
        s_xT, s_xh, s_xl = sem("s_xT"), sem("s_xTh"), sem("s_xTl")
        s_u, s_sg, s_gu = sem("s_u"), sem("s_sg"), sem("s_gu")
        s_gT, s_gh, s_gl = sem("s_gT"), sem("s_gTh"), sem("s_gTl")
        s_y = sem("s_y")
        s_ye = [sem(f"s_ye{i}") for i in range(2)]
        s_yd = [sem(f"s_yd{i}") for i in range(2)]
        block = ctx.enter_context(nc.Block())

        def tiles(eng, step):
            step(0, 0, 0)
            with eng.Fori(0, (NS - 3) // 2) as i:
                step(2 * i + 1, 1, 1)
                step(2 * i + 2, 0, 1)
            for n in range(NS - 2, NS):
                step(n, n % 2, 1 if n < NS - 1 else 2)

        assert NS % 2 == 1

        @block.sync
        def _(sp):
            for e in range(E):
                if e >= 2:
                    sp.wait_ge(s_ml, e - 1)
                sp.dma_start(raw[e % 2][:, :, :], ctx_t[e]).then_inc(s_raw[e % 2], 16)

            def load(n, i):
                sp.wait_ge(s_xT, n - 1)
                sp.dma_start(rows[i][:, :], src[n]).then_inc(s_rows[i], 16)

            def store(n, i):
                sp.wait_ge(s_ye[i], n - i + 2)
                sp.dma_start(dst[n], y[i][:, :]).then_inc(s_yd[i], 16)

            sp.dma_start(rows[0][:, :], src[0]).then_inc(s_rows[0], 16)
            sp.dma_start(rows[1][:, :], src[1]).then_inc(s_rows[1], 16)
            load(2, 0)
            with sp.Fori(0, (NS - 3) // 2) as i:
                load(2 * i + 3, 1)
                load(2 * i + 4, 0)
                store(2 * i, 0)
                store(2 * i + 1, 1)
            for n in range(NS - 3, NS):
                store(n, n % 2)
            sp.wait_ge(s_yd[0], (NS + 1) // 2 * 16)
            sp.wait_ge(s_yd[1], NS // 2 * 16)

        @block.tensor
        def _(pe):
            def x_transposes(n, i):
                pe.wait_ge(s_rows[i], (n - i) * 8 + 16)
                pe.wait_ge(s_xl, n - 1 if not isinstance(n, int) or n > 1 else 0)
                for k in range(KT):
                    ins = pe.transpose(XB[i][:, k * P:(k + 1) * P], rows[i][:, k * P:(k + 1) * P], ident[:, :])
                ins.then_inc(s_xT, 1)

            def gu_transposes(n, i):
                pe.wait_ge(s_gu, n + 1)
                if not isinstance(n, int) or n > 1:
                    pe.wait_ge(s_gl, n - 1)
                for k in range(KT):
                    ins = pe.transpose(GB[i][:, k * P:(k + 1) * P], gu[i][:, k * P:(k + 1) * P], ident[:, :])
                ins.then_inc(s_gT, 1)

            def expert_of(n):
                return pe.value_load(tile_expert[0:1, bass.ds(n, 1)], min_val=0, max_val=E - 1)

            def times_expert(e, out, a):
                return matmul3(pe, out[:, :], lambda k, i: a[i][:, k, :],
                               lambda k, j: m_hl[j][:, bass.ds(e, 1), k, :].rearrange("p a n -> p (a n)"), KT)

            def step(n, i, where):
                e = expert_of(n)
                e_last = expert_of(n - 1) if where > 0 else None
                pe.wait_ge(s_xl, n + 1)
                if not isinstance(n, int) or n > 1:
                    pe.wait_ge(s_gu, n - 1)
                times_expert(e, UB[i], [xt[h][i] for h in range(2)]).then_inc(s_u, 1)
                if where < 2:
                    x_transposes(n + 1, 1 - i)
                if where > 0:
                    last(e_last, n - 1, 1 - i)
                gu_transposes(n, i)

            def last(e, n, i):
                pe.wait_ge(s_gl, n + 1)
                pe.wait_ge(s_ye[i], n - i)
                times_expert(e, YB[i], [gt[h][i] for h in range(2)]).then_inc(s_y, 1)

            pe.wait_ge(s_ml, E)
            x_transposes(0, 0)
            tiles(pe, step)
            last(expert_of(NS - 1), NS - 1, 0)

        @block.scalar
        def _(act):
            for e in range(E):
                act.wait_ge(s_raw[e % 2], 16 * (e // 2 + 1))
                act.activation(m_hl[0][:, e, :, :], raw[e % 2][:, :, :], ACT.Copy).then_inc(s_mh, 1)

            def x_hi(n, i):
                act.wait_ge(s_xT, n + 1)
                if not isinstance(n, int) or n > 1:
                    act.wait_ge(s_u, n - 1)
                act.activation(xt[0][i][:, :, :].rearrange("p k t -> p (k t)"), XB[i][:, :],
                               ACT.Copy).then_inc(s_xh, 1)

            def step(n, i, where):
                act.wait_ge(s_u, n + 1)
                if not isinstance(n, int) or n > 1:
                    act.wait_ge(s_gu, n - 1)
                act.activation(sg[i][:, :], UB[i][:, :], ACT.Silu).then_inc(s_sg, 1)
                if where < 2:
                    x_hi(n + 1, 1 - i)
                if where > 0:
                    y_out(n - 1, 1 - i)
                act.wait_ge(s_gT, n + 1)
                if not isinstance(n, int) or n > 1:
                    act.wait_ge(s_y, n - 1)
                act.activation(gt[0][i][:, :, :].rearrange("p k t -> p (k t)"), GB[i][:, :],
                               ACT.Copy).then_inc(s_gh, 1)

            def y_out(n, i):
                act.wait_ge(s_y, n + 1)
                if not isinstance(n, int) or n > 1:
                    act.wait_ge(s_yd[i], (n - i) * 8)
                act.activation(y[i][:, :], YB[i][:, :], ACT.Copy).then_inc(s_ye[i], 2)

            x_hi(0, 0)
            tiles(act, step)
            y_out(NS - 1, 0)

        @block.vector
        def _(dve):
            for e in range(E):
                dve.wait_ge(s_mh, e + 1)
                dve.tensor_tensor(m_hl[1][:, e, :, :], raw[e % 2][:, :, :], m_hl[0][:, e, :, :].bitcast(F32),
                                  ALU.subtract).then_inc(s_ml, 1)

            def lo(dst_hl, banks, i, s_in, s_out, n):
                dve.wait_ge(s_in, n + 1)
                dve.tensor_tensor(dst_hl[1][i][:, :, :].rearrange("p k t -> p (k t)"), banks[i][:, :],
                                  dst_hl[0][i][:, :, :].rearrange("p k t -> p (k t)").bitcast(F32),
                                  ALU.subtract).then_inc(s_out, 1)

            def step(n, i, where):
                dve.wait_ge(s_sg, n + 1)
                if not isinstance(n, int) or n > 1:
                    dve.wait_ge(s_gT, n - 1)
                dve.tensor_tensor(gu[i][:, :], UB[i][:, :], sg[i][:, :], ALU.mult).then_inc(s_gu, 1)
                if where < 2:
                    lo(xt, XB, 1 - i, s_xh, s_xl, n + 1)
                lo(gt, GB, i, s_gh, s_gl, n)

            lo(xt, XB, 0, s_xh, s_xl, 0)
            tiles(dve, step)


def ffn(nc, big, x2, ident, idx_all, x1_rows, expert_rows, gate, up, down, out_rows, N, D, I):
    KT = D // P
    J = 4
    TW = 512
    RW = TW // P
    CH = J * P
    NCH = I // CH
    NR = N // TW
    GUP, DP, RING = 2 * J, J, 4
    PIECES = GUP + DP
    LINKS = 11
    xt = [b[:, 0:KT * N].rearrange("p (k n) -> p k n", k=KT) for b in big]
    with ExitStack() as ctx:
        def sb(name, shape, dt=F32):
            return ctx.enter_context(nc.sbuf_tensor(name, shape, dt))

        def sem(name):
            return ctx.enter_context(nc.semaphore(name))

        w_raw = [sb(f"fw_raw{i}", [P, D]) for i in range(RING)]
        wg = [sb(f"wg_{h}", [P, J, KT, P], F32R) for h in ("hi", "lo")]
        wu = [sb(f"wu_{h}", [P, J, KT, P], F32R) for h in ("hi", "lo")]
        wd = [sb(f"wd_{h}", [P, J, D], F32R) for h in ("hi", "lo")]
        sg = [sb(f"fsg{i}", [P, TW]) for i in range(2)]
        h = [sb(f"h{i}", [P, J, TW]) for i in range(2)]
        mag = sb("mag", [P, J, TW])
        beats = sb("beats", [P, 6, TW], BF16)
        wins = sb("wins", [P, J, TW], BF16)
        hs = [sb(f"hs_{x}", [P, J, TW], F32R) for x in ("hi", "lo")]
        gathered = [mag, hs[0], hs[1], wd[0]]
        ln = LayerNorm(nc, ctx, "ln3", D)
        ln2 = LayerNorm(nc, ctx, "ln2", D)
        bank = [ctx.enter_context(nc.psum_tensor(f"f_bank{i}", [P, 512], F32)) for i in range(8)]
        GB, UB, YB = bank[0:2], bank[2:4], bank[4:8]
        s_raw = [sem(f"s_fraw{i}") for i in range(RING)]
        s_ph, s_pl = sem("s_ph"), sem("s_pl")
        s_g, s_u, s_sg, s_h = sem("s_fg"), sem("s_fu"), sem("s_fsg"), sem("s_fh")
        s_mag, s_ch, s_hh, s_hl = sem("s_mag"), sem("s_ch"), sem("s_hh"), sem("s_hl")
        s_y, s_acc = sem("s_fy"), sem("s_facc")
        s_x3, s_out = sem("s_x3"), sem("s_fout")
        s_x1 = [sem(f"s_x1r{r}") for r in range(NR)]
        s_gat = [sem(f"s_gat{r}") for r in range(NR)]
        s_z2, s_x2 = sem("s_z2"), sem("s_x2")
        s_xT, s_xTh, s_xTl = sem("s_x2T"), sem("s_x2Th"), sem("s_x2Tl")
        block = ctx.enter_context(nc.Block())

        def chunks(eng, body):
            body(0, True, False)
            with eng.Fori(1, NCH - 1) as c:
                body(c, False, False)
            body(NCH - 1, False, True)

        normed_at = {v: RW + 2 * v for v in range(J + 2)}

        def before(c, v, k):
            r = v // J - k
            return (c, r) if r >= 0 else (c - 1, r + NR)

        def gate_up(i):
            return i % 2, i // 2

        @block.sync
        def _(sp):
            def load(n, i, src):
                if not isinstance(n, int) or n >= RING:
                    sp.wait_ge(s_pl, n - RING + 1)
                sp.dma_start(w_raw[i % RING][:, :], src).then_inc(s_raw[i % RING], 16)

            def load_gate_up(c, base):
                for i in range(GUP):
                    m, j = gate_up(i)
                    load(base + i, i, (gate, up)[m][c, j])

            def body(c, first, last):
                for j in range(J):
                    load(PIECES * c + GUP + j, j, down[c][:, j, :])
                if not last:
                    load_gate_up(c + 1, PIECES * (c + 1))

            sp.dma_start(x2[:, 0:RW, :], x1_rows[0]).then_inc(s_x1[0], 16)
            load_gate_up(0, 0)
            for r in range(1, NR):
                sp.dma_start(x2[:, r * RW:(r + 1) * RW, :], x1_rows[r]).then_inc(s_x1[r], 16)
            chunks(sp, body)
            for t in range(N // P):
                sp.wait_ge(s_x3, t + 1)
                sp.dma_start(out_rows[t], x2[:, t, :]).then_inc(s_out, 16)
            sp.wait_ge(s_out, N // P * 16)

        @block.gpsimd
        def _(pool):
            def gather(t):
                dst = gathered[t // RW][:, t % RW, :]
                pool.indirect_dma_start(dst if t < RW else dst.bitcast(F32), None, expert_rows,
                                        bass.IndirectOffsetOnAxis(idx_all[:, t:t + 1], 0)).then_inc(s_gat[t // RW], 16)
            ln2.start(pool)
            ln.start(pool)
            for t in range(N // P):
                gather(t)
                if t >= RW:
                    ln2.rstd(pool, t - RW, t % 4)
            for t in range(N // P - RW, N // P):
                ln2.rstd(pool, t, t % 4)
            for t in range(N // P):
                ln.rstd(pool, t, t % 4)

        @block.tensor
        def _(pe):
            def turn(t):
                pe.wait_ge(s_x2, t + 1)
                if t >= RW:
                    pe.wait_ge(s_xTl, t - RW + 1)
                for k in range(KT):
                    ins = pe.transpose(YB[t % RW][:, k * P:(k + 1) * P], x2[:, t, k * P:(k + 1) * P], ident[:, :])
                ins.then_inc(s_xT, 1)

            def inner(c, v):
                r, j = v // J, v % J
                if isinstance(c, int) and c == 0 and j == 0:
                    pe.wait_ge(s_xTl, (r + 1) * RW)
                n = c * NR * J + v
                for m, (w, banks, s_read, s_done) in enumerate(((wg, GB, s_sg, s_g), (wu, UB, s_h, s_u))):
                    if r == 0:
                        pe.wait_ge(s_pl, PIECES * c + 2 * j + m + 1)
                    if not isinstance(n, int) or n >= 2:
                        pe.wait_ge(s_read, n - 1)
                    matmul3(pe, banks[v % 2][:, :], lambda k, i: w[i][:, j, k, :],
                            lambda k, i: xt[i][:, k, r * TW:(r + 1) * TW], KT).then_inc(s_done, 1)

            def outer(c, r):
                n = c * NR + r
                pe.wait_ge(s_pl, PIECES * c + PIECES)
                pe.wait_ge(s_hl, n + 1)
                for t in range(RW):
                    if not isinstance(n, int) or n >= 1:
                        pe.wait_ge(s_acc, RW * (n - 1) + t + 1)
                    matmul3(pe, YB[t][:, :], lambda k, i: hs[i][:, k, t * P:(t + 1) * P],
                            lambda k, i: wd[i][:, k, :], J).then_inc(s_y, 1)

            def body(c, first, last):
                for v in range(NR * J):
                    inner(c, v)
                    if first:
                        if v - 1 in normed_at:
                            turn(normed_at[v - 1])
                            turn(normed_at[v - 1] + 1)
                    if v % J == J - 1 and (v > J or not first):
                        outer(*before(c, v, 1))

            for t in range(RW):
                turn(t)
            chunks(pe, body)
            outer(NCH - 1, NR - 1)

        @block.scalar
        def _(act):
            def piece(n, i, dst, s_free=None, free=0):
                act.wait_ge(s_raw[i % RING], (n - i % RING) * (16 // RING) + 16)
                if s_free is not None:
                    act.wait_ge(s_free, free)
                act.activation(dst, w_raw[i % RING][:, :], ACT.Copy).then_inc(s_ph, 1)

            def gate_up_piece(c, i, base, guarded):
                m, j = gate_up(i)
                dst = (wg, wu)[m][0][:, j, :, :].rearrange("p k n -> p (k n)")
                if guarded:
                    piece(base + i, i, dst, (s_g, s_u)[m], c * NR * J + (NR - 1) * J + j + 1)
                else:
                    piece(base + i, i, dst)

            def turned_hi(t):
                act.wait_ge(s_xT, t + 1)
                act.activation(xt[0][:, :, t * P:(t + 1) * P],
                               YB[t % RW][:, :].rearrange("p (k t) -> p k t", k=KT), ACT.Copy).then_inc(s_xTh, 1)

            def silu(c, v):
                n = c * NR * J + v
                act.wait_ge(s_g, n + 1)
                if not isinstance(n, int) or n >= 2:
                    act.wait_ge(s_h, n - 1)
                act.activation(sg[v % 2][:, :], GB[v % 2][:, :], ACT.Silu).then_inc(s_sg, 1)

            def magnitudes(c, r):
                n = c * NR + r
                act.wait_ge(s_h, J * (n + 1))
                if not isinstance(n, int) or n >= 1:
                    act.wait_ge(s_ch, LINKS * (n - 1) + 3)
                act.activation(mag[:, :, :], h[r % 2][:, :, :], ACT.Abs).then_inc(s_mag, 1)

            def kept_hi(c, r):
                n = c * NR + r
                act.wait_ge(s_ch, LINKS * (n + 1))
                act.wait_ge(s_y, RW * n)
                act.activation(hs[0][:, :, :], h[r % 2][:, :, :], ACT.Copy).then_inc(s_hh, 1)

            def body(c, first, last):
                for v in range(NR * J):
                    silu(c, v)
                    if first:
                        if v - 1 in normed_at:
                            turned_hi(normed_at[v - 1])
                            turned_hi(normed_at[v - 1] + 1)
                    if v == J + 2:
                        if first:
                            act.wait_ge(s_z2, N // P)
                        for j in range(J):
                            piece(PIECES * c + GUP + j, j, wd[0][:, j, :], s_y, RW * (c * NR))
                    if v % J == 1 and (v > J or not first):
                        kept_hi(*before(c, v, 1))
                    if v % J == J - 1:
                        magnitudes(c, v // J)
                    if v > (NR - 1) * J and not last:
                        j = v - (NR - 1) * J - 1
                        for i in (2 * j, 2 * j + 1):
                            gate_up_piece(c, i, PIECES * (c + 1), True)
                if not last:
                    for i in (2 * J - 2, 2 * J - 1):
                        gate_up_piece(c, i, PIECES * (c + 1), True)

            for i in range(GUP):
                gate_up_piece(0, i, 0, False)
                if i % 2 == 1:
                    turned_hi(i // 2)
            chunks(act, body)
            kept_hi(NCH - 1, NR - 1)

        @block.vector
        def _(dve):
            def piece(n, i, dst, hi):
                dve.wait_ge(s_ph, n + 1)
                dve.tensor_tensor(dst, w_raw[i % RING][:, :], hi.bitcast(F32), ALU.subtract).then_inc(s_pl, 1)

            def gate_up_piece(i, base):
                m, j = gate_up(i)
                w = (wg, wu)[m]
                piece(base + i, i, w[1][:, j, :, :].rearrange("p k n -> p (k n)"),
                      w[0][:, j, :, :].rearrange("p k n -> p (k n)"))

            def normed(t):
                r = t // RW
                for i in (t, t + 1):
                    dve.wait_ge(s_x1[r], 16)
                    dve.wait_ge(s_gat[r], RW * 16)
                    g = gathered[r][:, i % RW, :]
                    dve.tensor_tensor(x2[:, i, :], x2[:, i, :], g if r == 0 else g.bitcast(F32),
                                      ALU.add).then_inc(s_z2, 1)
                    ln2.statistics(dve, x2[:, i, :], s_z2, i + 1, i, i % 4)
                for i in (t, t + 1):
                    ln2.scale(dve, x2[:, i, :], x2[:, i, :], i, i % 4, s_x2)

            def turned_lo(t):
                for i in (t, t + 1):
                    dve.wait_ge(s_xTh, i + 1)
                    at = slice(i * P, (i + 1) * P)
                    dve.tensor_tensor(xt[1][:, :, at], YB[i % RW][:, :].rearrange("p (k t) -> p k t", k=KT),
                                      xt[0][:, :, at].bitcast(F32), ALU.subtract).then_inc(s_xTl, 1)

            def product(c, v):
                r, j = v // J, v % J
                n = c * NR * J + v
                dve.wait_ge(s_u, n + 1)
                dve.wait_ge(s_sg, n + 1)
                rr = c * NR + r
                if j == 0 and (not isinstance(rr, int) or rr >= 2):
                    dve.wait_ge(s_hh, rr - 1)
                dve.tensor_tensor(h[r % 2][:, j, :], UB[v % 2][:, :], sg[v % 2][:, :], ALU.mult).then_inc(s_h, 1)

            def pair(x, i, j):
                return x[:, i:j + 1:j - i, :]

            def compare(c, r):
                n = c * NR + r
                dve.wait_ge(s_mag, n + 1)
                for i, at in ((0, 0), (1, 3), (2, 5)):
                    w = J - 1 - i
                    dve.tensor_tensor(beats[:, at:at + w, :], mag[:, i:i + 1, :].broadcast_to([P, w, TW]),
                                      mag[:, i + 1:J, :], ALU.is_ge).then_inc(s_ch, 1)
                dve.wait_ge(s_ch, LINKS * n + 3)

            def choose(c, r):
                n = c * NR + r
                hr = h[r % 2]
                b01, b02, b03, b12, b13, b23 = range(6)
                dve.tensor_tensor(pair(wins, 0, 3), pair(beats, b01, b03), pair(beats, b02, b13),
                                  ALU.add).then_inc(s_ch, 1)
                dve.tensor_tensor(wins[:, 1, :], beats[:, b12, :], beats[:, b13, :], ALU.add).then_inc(s_ch, 1)
                dve.tensor_tensor(wins[:, 2, :], beats[:, b02, :], beats[:, b12, :], ALU.add).then_inc(s_ch, 1)
                dve.wait_ge(s_ch, LINKS * n + 6)
                dve.tensor_tensor(pair(wins, 0, 3), pair(wins, 0, 3), pair(beats, b03, b23),
                                  ALU.add).then_inc(s_ch, 1)
                dve.tensor_tensor(wins[:, 1, :], wins[:, 1, :], beats[:, b01, :], ALU.subtract)
                dve.tensor_tensor(wins[:, 2, :], wins[:, 2, :], beats[:, b23, :], ALU.subtract).then_inc(s_ch, 1)
                dve.wait_ge(s_ch, LINKS * n + 8)
                for j, (op, least) in enumerate(((ALU.is_ge, 1.5), (ALU.is_ge, 0.5), (ALU.is_le, 0.5),
                                                 (ALU.is_le, 1.5))):
                    ins = dve.scalar_tensor_tensor(out=hr[:, j, :], in0=wins[:, j, :], scalar=least,
                                                   in1=hr[:, j, :], op0=op, op1=ALU.mult)
                    if j > 0:
                        ins.then_inc(s_ch, 1)

            def kept_lo(c, r):
                n = c * NR + r
                dve.wait_ge(s_hh, n + 1)
                dve.wait_ge(s_y, RW * n)
                dve.tensor_tensor(hs[1][:, :, :], h[r % 2][:, :, :], hs[0][:, :, :].bitcast(F32),
                                  ALU.subtract).then_inc(s_hl, 1)

            def add_up(c, r, norm):
                n = c * NR + r
                for t in range(RW):
                    dve.wait_ge(s_y, RW * n + t + 1)
                    rows = x2[:, r * RW + t, :]
                    dve.tensor_tensor(rows, YB[t][:, :], rows, ALU.add).then_inc(s_acc, 1)
                    if norm:
                        ln.statistics(dve, rows, s_acc, RW * n + t + 1, r * RW + t, t)

            def norm_rows(r):
                for t in range(RW):
                    rows = x2[:, r * RW + t, :]
                    ln.scale(dve, rows, rows, r * RW + t, t, s_x3)

            def body(c, first, last):
                for v in range(NR * J):
                    product(c, v)
                    if first:
                        if v - 1 in normed_at:
                            turned_lo(normed_at[v - 1])
                        if v in normed_at:
                            normed(normed_at[v])
                    if v >= J or not first:
                        if v % J == 0:
                            compare(*before(c, v, 1))
                            choose(*before(c, v, 1))
                        if v % J == 1:
                            kept_lo(*before(c, v, 1))
                    if v % J == 2 and (v >= 2 * J or not first):
                        add_up(*before(c, v, 2), last and v >= 2 * J)
                    if v % J == 3 and v >= 2 * J and last:
                        norm_rows(v // J - 2)
                    if v == J + 2:
                        for j in range(J):
                            piece(PIECES * c + GUP + j, j, wd[1][:, j, :], wd[0][:, j, :])
                    if v > (NR - 1) * J and not last:
                        j = v - (NR - 1) * J - 1
                        for i in (2 * j, 2 * j + 1):
                            gate_up_piece(i, PIECES * (c + 1))
                if not last:
                    for i in (2 * J - 2, 2 * J - 1):
                        gate_up_piece(i, PIECES * (c + 1))

            for i in range(GUP):
                gate_up_piece(i, 0)
                if i % 4 == 1:
                    normed(i // 2)
                if i % 4 == 3:
                    turned_lo(i // 2 - 1)
            chunks(dve, body)
            last = (NCH - 1, NR - 1)
            compare(*last)
            choose(*last)
            kept_lo(*last)
            add_up(NCH - 1, NR - 2, True)
            norm_rows(NR - 2)
            add_up(*last, True)
            norm_rows(NR - 1)


def build(nc, x, x_t, tok, ctx_t, wq, wk, wv, wo, gate, up, down, out):
    B, T, D = x.shape
    N = B * T
    E = ctx_t.shape[0]
    I = down.shape[0]
    VOCAB = 25000
    KT = D // P
    NS = N // P + E - 1

    def scratch(name, shape):
        return nc.dram_tensor(name, shape, F32, kind="Internal").ap()

    qk_dram = [[scratch(f"{n}_{h}_dram", [P, T]) for h in ("hi", "lo")] for n in "qk"]
    x1_rows = scratch("x1_dram", [B, T, D])
    sorted_rows = scratch("sorted_dram", [NS * P, D])
    expert_rows = scratch("expert_dram", [NS * P, D])
    with ExitStack() as ctx:
        def sb(name, shape, dt):
            return ctx.enter_context(nc.sbuf_tensor(name, shape, dt))

        ident = sb("ident", [P, P], F32)
        idx_all = sb("idx_all", [P, N // P], I32)
        tile_expert = sb("tile_expert", [P, NS], I32)
        route(nc, tok, idx_all, tile_expert, sorted_rows, N, E, VOCAB, D)
        with ExitStack() as wctx:
            w_split = [[wctx.enter_context(nc.sbuf_tensor(f"w{n}_{h}", [P, KT, D], F32R)) for n in "qkvo"]
                       for h in ("hi", "lo")]
            setup(nc, [w.rearrange("(k p) n -> p k n", p=P) for w in (wq, wk, wv, wo)], w_split, ident, D)
            attention(nc, w_split, ident, idx_all, x_t.rearrange("b (k p) t -> b p k t", p=P),
                      x.rearrange("b (r p) d -> b p r d", p=P),
                      x1_rows.rearrange("b (r p) d -> b p r d", p=P), sorted_rows, qk_dram, B, T, D)
        big = [sb(f"big_{h}", [P, max(E * KT * D, KT * N)], F32R) for h in ("hi", "lo")]
        experts(nc, big, ident, tile_expert, ctx_t.rearrange("e (k p) n -> e p k n", p=P), sorted_rows,
                expert_rows, N, E, D)
        x2 = sb("x2", [P, N // P, D], F32)
        ffn(nc, big, x2, ident, idx_all, x1_rows.rearrange("b (r p) d -> b p r d", p=P), expert_rows, gate, up, down.rearrange("(c p j) n -> c p j n", p=P, j=4),
            out.rearrange("b (r p) d -> (b r) p d", p=P), N, D, I)


def kernel(x, itok_BxS_13_99985, ctx_2048, L0_attn_Wq, L0_attn_Wk, L0_attn_Wv, L0_attn_Wo, L0_ffn_w_gate,
           L0_ffn_w_up, L0_ffn_w_down):
    import numpy as np
    from concourse import bacc
    from concourse.bass_utils import run_bass_kernel_spmd

    def by_group(w):
        d, i = w.shape
        w = w.reshape(d // P, P, i // 512, P, 4)
        return np.ascontiguousarray(w.transpose(2, 4, 1, 0, 3)).reshape(i // 512, 4, P, d)

    x = np.asarray(x)
    arrays = {
        "x": x,
        "x_t": np.ascontiguousarray(x.transpose(0, 2, 1)),
        "tok": np.ascontiguousarray(np.asarray(itok_BxS_13_99985).reshape(-1, P).T),
        "ctx_t": np.ascontiguousarray(np.asarray(ctx_2048).transpose(0, 2, 1)),
        "wq": np.asarray(L0_attn_Wq),
        "wk": np.asarray(L0_attn_Wk),
        "wv": np.asarray(L0_attn_Wv),
        "wo": np.asarray(L0_attn_Wo),
        "gate": by_group(np.asarray(L0_ffn_w_gate)),
        "up": by_group(np.asarray(L0_ffn_w_up)),
        "down": np.asarray(L0_ffn_w_down),
    }
    nc = bacc.Bacc("TRN2", target_bir_lowering=False, num_devices=1)
    aps = [nc.dram_tensor(n, a.shape, mybir.dt.from_np(a.dtype), kind="ExternalInput").ap()
           for n, a in arrays.items()]
    out = nc.dram_tensor("out", x.shape, F32, kind="ExternalOutput").ap()
    build(nc, *aps, out)
    got = run_bass_kernel_spmd(nc, [arrays], core_ids=[0])
    return got.results[0]["out"]
```

```python
from contextlib import ExitStack

import concourse.bass as bass
from concourse import mybir

F32 = mybir.dt.float32
F32R = mybir.dt.float32r
BF16 = mybir.dt.bfloat16
F16 = mybir.dt.float16
I32 = mybir.dt.int32
ALU = mybir.AluOpType
ACT = mybir.ActivationFunctionType
AX = mybir.AxisListType

P = 128
HEADS = 16
EPS = 1e-5
NEG = -3.0e38


def wait_apart(eng, passed, waits):
    for sem, value in waits:
        eng.wait_ge(sem, value)
    eng.sem_inc(passed, 1)


def matmul3(pe, out, a, b, steps, first=0, last=None):
    chain = [(k, i, j) for k in range(steps) for i, j in ((0, 0), (0, 1), (1, 0))]
    last = len(chain) if last is None else last
    for n in range(first, last):
        k, i, j = chain[n]
        ins = pe.matmul(out, a(k, i), b(k, j), start=(n == 0), stop=(n == len(chain) - 1))
    return ins


def attention(nc, w_split, stacks, ident, idx_all, x_t, x_raw, s_xraw, x_rows, x1_rows,
              sorted_rows, route, context, scratch, B, T, D):
    KT = D // P
    NB = T // P
    HD = D // HEADS
    SLOTS = P // HD
    HPT = P // HD
    NM = D // P
    UPM = HPT * NB
    UPB = NM * UPM
    AHEAD_S, AHEAD_MAX, AHEAD_HI, AHEAD_LO, AHEAD_V = 3, 2, -1, -1, -2
    RP = 4
    scale = 1.0 / float(T) ** 0.5

    wh, wl = w_split
    with ExitStack() as ctx:
        def sb(name, shape, dt):
            return ctx.enter_context(nc.sbuf_tensor(name, shape, dt))

        def sem(name):
            return ctx.enter_context(nc.semaphore(name))

        x_turned = x_raw[:, :].rearrange("p (k t) -> p k t", k=KT)
        x_res = x_raw[:, :].rearrange("p (r d) -> p r d", r=NB)
        x_hl = [sb("x_hi", [P, KT, T], F32R), sb("x_lo", [P, KT, T], F32R)]
        qk_hl = [[sb(f"{n}_{h}", [P, T], F32R) for h in ("hi", "lo")] for n in "qk"]
        stack_all = stacks[:, 0:4 * HPT * T].rearrange("p (s i h t) -> p s i h t", s=2, i=2, h=HPT)
        stack = [[stack_all[:, side, i] for i in range(2)] for side in range(2)]
        v3 = sb("v3", [P, NB, 3, D], BF16)
        v_rest = [sb(f"v_rest{i}", [P, D], F32) for i in range(2)]
        v_tail = sb("v_tail", [P, NB - 1, D], F32)
        probs = [sb(f"probs{i}", [P, T], F32) for i in range(RP)]
        pt_hi = [sb(f"pt_hi{i}", [P, T], F16) for i in range(RP)]
        pt_lo = [sb(f"pt_lo{i}", [P, T], F16) for i in range(RP)]
        o_raw = sb("o_raw", [P, NB, HEADS, HD], F32)
        o_tmp = [sb(f"o_tmp{i}", [P, NB - 1, HPT, HD], F32) for i in range(2)]
        ot_hl = [[sb(f"ot_{h}{i}", [P, KT, P], F32R) for i in range(2)] for h in ("hi", "lo")]
        zero = sb("zero", [P, D], F32)
        mask = sb("mask", [P, T], F32)
        minus_one = sb("minus_one", [P, 1], F32)
        ones_bf = sb("ones_bf", [P, P], BF16)
        smax = sb("smax", [P, NB, HEADS], F32)
        nmax = sb("nmax", [P, NB, HEADS], F32)
        rsum = sb("rsum", [P, NB, HEADS], F32)
        c_up = sb("c_up", [P, NB, HEADS], F32)
        n_up = sb("n_up", [P, NB, HEADS], F32)
        den = sb("den", [P, NB, HEADS], F32)
        den2 = sb("den2", [P, NB, HEADS], F32)
        rinv = sb("rinv", [P, NB, HEADS], F32)
        z = [sb(f"z{i}", [P, D], F32) for i in range(2)]
        x1 = [sb(f"x1_{i}", [P, D], F32) for i in range(2)]
        idx = sb("idx", [P, NB], I32)
        s_sc = [sem(f"s_sc{i}") for i in range(2)]
        s_idx, s_scattered = sem("s_idx"), sem("s_scattered")
        ln = LayerNorm(nc, ctx, "ln1", D)
        bank = [ctx.enter_context(nc.psum_tensor(f"bank{i}", [P, 512], F32)) for i in range(8)]
        S, TP, OB, PJ = bank[0:3], bank[3:5], bank[5:7], bank[7]
        VB, SF, OT, WB = bank[0:4], (bank[3], bank[5], bank[6]), bank[5:7], (bank[4], bank[7])
        SR, TR, OR = len(S), len(TP), len(OB)

        s_const = sem("s_const")
        s_passed, s_passed_sp = sem("s_passed"), sem("s_passed_sp")
        s_zero = sem("s_zero")
        s_xh = sem("s_xh")
        s_xl = sem("s_xl")
        s_xres = sem("s_xres")
        s_vp = sem("s_vp")
        s_v0 = sem("s_v0")
        s_vr = sem("s_vr")
        s_v1 = sem("s_v1")
        s_v2 = sem("s_v2")
        s_sf = sem("s_sf")
        s_sfe = sem("s_sfe")
        s_pj = sem("s_pj")
        s_pjh = sem("s_pjh")
        s_pjl = sem("s_pjl")
        s_dw = sem("s_dw")
        s_st = [sem("s_stq"), sem("s_stk")]
        s_S = sem("s_S")
        s_mx = sem("s_mx")
        s_nm = sem("s_nm")
        s_e = sem("s_e")
        s_T = sem("s_T")
        s_hi = sem("s_hi")
        s_lo = sem("s_lo")
        s_pv = sem("s_pv")
        s_oe = sem("s_oe")
        s_c = sem("s_c")
        s_t = [sem("s_t_pool"), sem("s_t_dve")]
        s_on = [sem("s_on_pool"), sem("s_on_dve")]
        s_ot = sem("s_ot")
        s_oth = sem("s_oth")
        s_otl = sem("s_otl")
        s_wo = sem("s_wo")
        s_z = sem("s_z")
        s_x1 = sem("s_x1")
        s_x1d = [sem(f"s_x1d{i}") for i in range(2)]

        row_blocks = (2, 3, 1, 0)
        units = [(u // UPM, (u // NB) % HPT, row_blocks[u % NB]) for u in range(UPB)]

        starts = {4: (2, 2), 5: (9, 2), 6: (17, 2), 7: (24, 2),
                  8: (38, 2), 9: (45, 2), 10: (52, 2), 11: (59, 3)}
        pieces = {}
        for g, (first, n) in starts.items():
            for i in range(0, 3 * KT, n):
                pieces[first + i // n] = (g, i, i + n)
        split_at = {first + 3 * KT // n: g for g, (first, n) in starts.items()}
        x_split_at = {31 + 2 * k: k for k in range(KT)}
        G_AHEAD = 4
        between = [("v", 0), ("turn", 0), ("turn", 1), ("v", 2), ("out", 0), ("turn", 2), ("out", 1),
                   ("turn", 3), ("out", 2), ("out", 3), ("sums", 0)]

        def cols(r):
            return (r + 1) * P

        def norm_heads(eng, side, b, m):
            per_batch = (NM - 1, 1)[side]
            n = (b * per_batch + (m if side == 0 else 0)) * 5
            hs = slice(m * HPT, (m + 1) * HPT)
            count = [0]

            def link(ins):
                count[0] += 1
                ins.then_inc(s_t[side], 1)
                eng.wait_ge(s_t[side], n + count[0])

            eng.wait_ge(s_e, b * UPB + (m + 1) * UPM)
            eng.wait_ge(s_c, b * NM + m + 1)
            eng.wait_ge(s_oe, b * NM + m + 1)
            link(eng.tensor_tensor(den[:, :, hs], c_up[:, :, hs], n_up[:, :, hs], ALU.mult))
            link(eng.tensor_tensor(den2[:, :, hs], den[:, :, hs], rsum[:, :, hs], ALU.add))
            if side == 0:
                link(eng.tensor_tensor(rinv[:, :, hs], den2[:, :, hs],
                                       minus_one[:, :].unsqueeze(2).broadcast_to([P, NB, HPT]), ALU.pow))
            else:
                link(eng.reciprocal(rinv[:, :, hs], den2[:, :, hs]))
            link(eng.tensor_tensor(o_tmp[side][:, :, :, :],
                                   v_tail[:, :, m * P:(m + 1) * P].rearrange("p r (h d) -> p r h d", h=HPT),
                                   c_up[:, 0:NB - 1, hs].unsqueeze(3).broadcast_to([P, NB - 1, HPT, HD]), ALU.mult))
            link(eng.tensor_tensor(o_raw[:, 0:NB - 1, hs, :], o_raw[:, 0:NB - 1, hs, :], o_tmp[side][:, :, :, :],
                                   ALU.add))
            ins = eng.tensor_tensor(o_raw[:, :, hs, :], o_raw[:, :, hs, :],
                                    rinv[:, :, hs].unsqueeze(3).broadcast_to([P, NB, HPT, HD]), ALU.mult)
            ins.then_inc(s_on[side], 1)

        counts = [OT[i][:, 0:route.E * route.NT] for i in range(2)]
        PRIMED = 1

        block = ctx.enter_context(nc.Block())

        @block.gpsimd
        def _(pool):
            pool.sem_inc(s_scattered, PRIMED)
            pool.memset(zero[:, :], 0.0).then_inc(s_const, 1)
            pool.memset(mask[:, :], 1.0).then_inc(s_const, 1)
            ln.start(pool)
            route.start(pool)
            pool.memset(ones_bf[:, :], 1.0).then_inc(s_const, 1)
            pool.memset(minus_one[:, :], -1.0).then_inc(s_const, 1)
            for r in range(NB):
                pool.memset(n_up[:, r, :], float((NB - 1 - r) * P)).then_inc(s_const, 1)
            pool.wait_ge(s_const, 4 + NB)
            pool.affine_select(out=mask[:, T - P:T], in_=mask[:, T - P:T], compare_op=ALU.is_ge, fill=0.0,
                               base=0, pattern=[[-1, P]], channel_multiplier=1).then_inc(s_const, 1)
            pool.wait_ge(s_zero, 16)
            pool.wait_ge(route.s_idx_all, 1)
            with pool.Fori(0, B) as b:
                pool.tensor_copy(idx[:, :], idx_all[:, bass.ds(b * NB, NB)]).then_inc(s_idx, 1)
                for m in range(NM - 1):
                    norm_heads(pool, 0, b, m)
                for n in range(NB + 1):
                    if n < NB:
                        ln.rstd(pool, b * NB + n, n)
                    if n > 0:
                        r = n - 1
                        wait_apart(pool, ln.s_passed[1],
                                   [(s_x1, PRIMED + b * NB + r + 1)] + [(s_idx, b + 1)] * (r == 0))
                        pool.indirect_dma_start(sorted_rows, bass.IndirectOffsetOnAxis(idx[:, r:r + 1], 0),
                                                x1[r % 2][:, :], None).then_inc(s_sc[r % 2], 16)
                wait_apart(pool, s_scattered, [(s_sc[i], (b + 1) * (NB // 2) * 16) for i in range(2)])

        NCONST = 5 + NB

        @block.sync
        def _(sp):
            def stack_up(b, g):
                m, side = g // 2, g % 2
                hd = scratch[side]
                sp.wait_ge(s_pjh, b * 2 * NM + g + 1)
                sp.dma_start(hd[0], qk_hl[side][0][:, :].bitcast(F32)).then_inc(s_dw, 16)
                sp.wait_ge(s_pjl, b * 2 * NM + g + 1)
                sp.dma_start(hd[1], qk_hl[side][1][:, :].bitcast(F32)).then_inc(s_dw, 16)
                wait_apart(sp, s_passed_sp, [(s_dw, (b * 2 * NM + g + 1) * 32)])
                sp.wait_ge(s_S, b * UPB + max(m - 1, 0) * UPM)
                order = (0, 1, 0, 1) if side == 0 else (0, 0, 1, 1)
                for slot, half in enumerate(order):
                    sp.dma_start(stack[side][m % 2][slot * HD:(slot + 1) * HD, :, :].bitcast(F32),
                                 hd[half].rearrange("(h r) t -> r h t", r=HD)).then_inc(s_st[side], 16)

            def batch(b, more):
                if more:
                    wait_apart(sp, s_passed_sp, [(s_xl, (b + 1) * KT)])
                    sp.wait_ge(s_z, PRIMED + b * NB)
                    sp.dma_start(x_turned, x_t[b + 1]).then_inc(s_xraw, 16)
                for g in range(G_AHEAD, 2 * NM):
                    stack_up(b, g)
                sp.wait_ge(s_xl, (b + 1 + more) * KT)
                if not more:
                    sp.wait_ge(s_z, PRIMED + b * NB)
                sp.dma_start(x_res, x_rows[b]).then_inc(s_xres, 16)
                if not more:
                    sp.wait_ge(s_pj, B * 2 * NM)
                    for e in range(len(context.raw)):
                        context.load(sp, e)
                if more:
                    for g in range(2 * NM, 2 * NM + G_AHEAD):
                        stack_up(b, g)
                for r in range(NB):
                    sp.wait_ge(s_x1, PRIMED + b * NB + r + 1)
                    sp.dma_start(x1_rows[b][:, r, :], x1[r % 2][:, :]).then_inc(s_x1d[r % 2], 16)

            for i in range(2):
                sp.sem_inc(s_x1d[i], PRIMED)
            route.load(sp)
            for g in range(G_AHEAD):
                stack_up(0, g)
            sp.wait_ge(s_const, NCONST)
            tiles = sorted_rows.rearrange("(t p) d -> p t d", p=P)
            zeros = zero[:, :].unsqueeze(1).broadcast_to([P, sorted_rows.shape[0] // P, D])
            sp.dma_start(tiles, zeros).then_inc(s_zero, 16)
            with sp.Fori(0, B - 1) as b:
                batch(b, True)
            batch(B - 1, False)
            for i in range(2):
                sp.wait_ge(s_x1d[i], PRIMED + B * NB // 2 * 16)

        @block.tensor
        def _(pe):
            def project(b, g, first, last):
                m, side = g // 2 % NM, g % 2
                if first == 0:
                    pe.wait_ge(s_xl, (b + 1 + g // (2 * NM)) * KT)
                    pe.wait_ge(s_pjl, b * 2 * NM + g)
                ins = matmul3(pe, PJ[:, :], lambda k, i: (wh, wl)[i][side][:, k, m * P:(m + 1) * P],
                              lambda k, j: x_hl[j][:, k, :], KT, first, last)
                if last == 3 * KT:
                    ins.then_inc(s_pj, 1)

            def scores(b, u):
                m, h, r = units[u]
                if u % UPM == 0:
                    for side in range(2):
                        pe.wait_ge(s_st[side], (b * NM + m + 1) * 16 * SLOTS)
                if u >= SR:
                    pe.wait_ge(s_e, b * UPB + u - SR + 1)
                pe.matmul(S[u % SR][:, 0:cols(r)], stack[0][m % 2][:, h, r * P:(r + 1) * P],
                          stack[1][m % 2][:, h, 0:cols(r)], start=True, stop=True).then_inc(s_S, 1)

            def transposes(b, u):
                _, _, r = units[u]
                pe.wait_ge(s_e, b * UPB + u + 1)
                if u >= TR:
                    pe.wait_ge(s_lo, b * UPB + u - TR + 1)
                for j in range(r + 1):
                    ins = pe.transpose(TP[u % TR][:, j * P:(j + 1) * P], probs[u % RP][:, j * P:(j + 1) * P],
                                       ident[:, :])
                ins.then_inc(s_T, 1)

            def values(b, u):
                m, h, r = units[u]
                if u % UPM == 0 and m >= OR:
                    pe.wait_ge(s_oe, b * NM + m - OR + 1)
                pe.wait_ge(s_lo, b * UPB + u + 1)
                out = OB[m % OR][:, (h * NB + r) * HD:(h * NB + r + 1) * HD]
                c = (m * HPT + h) * HD
                chain = [(j, half, part) for j in range(r + 1)
                         for half, part in ((0, 0), (0, 1), (0, 2), (1, 0), (1, 1))]
                for n, (j, half, part) in enumerate(chain):
                    p = (pt_hi, pt_lo)[half][u % RP][:, j * P:(j + 1) * P]
                    ins = pe.matmul(out, p, v3[:, j, part, c:c + HD], start=(n == 0), stop=(n == len(chain) - 1))
                ins.then_inc(s_pv, 1)

            def v_product(j):
                matmul3(pe, VB[j][:, :], lambda k, i: x_hl[i][:, k, j * P:(j + 1) * P],
                        lambda k, i: (wh, wl)[i][2][:, k, :], KT).then_inc(s_vp, 1)

            def v_sums(b):
                pe.wait_ge(s_v2, (b + 1) * NB)
                for n in range(NB - 1):
                    for part in range(3):
                        ins = pe.matmul(SF[n][:, :], ones_bf[:, :], v3[:, NB - 1 - n, part, :],
                                        start=(part == 0), stop=(part == 2))
                    ins.then_inc(s_sf, 1)

            def turn_heads(b, r):
                if r == 0:
                    pe.wait_ge(s_on[0], (b + 1) * (NM - 1))
                    pe.wait_ge(s_on[1], b + 1)
                if r >= 2:
                    pe.wait_ge(s_otl, b * NB + r - 1)
                for k in range(KT):
                    ins = pe.transpose(OT[r % 2][:, k * P:(k + 1) * P],
                                       o_raw[:, r, k * HPT:(k + 1) * HPT, :].rearrange("p h d -> p (h d)"),
                                       ident[:, :])
                ins.then_inc(s_ot, 1)

            def out_product(b, r):
                pe.wait_ge(s_otl, b * NB + r + 1)
                if r >= 2:
                    pe.wait_ge(s_z, PRIMED + b * NB + r - 1)
                matmul3(pe, WB[r % 2][:, :], lambda k, i: ot_hl[i][r % 2][:, k, :],
                        lambda k, i: (wh, wl)[i][3][:, k, :], KT).then_inc(s_wo, 1)

            def batch(b, more):
                for u in range(-AHEAD_S, UPB - AHEAD_V):
                    if u == 0:
                        pe.wait_ge(s_sfe, (b + 1) * (NB - 1))
                        pe.wait_ge(s_z, PRIMED + b * NB)
                    if 0 <= u < UPB:
                        transposes(b, u)
                    if u + AHEAD_S < UPB:
                        scores(b, u + AHEAD_S)
                    if u in pieces and (more or pieces[u][0] < 2 * NM):
                        project(b, *pieces[u])
                    if u + AHEAD_V >= 0:
                        values(b, u + AHEAD_V)
                for step, r in between:
                    if step == "v" and more:
                        v_product(r)
                        v_product(r + 1)
                    elif step == "turn":
                        turn_heads(b, r)
                    elif step == "out":
                        out_product(b, r)
                    elif step == "sums" and more:
                        v_sums(b + 1)

            for g in range(G_AHEAD):
                project(0, g, 0, 3 * KT)
                v_product(g)
                if g == 1:
                    pe.wait_ge(s_const, NCONST)
                    route.count(pe, ones_bf[:, :], counts[0], counts[1])
            v_sums(0)
            with pe.Fori(0, B - 1) as b:
                batch(b, True)
            batch(B - 1, False)

        @block.scalar
        def _(act):
            def split_proj(b, g):
                side = g % 2
                act.wait_ge(s_pj, b * 2 * NM + g + 1)
                act.wait_ge(s_dw, b * 2 * NM * 32 + max(g - 1, 0) * 32)
                act.activation(qk_hl[side][0][:, :], PJ[:, :], ACT.Copy,
                               scale=(scale if side == 0 else 1.0)).then_inc(s_pjh, 1)

            def exps(b, u):
                m, h, r = units[u]
                c = m * HPT + h
                act.wait_ge(s_nm, b * UPB + u + 1)
                if u >= RP:
                    act.wait_ge(s_T, b * UPB + u - RP + 1)
                act.activation(probs[u % RP][:, 0:cols(r)], S[u % SR][:, 0:cols(r)], ACT.Exp,
                               bias=nmax[:, r, c:c + 1], accum_out=rsum[:, r, c:c + 1]).then_inc(s_e, 1)

            def hi(b, u):
                _, _, r = units[u]
                act.wait_ge(s_T, b * UPB + u + 1)
                if u >= RP:
                    act.wait_ge(s_pv, b * UPB + u - RP + 1)
                act.activation(pt_hi[u % RP][:, 0:cols(r)], TP[u % TR][:, 0:cols(r)], ACT.Copy).then_inc(s_hi, 1)

            def x_split(b, k):
                act.wait_ge(s_xraw, (b + 1) * 16)
                act.activation(x_hl[0][:, k, :], x_turned[:, k, :], ACT.Copy).then_inc(s_xh, 1)

            def v_split(b, blocks):
                for j in blocks:
                    act.wait_ge(s_vp, b * NB + j + 1)
                    act.activation(v3[:, j, 0, :], VB[j][:, :], ACT.Copy).then_inc(s_v0, 1)
                for j in blocks:
                    act.wait_ge(s_vr, b * NB + j + 1)
                    act.activation(v3[:, j, 1, :], v_rest[j % 2][:, :], ACT.Copy).then_inc(s_v1, 1)

            def copy_out(b, m):
                act.wait_ge(s_pv, b * UPB + (m + 1) * UPM)
                act.activation(o_raw[:, :, m * HPT:(m + 1) * HPT, :].rearrange("p r h d -> p h r d"),
                                OB[m % OR][:, :].rearrange("p (h r d) -> p h r d", h=HPT, r=NB),
                               ACT.Copy).then_inc(s_oe, 1)

            def turned_hi(b, r):
                act.wait_ge(s_ot, b * NB + r + 1)
                if r >= 2:
                    act.wait_ge(s_wo, b * NB + r - 1)
                act.activation(ot_hl[0][r % 2][:, :, :].rearrange("p k t -> p (k t)"), OT[r % 2][:, :],
                               ACT.Copy).then_inc(s_oth, 1)

            def above(b, m):
                act.wait_ge(s_nm, b * UPB + (m + 1) * UPM)
                act.activation(c_up[:, :, m * HPT:(m + 1) * HPT], nmax[:, :, m * HPT:(m + 1) * HPT],
                               ACT.Exp).then_inc(s_c, 1)

            def batch(b, more):
                for u in range(UPB - AHEAD_HI):
                    if u < UPB:
                        exps(b, u)
                    if u + AHEAD_HI >= 0:
                        hi(b, u + AHEAD_HI)
                    if u in split_at and (more or split_at[u] < 2 * NM):
                        split_proj(b, split_at[u])
                    if more and u in x_split_at:
                        if x_split_at[u] == 0:
                            act.wait_ge(s_pj, (b + 1) * 2 * NM)
                        x_split(b + 1, x_split_at[u])
                    if u % UPM == 1 and UPM < u < UPB:
                        above(b, u // UPM - 1)
                    if u % UPM == 4 and UPM <= u < UPB:
                        copy_out(b, u // UPM - 1)
                above(b, NM - 1)
                copy_out(b, NM - 1)
                act.wait_ge(s_pv, (b + 1) * UPB)
                for step, r in between:
                    if step == "v" and more:
                        v_split(b + 1, (r, r + 1))
                    elif step == "turn":
                        turned_hi(b, r)
                if not more:
                    act.wait_ge(s_S, B * UPB)
                    for e in range(len(context.raw)):
                        context.cut_hi(act, e)

            for k in range(KT):
                x_split(0, k)
            for g in range(G_AHEAD):
                split_proj(0, g)
                v_split(0, (g,))
            with act.Fori(0, B - 1) as b:
                batch(b, True)
            batch(B - 1, False)

        @block.vector
        def _(dve):
            dve.sem_inc(s_z, PRIMED)
            dve.sem_inc(s_x1, PRIMED)

            def split_proj(b, g):
                side = g % 2
                dve.wait_ge(s_pjh, b * 2 * NM + g + 1)
                dve.scalar_tensor_tensor(out=qk_hl[side][1][:, :], in0=PJ[:, :],
                                         scalar=(scale if side == 0 else 1.0),
                                         in1=qk_hl[side][0][:, :].bitcast(F32), op0=ALU.mult,
                                         op1=ALU.subtract).then_inc(s_pjl, 1)

            def maxima(b, u):
                m, h, r = units[u]
                c = m * HPT + h
                wait_apart(dve, s_passed, [(s_S, b * UPB + u + 1)])
                dve.tensor_tensor_reduce(out=S[u % SR][:, 0:cols(r)], in0=S[u % SR][:, 0:cols(r)],
                                         in1=mask[:, T - cols(r):T], scale=1.0, scalar=NEG, op0=ALU.mult,
                                         op1=ALU.max, accum_out=smax[:, r, c:c + 1]).then_inc(s_mx, 1)

            def negated(b, u):
                m, h, r = units[u]
                c = m * HPT + h
                dve.wait_ge(s_mx, b * UPB + u + 1)
                if r < NB - 1:
                    dve.tensor_scalar(nmax[:, r, c:c + 1], smax[:, r, c:c + 1], 0.0, -1.0, ALU.max,
                                      ALU.mult).then_inc(s_nm, 1)
                else:
                    dve.tensor_scalar(nmax[:, r, c:c + 1], smax[:, r, c:c + 1], -1.0, None,
                                      ALU.mult).then_inc(s_nm, 1)

            def lo(b, u):
                _, _, r = units[u]
                dve.wait_ge(s_hi, b * UPB + u + 1)
                dve.tensor_tensor(pt_lo[u % RP][:, 0:cols(r)], TP[u % TR][:, 0:cols(r)],
                                  pt_hi[u % RP][:, 0:cols(r)], ALU.subtract).then_inc(s_lo, 1)

            def x_split(b, k):
                dve.wait_ge(s_xh, b * KT + k + 1)
                dve.tensor_tensor(x_hl[1][:, k, :], x_turned[:, k, :], x_hl[0][:, k, :].bitcast(F32),
                                  ALU.subtract).then_inc(s_xl, 1)

            def v_split(b, blocks):
                for j in blocks:
                    dve.wait_ge(s_v0, b * NB + j + 1)
                    dve.wait_ge(s_v2, b * NB + max(j - 1, 0))
                    dve.tensor_tensor(v_rest[j % 2][:, :], VB[j][:, :], v3[:, j, 0, :],
                                      ALU.subtract).then_inc(s_vr, 1)
                for j in blocks:
                    dve.wait_ge(s_v1, b * NB + j + 1)
                    dve.tensor_tensor(v3[:, j, 2, :], v_rest[j % 2][:, :], v3[:, j, 1, :],
                                      ALU.subtract).then_inc(s_v2, 1)

            def v_above(b):
                for n in range(NB - 1):
                    r = NB - 2 - n
                    dve.wait_ge(s_sf, b * (NB - 1) + n + 1)
                    if n == 0:
                        dve.tensor_copy(v_tail[:, r, :], SF[n][:, :]).then_inc(s_sfe, 1)
                    else:
                        dve.wait_ge(s_sfe, b * (NB - 1) + n)
                        dve.tensor_tensor(v_tail[:, r, :], SF[n][:, :], v_tail[:, r + 1, :],
                                          ALU.add).then_inc(s_sfe, 1)

            def turned_lo(b, r):
                dve.wait_ge(s_oth, b * NB + r + 1)
                if r >= 2:
                    dve.wait_ge(s_wo, b * NB + r - 1)
                dve.tensor_tensor(ot_hl[1][r % 2][:, :, :].rearrange("p k t -> p (k t)"), OT[r % 2][:, :],
                                  ot_hl[0][r % 2][:, :, :].rearrange("p k t -> p (k t)").bitcast(F32),
                                  ALU.subtract).then_inc(s_otl, 1)

            def add_x(b, r):
                dve.wait_ge(s_wo, b * NB + r + 1)
                dve.wait_ge(s_xres, (b + 1) * 16)
                dve.wait_ge(s_x1, PRIMED + b * NB + max(r - 1, 0))
                dve.tensor_tensor(z[r % 2][:, :], WB[r % 2][:, :], x_res[:, r, :], ALU.add).then_inc(s_z, 1)
                ln.statistics(dve, z[r % 2], s_z, PRIMED + b * NB + r + 1, b * NB + r, r)

            def norm_rows(b, r):
                dve.wait_ge(s_x1d[r % 2], PRIMED + (b * (NB // 2) + r // 2) * 16)
                if r < 2:
                    dve.wait_ge(s_scattered, PRIMED + b)
                else:
                    dve.wait_ge(s_sc[r % 2], (b * (NB // 2) + r // 2) * 16)
                ln.scale(dve, z[r % 2], x1[r % 2], b * NB + r, r, s_x1)

            def batch(b, more):
                for u in range(-AHEAD_MAX, UPB - AHEAD_LO):
                    if u + AHEAD_MAX < UPB:
                        maxima(b, u + AHEAD_MAX)
                    if u + AHEAD_LO >= 0:
                        lo(b, u + AHEAD_LO)
                    if u + AHEAD_MAX < UPB:
                        negated(b, u + AHEAD_MAX)
                    if u in split_at and (more or split_at[u] < 2 * NM):
                        split_proj(b, split_at[u])
                    if more and u in x_split_at:
                        x_split(b + 1, x_split_at[u])
                norm_heads(dve, 1, b, NM - 1)
                for step, r in between:
                    if step == "v" and more:
                        v_split(b + 1, (r, r + 1))
                    elif step == "turn":
                        turned_lo(b, r)
                    elif step == "out":
                        add_x(b, r)
                        if r >= 1:
                            norm_rows(b, r - 1)
                    elif step == "sums" and more:
                        v_above(b + 1)
                norm_rows(b, NB - 1)
                if not more:
                    dve.wait_ge(s_vp, B * NB)
                    for e in range(len(context.raw) // 2):
                        context.cut_lo(dve, e)

            for k in range(KT):
                x_split(0, k)
            routing = route.chain(dve, counts[0], counts[1])
            for g in range(G_AHEAD):
                split_proj(0, g)
                v_split(0, (g,))
                next(routing, None)
            dve.wait_ge(s_const, NCONST)
            v_above(0)
            with dve.Fori(0, B - 1) as b:
                batch(b, True)
            batch(B - 1, False)


class LayerNorm:

    def __init__(self, nc, ctx, name, D, ring=4):
        self.D = D
        sb = lambda n, shape: ctx.enter_context(nc.sbuf_tensor(f"{name}_{n}", shape, F32))
        self.stats = sb("stats", [P, ring, 6])
        self.mv = sb("mv", [P, ring, 2])
        self.var = sb("var", [P, ring, 1])
        self.r = sb("r", [P, ring, 1])
        self.half = sb("half", [P, 1])
        self.s_half = ctx.enter_context(nc.semaphore(f"{name}_s_half"))
        self.s_passed = [ctx.enter_context(nc.semaphore(f"{name}_s_passed{i}")) for i in range(2)]
        self.s_st = ctx.enter_context(nc.semaphore(f"{name}_s_stats"))
        self.s_mv = ctx.enter_context(nc.semaphore(f"{name}_s_mv"))
        self.s_ve = ctx.enter_context(nc.semaphore(f"{name}_s_ve"))
        self.s_r = ctx.enter_context(nc.semaphore(f"{name}_s_r"))

    def start(self, pool):
        pool.memset(self.half[:, :], -0.5).then_inc(self.s_half, 1)

    def statistics(self, dve, z, s_z, z_count, n, i):
        dve.wait_ge(s_z, z_count)
        dve.bn_stats(self.stats[:, i, :], z[:, :]).then_inc(self.s_st, 1)
        wait_apart(dve, self.s_passed[0], [(self.s_st, n + 1)])
        dve.bn_aggr(self.mv[:, i, :], self.stats[:, i, :]).then_inc(self.s_mv, 1)

    def scale(self, dve, z, out, n, i, s_out):
        dve.wait_ge(self.s_r, n + 1)
        dve.tensor_scalar(out[:, :], z[:, :], self.mv[:, i, 0:1], self.r[:, i, :], ALU.subtract,
                          ALU.mult).then_inc(s_out, 1)

    def rstd(self, pool, n, i):
        wait_apart(pool, self.s_passed[1], [(self.s_mv, n + 1)])
        pool.tensor_scalar(self.var[:, i, :], self.mv[:, i, 1:2], EPS, None, ALU.add).then_inc(self.s_ve, 1)
        pool.wait_ge(self.s_ve, n + 1)
        pool.tensor_tensor(self.r[:, i, :], self.var[:, i, :], self.half[:, :], ALU.pow).then_inc(self.s_r, 1)


class Route:

    def __init__(self, nc, ctx, tok_src, idx_all, tile_expert, N, E, VOCAB):
        NT = N // P
        NS = NT + E - 1
        self.NT, self.NS, self.E, self.per_expert = NT, NS, E, VOCAB // E
        self.tok_src, self.idx_all, self.tile_expert = tok_src, idx_all, tile_expert

        def sb(name, shape, dt=F32):
            return ctx.enter_context(nc.sbuf_tensor(name, shape, dt))

        self.tok = sb("tok_sb", [P, NT], I32)
        self.tok_f = sb("tok_f", [P, NT])
        self.ge = sb("ge", [P, E + 1, NT])
        self.onehot = sb("onehot", [P, E, NT])
        self.onehot_bf = sb("onehot_bf", [P, E, NT], BF16)
        self.before = sb("before", [P, P], BF16)
        self.run = [sb(f"run{i}", [P, E, 2 * NT]) for i in range(2)]
        self.total = sb("total", [P, E, NT])
        self.rank = sb("rank", [P, E, NT])
        self.n_pad = sb("n_pad", [P, E], I32)
        self.n_tiles = sb("n_tiles", [P, E], I32)
        self.n_rows = sb("n_rows", [P, E], I32)
        self.rows_f = sb("rows_f", [P, E])
        self.base = sb("base", [P, E])
        self.at = sb("at", [P, E, NT])
        self.at2 = sb("at2", [P, E, NT])
        self.pos = sb("pos", [P, NT])
        self.tile_i = sb("tile_i", [P, NS], I32)
        self.tile_f = sb("tile_f", [P, NS])
        self.past = sb("past", [P, E - 1, NS])
        self.expert_f = sb("expert_f", [P, NS])
        self.s_tok, self.s_c, self.s_v, self.s_m = [ctx.enter_context(nc.semaphore(n))
                                                    for n in ("s_tok", "s_rc", "s_rv", "s_rm")]
        self.N_ONEHOT = 3 + 2 * E + 1
        self.s_idx_all = ctx.enter_context(nc.semaphore("s_idx_all"))

    def load(self, sp):
        sp.dma_start(self.tok[:, :], self.tok_src).then_inc(self.s_tok, 16)

    def start(self, pool):
        pool.memset(self.before[:, :], 1.0).then_inc(self.s_c, 1)
        pool.iota(self.tile_i[:, :], [[P, self.NS]], base=0, channel_multiplier=0).then_inc(self.s_c, 1)
        pool.wait_ge(self.s_c, 2)
        pool.affine_select(out=self.before[:, :], in_=self.before[:, :], compare_op=ALU.is_gt, fill=0.0, base=0,
                           pattern=[[1, P]], channel_multiplier=-1).then_inc(self.s_c, 1)

    def count(self, pe, ones, inside, tiles):
        pe.wait_ge(self.s_c, 3)
        pe.wait_ge(self.s_v, self.N_ONEHOT)
        flat = self.onehot_bf[:, :, :].rearrange("p e t -> p (e t)")
        pe.matmul(inside, self.before[:, :], flat, start=True, stop=True)
        pe.matmul(tiles, ones, flat, start=True, stop=True).then_inc(self.s_m, 1)

    def chain(self, dve, inside, tiles):
        E, NT = self.E, self.NT
        ge, onehot, run, total, at, at2, base = self.ge, self.onehot, self.run, self.total, self.at, self.at2, self.base
        inside = inside.rearrange("p (e t) -> p e t", e=E)
        tiles = tiles.rearrange("p (e t) -> p e t", e=E)
        count = [0]

        def step(ins):
            count[0] += 1
            ins.then_inc(self.s_v, 1)
            dve.wait_ge(self.s_v, count[0])

        dve.wait_ge(self.s_tok, 16)
        step(dve.tensor_copy(self.tok_f[:, :], self.tok[:, :]))
        step(dve.memset(ge[:, 0, :], 1.0))
        step(dve.memset(ge[:, E, :], 0.0))
        for e in range(1, E):
            step(dve.tensor_scalar(ge[:, e, :], self.tok_f[:, :], float(e * self.per_expert), None, ALU.is_ge))
        step(dve.tensor_tensor(onehot[:, :, :], ge[:, 0:E, :], ge[:, 1:E + 1, :], ALU.subtract))
        step(dve.tensor_copy(self.onehot_bf[:, :, :], onehot[:, :, :]))
        while count[0] < self.N_ONEHOT:
            step(dve.memset(run[count[0] % 2][:, :, :], 0.0))
        yield
        dve.wait_ge(self.s_m, 1)
        step(dve.tensor_copy(total[:, :, :], tiles))
        step(dve.tensor_copy(run[0][:, :, NT:], total[:, :, :]))
        shift, i = 1, 0
        while shift < NT:
            step(dve.tensor_tensor(run[1 - i][:, :, NT:], run[i][:, :, NT:],
                                   run[i][:, :, NT - shift:2 * NT - shift], ALU.add))
            shift, i = 2 * shift, 1 - i
        step(dve.tensor_tensor(self.rank[:, :, :], run[i][:, :, NT:], total[:, :, :], ALU.subtract))
        step(dve.tensor_tensor(at[:, :, :], inside, self.rank[:, :, :], ALU.add))
        yield
        step(dve.tensor_scalar(self.n_pad[:, :], run[i][:, :, 2 * NT - 1], float(P - 1), None, ALU.add))
        step(dve.tensor_scalar(self.n_tiles[:, :], self.n_pad[:, :], P.bit_length() - 1, None,
                               ALU.logical_shift_right))
        step(dve.tensor_scalar(self.n_rows[:, :], self.n_tiles[:, :], P.bit_length() - 1, None,
                               ALU.logical_shift_left))
        step(dve.tensor_copy(self.rows_f[:, :], self.n_rows[:, :]))
        step(dve.memset(base[:, :], 0.0))
        for e in range(1, E):
            step(dve.tensor_tensor(base[:, e:e + 1], base[:, e - 1:e], self.rows_f[:, e - 1:e], ALU.add))
        step(dve.tensor_tensor(at2[:, :, :], at[:, :, :], base[:, :].unsqueeze(2).broadcast_to([P, E, NT]),
                               ALU.add))
        step(dve.tensor_tensor(at[:, :, :], at2[:, :, :], onehot[:, :, :], ALU.mult))
        step(dve.tensor_reduce(self.pos[:, :], at[:, :, :].rearrange("p e t -> p t e"), AX.X, ALU.add))
        yield
        step(dve.tensor_copy(self.tile_f[:, :], self.tile_i[:, :]))
        for e in range(1, E):
            step(dve.tensor_scalar(self.past[:, e - 1, :], self.tile_f[:, :], base[:, e:e + 1], None, ALU.is_ge))
        step(dve.tensor_reduce(self.expert_f[:, :], self.past[:, :, :].rearrange("p e t -> p t e"), AX.X, ALU.add))
        step(dve.tensor_copy(self.tile_expert[:, :], self.expert_f[:, :]))
        dve.tensor_copy(self.idx_all[:, :], self.pos[:, :]).then_inc(self.s_idx_all, 1)


def prepare(nc, w_dram, w_split, ident, x_src, x_turned, s_xraw, D):
    KT = D // P
    wh, wl = w_split
    n_w = len(w_dram)
    with ExitStack() as ctx:
        raw = [ctx.enter_context(nc.sbuf_tensor(f"w_raw{i}", [P, KT, D], F32)) for i in range(n_w)]
        s_w = [ctx.enter_context(nc.semaphore(f"s_w{i}")) for i in range(n_w)]
        s_id = ctx.enter_context(nc.semaphore("s_id"))
        s_wh = ctx.enter_context(nc.semaphore("s_wh"))
        block = ctx.enter_context(nc.Block())

        @block.sync
        def _(sp):
            for i in range(n_w):
                sp.dma_start(raw[i][:, :, :], w_dram[i]).then_inc(s_w[i], 16)
            sp.dma_start(x_turned, x_src).then_inc(s_xraw, 16)

        @block.gpsimd
        def _(pool):
            pool.memset(ident[:, :], 0.0).then_inc(s_id, 1)
            pool.wait_ge(s_id, 1)
            pool.affine_select(out=ident[:, :], in_=ident[:, :], compare_op=ALU.not_equal, fill=1.0, base=0,
                               pattern=[[-1, P]], channel_multiplier=1).then_inc(s_id, 1)

        @block.scalar
        def _(act):
            for i in range(n_w):
                act.wait_ge(s_w[i], 16)
                act.activation(wh[i], raw[i][:, :, :], ACT.Copy).then_inc(s_wh, 1)

        @block.vector
        def _(dve):
            for i in range(n_w):
                dve.wait_ge(s_wh, i + 1)
                dve.tensor_tensor(wl[i], raw[i][:, :, :], wh[i].bitcast(F32), ALU.subtract)


class ContextHalves:

    def __init__(self, nc, ctx, src, raw, hi, lo):
        self.src, self.raw, self.hi, self.lo = src, raw, hi, lo
        self.s_in = [ctx.enter_context(nc.semaphore(f"s_ctx{e}")) for e in range(len(raw))]
        self.s_hi = ctx.enter_context(nc.semaphore("s_mh"))
        self.s_lo = ctx.enter_context(nc.semaphore("s_ml"))

    def load(self, sp, e):
        sp.dma_start(self.raw[e], self.src[e]).then_inc(self.s_in[e], 16)

    def cut_hi(self, act, e):
        act.wait_ge(self.s_in[e], 16)
        act.activation(self.hi[:, e], self.raw[e], ACT.Copy).then_inc(self.s_hi, 1)

    def cut_lo(self, dve, e):
        dve.wait_ge(self.s_hi, e + 1)
        dve.tensor_tensor(self.lo[:, e], self.raw[e], self.hi[:, e].bitcast(F32), ALU.subtract).then_inc(self.s_lo, 1)


def experts(nc, context, ident, tile_expert, sorted_rows, out_rows, weights, ffn_src, x1_in, N, E, D):
    KT = D // P
    NS = N // P + E - 1
    RING = weights.RING
    m_hl = [context.hi, context.lo]
    src = sorted_rows.rearrange("(t p) d -> t p d", p=P)
    dst = out_rows.rearrange("(t p) d -> t p d", p=P)
    with ExitStack() as ctx:
        def sb(name, shape, dt=F32):
            return ctx.enter_context(nc.sbuf_tensor(name, shape, dt))

        def sem(name):
            return ctx.enter_context(nc.semaphore(name))

        rows = [sb(f"rows{i}", [P, D]) for i in range(2)]
        xt = [[sb(f"xt_{h}{i}", [P, KT, P], F32R) for i in range(2)] for h in ("hi", "lo")]
        sg = [sb(f"sg{i}", [P, D]) for i in range(2)]
        gu = [sb(f"gu{i}", [P, D]) for i in range(2)]
        gt = [[sb(f"gt_{h}{i}", [P, KT, P], F32R) for i in range(2)] for h in ("hi", "lo")]
        y = [sb(f"y{i}", [P, D]) for i in range(2)]
        bank = [ctx.enter_context(nc.psum_tensor(f"e_bank{i}", [P, 512], F32)) for i in range(8)]
        XB, UB, GB, YB = bank[0:2], bank[2:4], bank[4:6], bank[6:8]
        s_ml = context.s_lo
        s_rows = [sem(f"s_rows{i}") for i in range(2)]
        s_xT, s_xh, s_xl = sem("s_xT"), sem("s_xTh"), sem("s_xTl")
        s_u, s_sg, s_gu = sem("s_u"), sem("s_sg"), sem("s_gu")
        s_gT, s_gh, s_gl = sem("s_gT"), sem("s_gTh"), sem("s_gTl")
        s_y = sem("s_y")
        s_ye = [sem(f"s_ye{i}") for i in range(2)]
        s_yd = [sem(f"s_yd{i}") for i in range(2)]
        block = ctx.enter_context(nc.Block())

        def tiles(eng, step):
            for n in range(3):
                step(n, n % 2, min(n, 1))
            with eng.Fori(1, (NS - 3) // 2) as i:
                step(2 * i + 1, 1, 1)
                step(2 * i + 2, 0, 1)
            for n in range(NS - 2, NS):
                step(n, n % 2, 1 if n < NS - 1 else 2)

        assert NS % 2 == 1

        @block.sync
        def _(sp):
            def load(n, i):
                sp.wait_ge(s_xT, n - 1)
                sp.dma_start(rows[i][:, :], src[n]).then_inc(s_rows[i], 16)

            def store(n, i):
                sp.wait_ge(s_ye[i], n - i + 2)
                sp.dma_start(dst[n], y[i][:, :]).then_inc(s_yd[i], 16)

            sp.dma_start(rows[0][:, :], src[0]).then_inc(s_rows[0], 16)
            sp.dma_start(rows[1][:, :], src[1]).then_inc(s_rows[1], 16)
            load(2, 0)
            with sp.Fori(0, (NS - 3) // 2) as i:
                load(2 * i + 3, 1)
                load(2 * i + 4, 0)
                store(2 * i, 0)
                store(2 * i + 1, 1)
            for i in range(RING):
                weights.load(sp, i, i, ffn_src[i])
            sp.wait_ge(s_ml, E)
            for x1_src, x1_dst, s_in in x1_in:
                sp.dma_start(x1_dst, x1_src).then_inc(s_in, 16)
            store(NS - 3, 0)
            store(NS - 2, 1)
            for i in range(RING, 2 * RING):
                weights.load(sp, i, i, ffn_src[i])
            store(NS - 1, 0)
            sp.wait_ge(s_yd[0], (NS + 1) // 2 * 16)
            sp.wait_ge(s_yd[1], NS // 2 * 16)

        @block.tensor
        def _(pe):
            def x_transposes(n, i):
                pe.wait_ge(s_rows[i], (n - i) * 8 + 16)
                pe.wait_ge(s_xl, n - 1 if not isinstance(n, int) or n > 1 else 0)
                for k in range(KT):
                    ins = pe.transpose(XB[i][:, k * P:(k + 1) * P], rows[i][:, k * P:(k + 1) * P], ident[:, :])
                ins.then_inc(s_xT, 1)

            def gu_transposes(n, i):
                pe.wait_ge(s_gu, n + 1)
                if not isinstance(n, int) or n > 1:
                    pe.wait_ge(s_gl, n - 1)
                for k in range(KT):
                    ins = pe.transpose(GB[i][:, k * P:(k + 1) * P], gu[i][:, k * P:(k + 1) * P], ident[:, :])
                ins.then_inc(s_gT, 1)

            def expert_of(n):
                return pe.value_load(tile_expert[0:1, bass.ds(n, 1)], min_val=0, max_val=E - 1)

            def times_expert(e, out, a):
                return matmul3(pe, out[:, :], lambda k, i: a[i][:, k, :],
                               lambda k, j: m_hl[j][:, bass.ds(e, 1), k, :].rearrange("p a n -> p (a n)"), KT)

            def step(n, i, where):
                e = expert_of(n)
                e_last = expert_of(n - 1) if where > 0 else None
                pe.wait_ge(s_xl, n + 1)
                if not isinstance(n, int) or n > 1:
                    pe.wait_ge(s_gu, n - 1)
                times_expert(e, UB[i], [xt[h][i] for h in range(2)]).then_inc(s_u, 1)
                if where < 2:
                    x_transposes(n + 1, 1 - i)
                if where > 0:
                    last(e_last, n - 1, 1 - i)
                gu_transposes(n, i)

            def last(e, n, i):
                pe.wait_ge(s_gl, n + 1)
                pe.wait_ge(s_ye[i], n - i)
                times_expert(e, YB[i], [gt[h][i] for h in range(2)]).then_inc(s_y, 1)

            x_transposes(0, 0)
            pe.wait_ge(s_ml, E)
            tiles(pe, step)
            last(expert_of(NS - 1), NS - 1, 0)

        @block.scalar
        def _(act):
            def x_hi(n, i):
                act.wait_ge(s_xT, n + 1)
                if not isinstance(n, int) or n > 1:
                    act.wait_ge(s_u, n - 1)
                act.activation(xt[0][i][:, :, :].rearrange("p k t -> p (k t)"), XB[i][:, :],
                               ACT.Copy).then_inc(s_xh, 1)

            x_hi(0, 0)
            def step(n, i, where):
                act.wait_ge(s_u, n + 1)
                if not isinstance(n, int) or n > 1:
                    act.wait_ge(s_gu, n - 1)
                act.activation(sg[i][:, :], UB[i][:, :], ACT.Silu).then_inc(s_sg, 1)
                if where < 2:
                    x_hi(n + 1, 1 - i)
                if where > 0:
                    y_out(n - 1, 1 - i)
                act.wait_ge(s_gT, n + 1)
                if not isinstance(n, int) or n > 1:
                    act.wait_ge(s_y, n - 1)
                act.activation(gt[0][i][:, :, :].rearrange("p k t -> p (k t)"), GB[i][:, :],
                               ACT.Copy).then_inc(s_gh, 1)
                if isinstance(n, int) and n == NS - 2:
                    for p in range(RING):
                        weights.cut_hi(act, p, p, weights.place(p, 0))

            def y_out(n, i):
                act.wait_ge(s_y, n + 1)
                if not isinstance(n, int) or n > 1:
                    act.wait_ge(s_yd[i], (n - i) * 8)
                act.activation(y[i][:, :], YB[i][:, :], ACT.Copy).then_inc(s_ye[i], 2)

            tiles(act, step)
            y_out(NS - 1, 0)
            for p in range(RING, 2 * RING):
                weights.cut_hi(act, p, p, weights.place(p, 0))

        @block.vector
        def _(dve):
            def lo(dst_hl, banks, i, s_in, s_out, n):
                dve.wait_ge(s_in, n + 1)
                dve.tensor_tensor(dst_hl[1][i][:, :, :].rearrange("p k t -> p (k t)"), banks[i][:, :],
                                  dst_hl[0][i][:, :, :].rearrange("p k t -> p (k t)").bitcast(F32),
                                  ALU.subtract).then_inc(s_out, 1)

            for e in range(E // 2, E):
                context.cut_lo(dve, e)
            lo(xt, XB, 0, s_xh, s_xl, 0)
            def step(n, i, where):
                dve.wait_ge(s_sg, n + 1)
                if not isinstance(n, int) or n > 1:
                    dve.wait_ge(s_gT, n - 1)
                dve.tensor_tensor(gu[i][:, :], UB[i][:, :], sg[i][:, :], ALU.mult).then_inc(s_gu, 1)
                if where < 2:
                    lo(xt, XB, 1 - i, s_xh, s_xl, n + 1)
                lo(gt, GB, i, s_gh, s_gl, n)
                if isinstance(n, int) and n == NS - 2:
                    for p in range(RING):
                        weights.cut_lo(dve, p, p, weights.place(p, 1), weights.place(p, 0))

            tiles(dve, step)
            for p in range(RING, 2 * RING):
                weights.cut_lo(dve, p, p, weights.place(p, 1), weights.place(p, 0))


class FfnWeights:

    RING = 4

    def __init__(self, nc, ctx, D, J):
        KT = D // P
        self.raw = [ctx.enter_context(nc.sbuf_tensor(f"fw_raw{i}", [P, D], F32)) for i in range(self.RING)]
        self.gate_up = [[ctx.enter_context(nc.sbuf_tensor(f"{n}_{h}", [P, J, KT, P], F32R)) for h in ("hi", "lo")]
                        for n in ("wg", "wu")]
        self.s_raw = [ctx.enter_context(nc.semaphore(f"s_fraw{i}")) for i in range(self.RING)]
        self.s_hi = ctx.enter_context(nc.semaphore("s_ph"))
        self.s_lo = ctx.enter_context(nc.semaphore("s_pl"))

    def place(self, i, half):
        return self.gate_up[i % 2][half][:, i // 2, :, :].rearrange("p k n -> p (k n)")

    def load(self, sp, n, i, src):
        if not isinstance(n, int) or n >= self.RING:
            sp.wait_ge(self.s_lo, n - self.RING + 1)
        sp.dma_start(self.raw[i % self.RING][:, :], src).then_inc(self.s_raw[i % self.RING], 16)

    def cut_hi(self, act, n, i, dst):
        act.wait_ge(self.s_raw[i % self.RING], (n - i % self.RING) * (16 // self.RING) + 16)
        act.activation(dst, self.raw[i % self.RING][:, :], ACT.Copy).then_inc(self.s_hi, 1)

    def cut_lo(self, dve, n, i, dst, hi):
        dve.wait_ge(self.s_hi, n + 1)
        dve.tensor_tensor(dst, self.raw[i % self.RING][:, :], hi.bitcast(F32), ALU.subtract).then_inc(self.s_lo, 1)


def ffn(nc, big, x2, weights, s_x1, ident, idx_all, expert_rows, gate, up, down, out_rows, N, D, I):
    KT = D // P
    J = 4
    TW = 512
    RW = TW // P
    CH = J * P
    NCH = I // CH
    NR = N // TW
    GUP, DP = 2 * J, J
    PIECES = GUP + DP
    LINKS = 11
    xt = [b[:, 0:KT * N].rearrange("p (k n) -> p k n", k=KT) for b in big]
    with ExitStack() as ctx:
        def sb(name, shape, dt=F32):
            return ctx.enter_context(nc.sbuf_tensor(name, shape, dt))

        def sem(name):
            return ctx.enter_context(nc.semaphore(name))

        wg, wu = weights.gate_up
        wd = [sb(f"wd_{h}", [P, J, D], F32R) for h in ("hi", "lo")]
        sg = [sb(f"fsg{i}", [P, TW]) for i in range(2)]
        h = [sb(f"h{i}", [P, J, TW]) for i in range(2)]
        mag = sb("mag", [P, J, TW])
        beats = sb("beats", [P, 6, TW], BF16)
        wins = sb("wins", [P, J, TW], BF16)
        hs = [sb(f"hs_{x}", [P, J, TW], F32R) for x in ("hi", "lo")]
        gathered = [mag, hs[0], hs[1], wd[0]]
        ln = LayerNorm(nc, ctx, "ln3", D)
        ln2 = LayerNorm(nc, ctx, "ln2", D)
        bank = [ctx.enter_context(nc.psum_tensor(f"f_bank{i}", [P, 512], F32)) for i in range(8)]
        GB, UB, YB = bank[0:2], bank[2:4], bank[4:8]
        s_pl = weights.s_lo
        s_g, s_u, s_sg, s_h = sem("s_fg"), sem("s_fu"), sem("s_fsg"), sem("s_fh")
        s_mag, s_ch, s_hh, s_hl = sem("s_mag"), sem("s_ch"), sem("s_hh"), sem("s_hl")
        s_y, s_acc = sem("s_fy"), sem("s_facc")
        s_x3, s_out = sem("s_x3"), sem("s_fout")
        s_gat = [sem(f"s_gat{i}") for i in range(RW + NR - 1)]

        def gathered_at(t):
            return (s_gat[t], 16) if t < RW else (s_gat[RW + t // RW - 1], RW * 16)

        s_z2, s_x2 = sem("s_z2"), sem("s_x2")
        s_xT, s_xTh, s_xTl = sem("s_x2T"), sem("s_x2Th"), sem("s_x2Tl")
        block = ctx.enter_context(nc.Block())

        def chunks(eng, body):
            body(0, True, False)
            with eng.Fori(1, NCH - 1) as c:
                body(c, False, False)
            body(NCH - 1, False, True)

        normed_at = {v: RW + 2 * v for v in range(J + 2)}
        turned_at = {v + 1: t for v, t in normed_at.items()}

        def tokens(half):
            return slice(0, TW) if half is None else slice(half * TW // 2, (half + 1) * TW // 2)

        def down_at(first):
            return J + 2 if first else J - 1

        def before(c, v, k):
            r = v // J - k
            return (c, r) if r >= 0 else (c - 1, r + NR)

        @block.sync
        def _(sp):
            def body(c, first, last):
                for j in range(J):
                    weights.load(sp, PIECES * c + GUP + j, j, down[c][:, j, :])
                if not last:
                    for i in range(GUP):
                        weights.load(sp, PIECES * (c + 1) + i, i, (gate, up)[i % 2][c + 1, i // 2])

            chunks(sp, body)
            for t in range(N // P):
                sp.wait_ge(s_x3, t + 1)
                sp.dma_start(out_rows[t], x2[:, t, :]).then_inc(s_out, 16)
            sp.wait_ge(s_out, N // P * 16)

        @block.gpsimd
        def _(pool):
            def gather(t):
                dst = gathered[t // RW][:, t % RW, :]
                pool.indirect_dma_start(dst if t < RW else dst.bitcast(F32), None, expert_rows,
                                        bass.IndirectOffsetOnAxis(idx_all[:, t:t + 1], 0)
                                        ).then_inc(gathered_at(t)[0], 16)
            ln2.start(pool)
            ln.start(pool)
            for t in range(N // P):
                gather(t)
                if t >= RW:
                    ln2.rstd(pool, t - RW, t % 4)
            for t in range(N // P - RW, N // P):
                ln2.rstd(pool, t, t % 4)
            for t in range(N // P):
                ln.rstd(pool, t, t % 4)

        @block.tensor
        def _(pe):
            def turn(t):
                pe.wait_ge(s_x2, t + 1)
                if t >= RW:
                    pe.wait_ge(s_xTl, t - RW + 1)
                for k in range(KT):
                    ins = pe.transpose(YB[t % RW][:, k * P:(k + 1) * P], x2[:, t, k * P:(k + 1) * P], ident[:, :])
                ins.then_inc(s_xT, 1)

            def inner(c, v):
                r, j = v // J, v % J
                if isinstance(c, int) and c == 0 and j == 0:
                    pe.wait_ge(s_xTl, (r + 1) * RW)
                n = c * NR * J + v
                for m, (w, banks, s_read, s_done) in enumerate(((wg, GB, s_sg, s_g), (wu, UB, s_h, s_u))):
                    if r == 0:
                        pe.wait_ge(s_pl, PIECES * c + 2 * j + m + 1)
                    if not isinstance(n, int) or n >= 2:
                        pe.wait_ge(s_read, n - 1)
                    matmul3(pe, banks[v % 2][:, :], lambda k, i: w[i][:, j, k, :],
                            lambda k, i: xt[i][:, k, r * TW:(r + 1) * TW], KT).then_inc(s_done, 1)

            def outer(c, r, half=None):
                n = c * NR + r
                pe.wait_ge(s_pl, PIECES * c + PIECES)
                pe.wait_ge(s_hl, n + 1 + (half or 0))
                for t in range(RW) if half is None else range(half * RW // 2, (half + 1) * RW // 2):
                    if not isinstance(n, int) or n >= 1:
                        pe.wait_ge(s_acc, RW * (n - 1) + t + 1)
                    matmul3(pe, YB[t][:, :], lambda k, i: hs[i][:, k, t * P:(t + 1) * P],
                            lambda k, i: wd[i][:, k, :], J).then_inc(s_y, 1)

            def body(c, first, last):
                for v in range(NR * J):
                    inner(c, v)
                    if first:
                        if v in turned_at:
                            turn(turned_at[v])
                            turn(turned_at[v] + 1)
                    if v % J == J - 1 and (v > J or not first):
                        outer(*before(c, v, 1))

            for t in range(RW):
                turn(t)
            chunks(pe, body)
            for half in range(2):
                outer(NCH - 1, NR - 1, half)

        @block.scalar
        def _(act):
            def gate_up_piece(c, i):
                act.wait_ge((s_g, s_u)[i % 2], c * NR * J + (NR - 1) * J + i // 2 + 1)
                weights.cut_hi(act, PIECES * (c + 1) + i, i, weights.place(i, 0))

            def turned_hi(t):
                act.wait_ge(s_xT, t + 1)
                act.activation(xt[0][:, :, t * P:(t + 1) * P],
                               YB[t % RW][:, :].rearrange("p (k t) -> p k t", k=KT), ACT.Copy).then_inc(s_xTh, 1)

            def silu(c, v):
                n = c * NR * J + v
                act.wait_ge(s_g, n + 1)
                if not isinstance(n, int) or n >= 2:
                    act.wait_ge(s_h, n - 1)
                act.activation(sg[v % 2][:, :], GB[v % 2][:, :], ACT.Silu).then_inc(s_sg, 1)

            def magnitudes(c, r, half=None):
                n = c * NR + r
                act.wait_ge(s_h, J * (n + 1))
                n, tw = n + (half or 0), tokens(half)
                if not isinstance(n, int) or n >= 1:
                    act.wait_ge(s_ch, LINKS * (n - 1) + 3)
                act.activation(mag[:, :, tw], h[r % 2][:, :, tw], ACT.Abs).then_inc(s_mag, 1)

            def kept_hi(c, r, half=None):
                n = c * NR + r
                tw = tokens(half)
                act.wait_ge(s_ch, LINKS * (n + 1 + (half or 0)))
                act.wait_ge(s_y, RW * n)
                act.activation(hs[0][:, :, tw], h[r % 2][:, :, tw], ACT.Copy).then_inc(s_hh, 1)

            def body(c, first, last):
                for v in range(NR * J):
                    silu(c, v)
                    if first:
                        if v in turned_at:
                            turned_hi(turned_at[v])
                            turned_hi(turned_at[v] + 1)
                    if v % J == 0 and (v > 0 or not first):
                        kept_hi(*before(c, v, 1))
                    if v % J == J - 1:
                        for half in range(2) if last and v == NR * J - 1 else (None,):
                            magnitudes(c, v // J, half)
                    if v == down_at(first):
                        if first:
                            act.wait_ge(s_z2, N // P)
                        else:
                            act.wait_ge(s_y, RW * (c * NR))
                        for j in range(J):
                            weights.cut_hi(act, PIECES * c + GUP + j, j, wd[0][:, j, :])
                    if v > (NR - 1) * J and not last:
                        j = v - (NR - 1) * J - 1
                        for i in (2 * j, 2 * j + 1):
                            gate_up_piece(c, i)
                if not last:
                    for i in (2 * J - 2, 2 * J - 1):
                        gate_up_piece(c, i)

            for t in range(RW):
                turned_hi(t)
            chunks(act, body)
            for half in range(2):
                kept_hi(NCH - 1, NR - 1, half)

        @block.vector
        def _(dve):
            def gate_up_piece(c, i):
                weights.cut_lo(dve, PIECES * (c + 1) + i, i, weights.place(i, 1), weights.place(i, 0))

            def normed(t):
                r = t // RW
                for i in (t, t + 1):
                    dve.wait_ge(s_x1[r], 16)
                    dve.wait_ge(*gathered_at(i))
                    g = gathered[r][:, i % RW, :]
                    dve.tensor_tensor(x2[:, i, :], x2[:, i, :], g if r == 0 else g.bitcast(F32),
                                      ALU.add).then_inc(s_z2, 1)
                    ln2.statistics(dve, x2[:, i, :], s_z2, i + 1, i, i % 4)
                for i in (t, t + 1):
                    ln2.scale(dve, x2[:, i, :], x2[:, i, :], i, i % 4, s_x2)

            def turned_lo(t):
                for i in (t, t + 1):
                    dve.wait_ge(s_xTh, i + 1)
                    at = slice(i * P, (i + 1) * P)
                    dve.tensor_tensor(xt[1][:, :, at], YB[i % RW][:, :].rearrange("p (k t) -> p k t", k=KT),
                                      xt[0][:, :, at].bitcast(F32), ALU.subtract).then_inc(s_xTl, 1)

            def product(c, v):
                r, j = v // J, v % J
                n = c * NR * J + v
                dve.wait_ge(s_u, n + 1)
                dve.wait_ge(s_sg, n + 1)
                rr = c * NR + r
                if j == 0 and (not isinstance(rr, int) or rr >= 2):
                    dve.wait_ge(s_hh, rr - 1)
                dve.tensor_tensor(h[r % 2][:, j, :], UB[v % 2][:, :], sg[v % 2][:, :], ALU.mult).then_inc(s_h, 1)

            def pair(x, i, j, tw):
                return x[:, i:j + 1:j - i, tw]

            def compare(c, r, half=None):
                n, tw = c * NR + r + (half or 0), tokens(half)
                dve.wait_ge(s_mag, n + 1)
                for i, at in ((0, 0), (1, 3), (2, 5)):
                    w = J - 1 - i
                    dve.tensor_tensor(beats[:, at:at + w, tw],
                                      mag[:, i:i + 1, tw].broadcast_to([P, w, tw.stop - tw.start]),
                                      mag[:, i + 1:J, tw], ALU.is_ge).then_inc(s_ch, 1)
                dve.wait_ge(s_ch, LINKS * n + 3)

            def choose(c, r, half=None):
                n, tw = c * NR + r + (half or 0), tokens(half)
                hr = h[r % 2]
                b01, b02, b03, b12, b13, b23 = range(6)
                dve.tensor_tensor(pair(wins, 0, 3, tw), pair(beats, b01, b03, tw), pair(beats, b02, b13, tw),
                                  ALU.add).then_inc(s_ch, 1)
                dve.tensor_tensor(wins[:, 1, tw], beats[:, b12, tw], beats[:, b13, tw], ALU.add).then_inc(s_ch, 1)
                dve.tensor_tensor(wins[:, 2, tw], beats[:, b02, tw], beats[:, b12, tw], ALU.add).then_inc(s_ch, 1)
                dve.wait_ge(s_ch, LINKS * n + 6)
                dve.tensor_tensor(pair(wins, 0, 3, tw), pair(wins, 0, 3, tw), pair(beats, b03, b23, tw),
                                  ALU.add).then_inc(s_ch, 1)
                dve.tensor_tensor(wins[:, 1, tw], wins[:, 1, tw], beats[:, b01, tw], ALU.subtract)
                dve.tensor_tensor(wins[:, 2, tw], wins[:, 2, tw], beats[:, b23, tw], ALU.subtract).then_inc(s_ch, 1)
                dve.wait_ge(s_ch, LINKS * n + 8)
                for j, (op, least) in enumerate(((ALU.is_ge, 1.5), (ALU.is_ge, 0.5), (ALU.is_le, 0.5),
                                                 (ALU.is_le, 1.5))):
                    ins = dve.scalar_tensor_tensor(out=hr[:, j, tw], in0=wins[:, j, tw], scalar=least,
                                                   in1=hr[:, j, tw], op0=op, op1=ALU.mult)
                    if j > 0:
                        ins.then_inc(s_ch, 1)

            def kept_lo(c, r, half=None):
                n, tw = c * NR + r, tokens(half)
                dve.wait_ge(s_hh, n + 1 + (half or 0))
                dve.wait_ge(s_y, RW * n)
                dve.tensor_tensor(hs[1][:, :, tw], h[r % 2][:, :, tw], hs[0][:, :, tw].bitcast(F32),
                                  ALU.subtract).then_inc(s_hl, 1)

            def add_up(c, r, norm):
                n = c * NR + r
                for t in range(RW):
                    dve.wait_ge(s_y, RW * n + t + 1)
                    rows = x2[:, r * RW + t, :]
                    dve.tensor_tensor(rows, YB[t][:, :], rows, ALU.add).then_inc(s_acc, 1)
                    if norm:
                        statistics(c, r, t)

            def statistics(c, r, t):
                ln.statistics(dve, x2[:, r * RW + t, :], s_acc, RW * (c * NR + r) + t + 1, r * RW + t, t)

            def norm_rows(r):
                for t in range(RW):
                    rows = x2[:, r * RW + t, :]
                    ln.scale(dve, rows, rows, r * RW + t, t, s_x3)

            def body(c, first, last):
                for v in range(NR * J):
                    product(c, v)
                    if first:
                        if v in turned_at:
                            turned_lo(turned_at[v])
                        if v in normed_at:
                            normed(normed_at[v])
                    if v % J == 0 and (v > 0 or not first):
                        kept_lo(*before(c, v, 1))
                    if v % J == 1 and (v >= 2 * J or not first):
                        add_up(*before(c, v, 2), last and v >= 2 * J)
                    if v % J == 2 and v >= 2 * J and last:
                        norm_rows(v // J - 2)
                    if v % J == J - 1 and not (last and v == NR * J - 1):
                        compare(c, v // J)
                        choose(c, v // J)
                    if v == down_at(first):
                        for j in range(J):
                            weights.cut_lo(dve, PIECES * c + GUP + j, j, wd[1][:, j, :], wd[0][:, j, :])
                    if v > (NR - 1) * J and not last:
                        j = v - (NR - 1) * J - 1
                        for i in (2 * j, 2 * j + 1):
                            gate_up_piece(c, i)
                if not last:
                    for i in (2 * J - 2, 2 * J - 1):
                        gate_up_piece(c, i)

            normed(0)
            normed(2)
            turned_lo(0)
            turned_lo(2)
            chunks(dve, body)
            last = (NCH - 1, NR - 1)
            compare(*last, 0)
            choose(*last, 0)
            compare(*last, 1)
            kept_lo(*last, 0)
            add_up(NCH - 1, NR - 2, False)
            choose(*last, 1)
            kept_lo(*last, 1)
            for t in range(RW):
                statistics(NCH - 1, NR - 2, t)
            norm_rows(NR - 2)
            add_up(*last, True)
            norm_rows(NR - 1)


def build(nc, x, x_t, tok, ctx_t, wq, wk, wv, wo, gate, up, down, out):
    B, T, D = x.shape
    N = B * T
    E = ctx_t.shape[0]
    I = down.shape[0]
    VOCAB = 25000
    KT = D // P
    NB = T // P
    NS = N // P + E - 1

    def scratch(name, shape):
        return nc.dram_tensor(name, shape, F32, kind="Internal").ap()

    qk_dram = [[scratch(f"{n}_{h}_dram", [P, T]) for h in ("hi", "lo")] for n in "qk"]
    x1_rows = scratch("x1_dram", [B, T, D])
    sorted_rows = scratch("sorted_dram", [NS * P, D])
    expert_rows = scratch("expert_dram", [NS * P, D])
    with ExitStack() as ctx:
        def sb(name, shape, dt):
            return ctx.enter_context(nc.sbuf_tensor(name, shape, dt))

        def sem(name):
            return ctx.enter_context(nc.semaphore(name))

        ident = sb("ident", [P, P], F32)
        idx_all = sb("idx_all", [P, N // P], I32)
        tile_expert = sb("tile_expert", [P, NS], I32)
        s_xraw = sem("s_xraw")
        big = [sb(f"big_{h}", [P, max(E * KT * D, KT * N)], F32R) for h in ("hi", "lo")]
        with nc.sbuf_tensor("w_qk", [P, 4, KT, D], F32R) as w_qk_tile:
            w_qk = w_qk_tile[:, :, :, :]
        rows_kept = sb("rows_kept", [P, N // P, D], F32)
        hi_lo = [b[:, 0:E * KT * D].rearrange("p (e k n) -> p e k n", e=E, k=KT) for b in (big[1], big[0])]
        context = ContextHalves(nc, ctx, ctx_t.rearrange("e (k p) n -> e p k n", p=P),
                                [rows_kept[:, e * KT:(e + 1) * KT, :] for e in range(E)], *hi_lo)
        x2 = rows_kept[:, :, :]
        s_x1 = [sem(f"s_x1r{b}") for b in range(B)]
        x1_blocks = x1_rows.rearrange("b (r p) d -> b p r d", p=P)
        with ExitStack() as actx:
            x_raw = actx.enter_context(nc.sbuf_tensor("x_raw", [P, KT * T], F32))
            x_turned = x_raw[:, :].rearrange("p (k t) -> p k t", k=KT)
            w_vo = big[0][:, 0:4 * KT * D].rearrange("p (i k n) -> p i k n", i=4, k=KT)
            w_split = [[w_qk[:, i], w_qk[:, 2 + i], w_vo[:, i], w_vo[:, 2 + i]] for i in range(2)]
            x_t = x_t.rearrange("b (k p) t -> b p k t", p=P)
            prepare(nc, [w.rearrange("(k p) n -> p k n", p=P) for w in (wq, wk, wv, wo)], w_split, ident,
                    x_t[0], x_turned, s_xraw, D)
            attention(nc, w_split, big[1], ident, idx_all, x_t, x_raw, s_xraw,
                      x.rearrange("b (r p) d -> b p r d", p=P), x1_blocks, sorted_rows,
                      Route(nc, actx, tok, idx_all, tile_expert, N, E, VOCAB), context, qk_dram, B, T, D)
        weights = FfnWeights(nc, ctx, D, 4)
        experts(nc, context, ident, tile_expert, sorted_rows, expert_rows, weights,
                [(gate, up)[i % 2][0, i // 2] for i in range(8)],
                [(x1_blocks[b], x2[:, b * NB:(b + 1) * NB, :], s_x1[b]) for b in range(B)], N, E, D)
        ffn(nc, big, x2, weights, s_x1, ident, idx_all, expert_rows, gate, up,
            down.rearrange("(c p j) n -> c p j n", p=P, j=4), out.rearrange("b (r p) d -> (b r) p d", p=P), N, D, I)


def kernel(x, itok_BxS_13_99985, ctx_2048, L0_attn_Wq, L0_attn_Wk, L0_attn_Wv, L0_attn_Wo, L0_ffn_w_gate,
           L0_ffn_w_up, L0_ffn_w_down):
    import numpy as np
    from concourse import bacc
    from concourse.bass_utils import run_bass_kernel_spmd

    def by_group(w):
        d, i = w.shape
        w = w.reshape(d // P, P, i // 512, P, 4)
        return np.ascontiguousarray(w.transpose(2, 4, 1, 0, 3)).reshape(i // 512, 4, P, d)

    x = np.asarray(x)
    arrays = {
        "x": x,
        "x_t": np.ascontiguousarray(x.transpose(0, 2, 1)),
        "tok": np.ascontiguousarray(np.asarray(itok_BxS_13_99985).reshape(-1, P).T),
        "ctx_t": np.ascontiguousarray(np.asarray(ctx_2048).transpose(0, 2, 1)),
        "wq": np.asarray(L0_attn_Wq),
        "wk": np.asarray(L0_attn_Wk),
        "wv": np.asarray(L0_attn_Wv),
        "wo": np.asarray(L0_attn_Wo),
        "gate": by_group(np.asarray(L0_ffn_w_gate)),
        "up": by_group(np.asarray(L0_ffn_w_up)),
        "down": np.asarray(L0_ffn_w_down),
    }
    nc = bacc.Bacc("TRN2", target_bir_lowering=False, num_devices=1)
    aps = [nc.dram_tensor(n, a.shape, mybir.dt.from_np(a.dtype), kind="ExternalInput").ap()
           for n, a in arrays.items()]
    out = nc.dram_tensor("out", x.shape, F32, kind="ExternalOutput").ap()
    build(nc, *aps, out)
    got = run_bass_kernel_spmd(nc, [arrays], core_ids=[0])
    return got.results[0]["out"]
```
